# Optimizing a Trainium2 kernel written in Bass

```python
import numpy as np
import jax
import jax.numpy as jnp

def _softmax(x, axis=-1):
    return jax.nn.softmax(x, axis=axis)

def _gelu(x):
    return jax.nn.gelu(x, approximate=True)

def _silu(x):
    return jax.nn.silu(x)

def _sigmoid(x):
    return jax.nn.sigmoid(x)

def _layernorm(x, axis=-1, eps=1e-05):
    m = jnp.mean(x, axis=axis, keepdims=True)
    v = jnp.var(x, axis=axis, keepdims=True)
    return (x - m) / jnp.sqrt(v + eps)

def _scatter_add(tgt, idx, src, axis=0):
    return tgt.at[idx].add(src)

def _segment_sum(src, seg, n):
    return jax.ops.segment_sum(src, seg, n)
kernel_name = 'mk_decoder_postln_d1_seqx_r8_bf5c67'

def setup_inputs(seed: int=0):
    np.random.seed(seed)
    _w = jnp.asarray

    def _rec_inputs():
        import jax
        import jax.numpy as jnp
        _rk = jax.random.key(seed)
        x = -0.000929 + 1 * jax.random.normal(jax.random.fold_in(_rk, 1), (8, 256, 128), jnp.float32)
        _lenS = 256 - jax.random.randint(jax.random.fold_in(_rk, 7), (8,), 0, max(1, 256 // 4) + 1, jnp.int32)
        _lenS2 = 256 - jax.random.randint(jax.random.fold_in(_rk, 8), (8,), 0, max(1, 256 // 4) + 1, jnp.int32)
        _ctx_1024P = jax.random.normal(jax.random.fold_in(_rk, 11), (8, 16, 128), jnp.float32)
        _ctx_1024c = jax.random.dirichlet(jax.random.fold_in(_rk, 511), 0.3 * jnp.ones((16,), jnp.float32), (8, 256))
        _ctx_1024t = jnp.einsum('bsk,bkd->bsd', _ctx_1024c, _ctx_1024P)
        _ctx_1024t = _ctx_1024t * jax.lax.rsqrt(jnp.mean(jnp.square(_ctx_1024t)) + 1e-12) * 0.953939
        ctx_1024 = -1.52775e-05 + 0.999936 * (_ctx_1024t + 0.3 * jax.random.normal(jax.random.fold_in(_rk, 611), (8, 256, 128), jnp.float32))
        return (x, ctx_1024)
    x, ctx_1024 = _rec_inputs()

    def _L0_attn_setup():
        import jax, jax.numpy as jnp
        import numpy as np
        from jax import lax
        D_OUTER, D, N, K = (128, 256, 16, 4)
        B_SZ, L = (2, 128)

        def _forward(X, ln_g, ln_b, W_up1, conv_w, conv_b, W_ll, b_ll, A_log, W_up2, W_down, b_down):
            X_res = X
            mu = jnp.mean(X, axis=-1, keepdims=True)
            var = jnp.var(X, axis=-1, keepdims=True)
            Xn = (X - mu) * lax.rsqrt(var + 1e-05) * ln_g + ln_b
            X_main = jnp.einsum('bld,ed->ble', Xn, W_up1)
            x_ncl = X_main.transpose(0, 2, 1)
            y = lax.conv_general_dilated(x_ncl, conv_w, window_strides=(1,), padding=[(K - 1, 0)], feature_group_count=D, dimension_numbers=('NCH', 'OIH', 'NCH'))
            X_main = (y + conv_b[None, :, None]).transpose(0, 2, 1)
            X_main = jax.nn.silu(X_main)
            pp = jnp.einsum('bld,ed->ble', X_main, W_ll) + b_ll
            delta = jax.nn.softplus(pp[..., :D])
            Bm = pp[..., D:D + N]
            Cm = pp[..., D + N:]
            A = -jnp.exp(A_log)
            dA = jnp.einsum('bld,dn->bldn', delta, A)
            A_bar = jnp.exp(dA)
            zoh = (A_bar - 1.0) / dA
            B_bar = zoh * (delta[..., None] * Bm[:, :, None, :])
            U = X_main[..., None] * B_bar
            H0 = jnp.zeros((X.shape[0], D, N), jnp.float32)

            def step(H, inp):
                Ab_t, U_t, C_t = inp
                H = Ab_t * H + U_t
                y_t = jnp.einsum('bn,bdn->bd', C_t, H)
                return (H, y_t)
            _, Ys = lax.scan(step, H0, (A_bar.swapaxes(0, 1), U.swapaxes(0, 1), Cm.swapaxes(0, 1)))
            Y_ssm = Ys.swapaxes(0, 1)
            X_gate = jax.nn.silu(jnp.einsum('bld,ed->ble', Xn, W_up2))
            Y = Y_ssm * X_gate
            Y_proj = jnp.einsum('bld,ed->ble', Y, W_down) + b_down
            return X_res + Y_proj
        key = jax.random.key(seed)
        ks = jax.random.split(key, 12)
        s = 0.02
        X = jax.random.normal(ks[0], (B_SZ, L, D_OUTER), jnp.float32)
        ln_g = jnp.ones((D_OUTER,), jnp.float32)
        ln_b = jnp.zeros((D_OUTER,), jnp.float32)
        W_up1 = jax.random.normal(ks[1], (D, D_OUTER), jnp.float32) * s
        conv_w = jax.random.normal(ks[2], (D, 1, K), jnp.float32) * 0.1
        conv_b = jax.random.normal(ks[3], (D,), jnp.float32) * 0.1
        W_ll = jax.random.normal(ks[4], (2 * N + D, D), jnp.float32) * s
        b_ll = jax.random.normal(ks[5], (2 * N + D,), jnp.float32) * 0.1
        A_log = jnp.log(jnp.tile(jnp.arange(1, N + 1, dtype=jnp.float32), (D, 1)))
        W_up2 = jax.random.normal(ks[6], (D, D_OUTER), jnp.float32) * s
        W_down = jax.random.normal(ks[7], (D_OUTER, D), jnp.float32) * s
        b_down = jax.random.normal(ks[8], (D_OUTER,), jnp.float32) * 0.1
        return {'X': X, 'ln_g': ln_g, 'ln_b': ln_b, 'W_up1': W_up1, 'conv_w': conv_w, 'conv_b': conv_b, 'W_ll': W_ll, 'b_ll': b_ll, 'A_log': A_log, 'W_up2': W_up2, 'W_down': W_down, 'b_down': b_down}
    _L0_attn_all = _L0_attn_setup()
    _L0_attn_in = {k: v for k, v in _L0_attn_all.items() if k in ('ln_g', 'ln_b', 'W_up1', 'conv_w', 'conv_b', 'W_ll', 'b_ll', 'A_log', 'W_up2', 'W_down', 'b_down')}
    del _L0_attn_all

    def _L0_xattn_setup():
        import jax, jax.numpy as jnp
        import numpy as np
        DIM = 128
        H = 16
        D = 64
        INNER = H * D
        EPS = 1e-05

        def layernorm(x, w, b):
            mu = jnp.mean(x, axis=-1, keepdims=True)
            var = jnp.var(x, axis=-1, keepdims=True)
            return (x - mu) * jax.lax.rsqrt(var + EPS) * w + b
        key = jax.random.key(seed)
        ks = jax.random.split(key, 8)
        B, N, S = (4, 32, 1024)
        s = 1.0 / np.sqrt(DIM)
        return {'latents': jax.random.normal(ks[0], (B, N, DIM), jnp.float32), 'context': jax.random.normal(ks[1], (B, S, DIM), jnp.float32), 'ln_l_w': jnp.ones((DIM,), jnp.float32), 'ln_l_b': jnp.zeros((DIM,), jnp.float32), 'ln_c_w': jnp.ones((DIM,), jnp.float32), 'ln_c_b': jnp.zeros((DIM,), jnp.float32), 'Wq': jax.random.normal(ks[2], (DIM, INNER), jnp.float32) * s, 'Wkv': jax.random.normal(ks[3], (DIM, 2 * INNER), jnp.float32) * s, 'Wo': jax.random.normal(ks[4], (INNER, DIM), jnp.float32) * (1.0 / np.sqrt(INNER)), 'bo': jnp.zeros((DIM,), jnp.float32)}
    _L0_xattn_all = _L0_xattn_setup()
    _L0_xattn_in = {k: v for k, v in _L0_xattn_all.items() if k in ('ln_l_w', 'ln_l_b', 'ln_c_w', 'ln_c_b', 'Wq', 'Wkv', 'Wo', 'bo')}
    del _L0_xattn_all

    def _L0_ffn_setup():
        import jax, jax.numpy as jnp
        import numpy as np
        DIM = 128
        DEPTH = 6
        HEADS = 16
        DIM_HEAD = 64
        WINDOW = 32
        INNER = HEADS * DIM_HEAD
        DIM_INNER = int(DIM * 4 * 2 / 3)
        QK_SCALE = 8.0

        def shift_tokens(t):
            a, s = jnp.split(t, 2, -1)
            s = jnp.pad(s, ((0, 0), (1, 0), (0, 0)))[:, :-1]
            return jnp.concatenate([a, s], -1)

        def l2norm(t):
            return t / jnp.maximum(jnp.linalg.norm(t, axis=-1, keepdims=True), 1e-12)

        def rotate_half(x):
            x1, x2 = jnp.split(x, 2, -1)
            return jnp.concatenate([-x2, x1], -1)

        def rotary_tables(n):
            half = jnp.arange(0, DIM_HEAD, 2, dtype=jnp.float32)
            inv_freq = 1.0 / 10000.0 ** (half / DIM_HEAD)
            t = jnp.arange(n, dtype=jnp.float32)
            freqs = t[:, None] * inv_freq[None, :]
            freqs = jnp.concatenate([freqs, freqs], -1)
            base_scale = (half + 0.4 * DIM_HEAD) / (1.4 * DIM_HEAD)
            power = (t - n // 2) / (WINDOW // 2)
            scale = base_scale[None, :] ** power[:, None]
            scale = jnp.concatenate([scale, scale], -1)
            return (freqs, scale)

        def local_attention(q, k, v):
            b, h, n, d = q.shape
            w = WINDOW
            nw = n // w
            bq = q.reshape(b, h, nw, w, d)
            bk = k.reshape(b, h, nw, w, d)
            bv = v.reshape(b, h, nw, w, d)

            def look(t):
                p = jnp.pad(t, ((0, 0), (0, 0), (1, 0), (0, 0), (0, 0)))
                return jnp.concatenate([p[:, :, :nw], p[:, :, 1:]], axis=3)
            bk2, bv2 = (look(bk), look(bv))
            seq = jnp.arange(n).reshape(nw, w)
            seq_p = jnp.pad(seq, ((1, 0), (0, 0)), constant_values=-1)
            jt = jnp.concatenate([seq_p[:nw], seq_p[1:]], axis=1)
            it = seq[:, :, None]
            jb = jt[:, None, :]
            mask = (it < jb) | (it > jb + w) | (jb == -1)
            sim = jnp.einsum('bhwie,bhwje->bhwij', bq, bk2) * QK_SCALE
            sim = jnp.where(mask, -jnp.finfo(sim.dtype).max, sim)
            attn = jax.nn.softmax(sim, -1)
            out = jnp.einsum('bhwij,bhwje->bhwie', attn, bv2)
            return out.reshape(b, h, n, d)

        def attn_layer(x, Wqkv, qs, ksc, Wo):
            b, n, _ = x.shape
            qkv = x @ Wqkv
            q, k, v = jnp.split(qkv, 3, -1)
            sh = lambda t: t.reshape(b, n, HEADS, DIM_HEAD).transpose(0, 2, 1, 3)
            q, k, v = (sh(q), sh(k), sh(v))
            q = l2norm(q) * qs
            k = l2norm(k) * ksc
            freqs, scale = rotary_tables(n)
            cos, sin = (jnp.cos(freqs), jnp.sin(freqs))
            q = q * cos * scale + rotate_half(q) * sin * scale
            inv = 1.0 / scale
            k = k * cos * inv + rotate_half(k) * sin * inv
            out = local_attention(q, k, v)
            out = out.transpose(0, 2, 1, 3).reshape(b, n, INNER)
            return out @ Wo

        def ffn_layer(x, g, bln, W1, b1, W2, b2):
            mu = x.mean(-1, keepdims=True)
            var = ((x - mu) ** 2).mean(-1, keepdims=True)
            xn = (x - mu) / jnp.sqrt(var + 1e-05) * g + bln
            hg = xn @ W1 + b1
            a, gate = jnp.split(hg, 2, -1)
            return a * jax.nn.gelu(gate, approximate=False) @ W2 + b2
        key = jax.random.key(seed)
        ks = jax.random.split(key, 8)
        B, N = (2, 256)
        init = lambda k, shape: jax.random.normal(k, shape, jnp.float32) * 0.02
        return {'x': jax.random.normal(ks[0], (B, N, DIM), jnp.float32), 'Wqkv': init(ks[1], (DEPTH, DIM, 3 * INNER)), 'q_scale': jnp.ones((DEPTH, DIM_HEAD), jnp.float32), 'k_scale': jnp.ones((DEPTH, DIM_HEAD), jnp.float32), 'Wo': init(ks[2], (DEPTH, INNER, DIM)), 'ln_g': jnp.ones((DEPTH, DIM), jnp.float32), 'ln_b': jnp.zeros((DEPTH, DIM), jnp.float32), 'W1': init(ks[3], (DEPTH, DIM, 2 * DIM_INNER)), 'b1': jnp.zeros((DEPTH, 2 * DIM_INNER), jnp.float32), 'W2': init(ks[4], (DEPTH, DIM_INNER, DIM)), 'b2': jnp.zeros((DEPTH, DIM), jnp.float32)}
    _L0_ffn_all = _L0_ffn_setup()
    _L0_ffn_in = {k: v for k, v in _L0_ffn_all.items() if k in ('Wqkv', 'q_scale', 'k_scale', 'Wo', 'ln_g', 'ln_b', 'W1', 'b1', 'W2', 'b2')}
    del _L0_ffn_all
    return {'x': x, 'ctx_1024': ctx_1024, 'L0_attn_ln_g': _L0_attn_in['ln_g'], 'L0_attn_ln_b': _L0_attn_in['ln_b'], 'L0_attn_W_up1': _L0_attn_in['W_up1'], 'L0_attn_conv_w': _L0_attn_in['conv_w'], 'L0_attn_conv_b': _L0_attn_in['conv_b'], 'L0_attn_W_ll': _L0_attn_in['W_ll'], 'L0_attn_b_ll': _L0_attn_in['b_ll'], 'L0_attn_A_log': _L0_attn_in['A_log'], 'L0_attn_W_up2': _L0_attn_in['W_up2'], 'L0_attn_W_down': _L0_attn_in['W_down'], 'L0_attn_b_down': _L0_attn_in['b_down'], 'L0_xattn_ln_l_w': _L0_xattn_in['ln_l_w'], 'L0_xattn_ln_l_b': _L0_xattn_in['ln_l_b'], 'L0_xattn_ln_c_w': _L0_xattn_in['ln_c_w'], 'L0_xattn_ln_c_b': _L0_xattn_in['ln_c_b'], 'L0_xattn_Wq': _L0_xattn_in['Wq'], 'L0_xattn_Wkv': _L0_xattn_in['Wkv'], 'L0_xattn_Wo': _L0_xattn_in['Wo'], 'L0_xattn_bo': _L0_xattn_in['bo'], 'L0_ffn_Wqkv': _L0_ffn_in['Wqkv'], 'L0_ffn_q_scale': _L0_ffn_in['q_scale'], 'L0_ffn_k_scale': _L0_ffn_in['k_scale'], 'L0_ffn_Wo': _L0_ffn_in['Wo'], 'L0_ffn_ln_g': _L0_ffn_in['ln_g'], 'L0_ffn_ln_b': _L0_ffn_in['ln_b'], 'L0_ffn_W1': _L0_ffn_in['W1'], 'L0_ffn_b1': _L0_ffn_in['b1'], 'L0_ffn_W2': _L0_ffn_in['W2'], 'L0_ffn_b2': _L0_ffn_in['b2']}

def reference(x, ctx_1024, L0_attn_ln_g, L0_attn_ln_b, L0_attn_W_up1, L0_attn_conv_w, L0_attn_conv_b, L0_attn_W_ll, L0_attn_b_ll, L0_attn_A_log, L0_attn_W_up2, L0_attn_W_down, L0_attn_b_down, L0_xattn_ln_l_w, L0_xattn_ln_l_b, L0_xattn_ln_c_w, L0_xattn_ln_c_b, L0_xattn_Wq, L0_xattn_Wkv, L0_xattn_Wo, L0_xattn_bo, L0_ffn_Wqkv, L0_ffn_q_scale, L0_ffn_k_scale, L0_ffn_Wo, L0_ffn_ln_g, L0_ffn_ln_b, L0_ffn_W1, L0_ffn_b1, L0_ffn_W2, L0_ffn_b2):
    import jax
    import jax.numpy as jnp

    def _L0_attn_ref(X, ln_g, ln_b, W_up1, conv_w, conv_b, W_ll, b_ll, A_log, W_up2, W_down, b_down):
        import jax, jax.numpy as jnp
        import numpy as np
        from jax import lax
        D_OUTER, D, N, K = (128, 256, 16, 4)
        B_SZ, L = (2, 128)

        def _forward(X, ln_g, ln_b, W_up1, conv_w, conv_b, W_ll, b_ll, A_log, W_up2, W_down, b_down):
            X_res = X
            mu = jnp.mean(X, axis=-1, keepdims=True)
            var = jnp.var(X, axis=-1, keepdims=True)
            Xn = (X - mu) * lax.rsqrt(var + 1e-05) * ln_g + ln_b
            X_main = jnp.einsum('bld,ed->ble', Xn, W_up1)
            x_ncl = X_main.transpose(0, 2, 1)
            y = lax.conv_general_dilated(x_ncl, conv_w, window_strides=(1,), padding=[(K - 1, 0)], feature_group_count=D, dimension_numbers=('NCH', 'OIH', 'NCH'))
            X_main = (y + conv_b[None, :, None]).transpose(0, 2, 1)
            X_main = jax.nn.silu(X_main)
            pp = jnp.einsum('bld,ed->ble', X_main, W_ll) + b_ll
            delta = jax.nn.softplus(pp[..., :D])
            Bm = pp[..., D:D + N]
            Cm = pp[..., D + N:]
            A = -jnp.exp(A_log)
            dA = jnp.einsum('bld,dn->bldn', delta, A)
            A_bar = jnp.exp(dA)
            zoh = (A_bar - 1.0) / dA
            B_bar = zoh * (delta[..., None] * Bm[:, :, None, :])
            U = X_main[..., None] * B_bar
            H0 = jnp.zeros((X.shape[0], D, N), jnp.float32)

            def step(H, inp):
                Ab_t, U_t, C_t = inp
                H = Ab_t * H + U_t
                y_t = jnp.einsum('bn,bdn->bd', C_t, H)
                return (H, y_t)
            _, Ys = lax.scan(step, H0, (A_bar.swapaxes(0, 1), U.swapaxes(0, 1), Cm.swapaxes(0, 1)))
            Y_ssm = Ys.swapaxes(0, 1)
            X_gate = jax.nn.silu(jnp.einsum('bld,ed->ble', Xn, W_up2))
            Y = Y_ssm * X_gate
            Y_proj = jnp.einsum('bld,ed->ble', Y, W_down) + b_down
            return X_res + Y_proj
        return _forward(X, ln_g, ln_b, W_up1, conv_w, conv_b, W_ll, b_ll, A_log, W_up2, W_down, b_down)

    def _L0_xattn_ref(latents, context, ln_l_w, ln_l_b, ln_c_w, ln_c_b, Wq, Wkv, Wo, bo):
        import jax, jax.numpy as jnp
        import numpy as np
        DIM = 128
        H = 16
        D = 64
        INNER = H * D
        EPS = 1e-05

        def layernorm(x, w, b):
            mu = jnp.mean(x, axis=-1, keepdims=True)
            var = jnp.var(x, axis=-1, keepdims=True)
            return (x - mu) * jax.lax.rsqrt(var + EPS) * w + b
        b, n, _ = latents.shape
        s = context.shape[1]
        lat = layernorm(latents, ln_l_w, ln_l_b)
        ctx = layernorm(context, ln_c_w, ln_c_b)
        q = (lat @ Wq).reshape(b, n, H, D).transpose(0, 2, 1, 3)
        kv = ctx @ Wkv
        k, v = jnp.split(kv, 2, axis=-1)
        k = k.reshape(b, s, H, D).transpose(0, 2, 1, 3)
        v = v.reshape(b, s, H, D).transpose(0, 2, 1, 3)
        scale = D ** (-0.5)
        attn = jnp.einsum('bhnd,bhsd->bhns', q, k) * scale
        attn = jnp.clip(attn, -11.0, 11.0)
        attn = jax.nn.softmax(attn, axis=-1)
        out = jnp.einsum('bhns,bhsd->bhnd', attn, v)
        out = out.transpose(0, 2, 1, 3).reshape(b, n, INNER)
        return out @ Wo + bo

    def _L0_ffn_ref(x, Wqkv, q_scale, k_scale, Wo, ln_g, ln_b, W1, b1, W2, b2):
        import jax, jax.numpy as jnp
        import numpy as np
        DIM = 128
        DEPTH = 6
        HEADS = 16
        DIM_HEAD = 64
        WINDOW = 32
        INNER = HEADS * DIM_HEAD
        DIM_INNER = int(DIM * 4 * 2 / 3)
        QK_SCALE = 8.0

        def shift_tokens(t):
            a, s = jnp.split(t, 2, -1)
            s = jnp.pad(s, ((0, 0), (1, 0), (0, 0)))[:, :-1]
            return jnp.concatenate([a, s], -1)

        def l2norm(t):
            return t / jnp.maximum(jnp.linalg.norm(t, axis=-1, keepdims=True), 1e-12)

        def rotate_half(x):
            x1, x2 = jnp.split(x, 2, -1)
            return jnp.concatenate([-x2, x1], -1)

        def rotary_tables(n):
            half = jnp.arange(0, DIM_HEAD, 2, dtype=jnp.float32)
            inv_freq = 1.0 / 10000.0 ** (half / DIM_HEAD)
            t = jnp.arange(n, dtype=jnp.float32)
            freqs = t[:, None] * inv_freq[None, :]
            freqs = jnp.concatenate([freqs, freqs], -1)
            base_scale = (half + 0.4 * DIM_HEAD) / (1.4 * DIM_HEAD)
            power = (t - n // 2) / (WINDOW // 2)
            scale = base_scale[None, :] ** power[:, None]
            scale = jnp.concatenate([scale, scale], -1)
            return (freqs, scale)

        def local_attention(q, k, v):
            b, h, n, d = q.shape
            w = WINDOW
            nw = n // w
            bq = q.reshape(b, h, nw, w, d)
            bk = k.reshape(b, h, nw, w, d)
            bv = v.reshape(b, h, nw, w, d)

            def look(t):
                p = jnp.pad(t, ((0, 0), (0, 0), (1, 0), (0, 0), (0, 0)))
                return jnp.concatenate([p[:, :, :nw], p[:, :, 1:]], axis=3)
            bk2, bv2 = (look(bk), look(bv))
            seq = jnp.arange(n).reshape(nw, w)
            seq_p = jnp.pad(seq, ((1, 0), (0, 0)), constant_values=-1)
            jt = jnp.concatenate([seq_p[:nw], seq_p[1:]], axis=1)
            it = seq[:, :, None]
            jb = jt[:, None, :]
            mask = (it < jb) | (it > jb + w) | (jb == -1)
            sim = jnp.einsum('bhwie,bhwje->bhwij', bq, bk2) * QK_SCALE
            sim = jnp.where(mask, -jnp.finfo(sim.dtype).max, sim)
            attn = jax.nn.softmax(sim, -1)
            out = jnp.einsum('bhwij,bhwje->bhwie', attn, bv2)
            return out.reshape(b, h, n, d)

        def attn_layer(x, Wqkv, qs, ksc, Wo):
            b, n, _ = x.shape
            qkv = x @ Wqkv
            q, k, v = jnp.split(qkv, 3, -1)
            sh = lambda t: t.reshape(b, n, HEADS, DIM_HEAD).transpose(0, 2, 1, 3)
            q, k, v = (sh(q), sh(k), sh(v))
            q = l2norm(q) * qs
            k = l2norm(k) * ksc
            freqs, scale = rotary_tables(n)
            cos, sin = (jnp.cos(freqs), jnp.sin(freqs))
            q = q * cos * scale + rotate_half(q) * sin * scale
            inv = 1.0 / scale
            k = k * cos * inv + rotate_half(k) * sin * inv
            out = local_attention(q, k, v)
            out = out.transpose(0, 2, 1, 3).reshape(b, n, INNER)
            return out @ Wo

        def ffn_layer(x, g, bln, W1, b1, W2, b2):
            mu = x.mean(-1, keepdims=True)
            var = ((x - mu) ** 2).mean(-1, keepdims=True)
            xn = (x - mu) / jnp.sqrt(var + 1e-05) * g + bln
            hg = xn @ W1 + b1
            a, gate = jnp.split(hg, 2, -1)
            return a * jax.nn.gelu(gate, approximate=False) @ W2 + b2
        for i in range(DEPTH):
            x = attn_layer(shift_tokens(x), Wqkv[i], q_scale[i], k_scale[i], Wo[i]) + x
            x = ffn_layer(shift_tokens(x), ln_g[i], ln_b[i], W1[i], b1[i], W2[i], b2[i]) + x
        return x
    x = _layernorm(x + _L0_attn_ref(x, L0_attn_ln_g, L0_attn_ln_b, L0_attn_W_up1, L0_attn_conv_w, L0_attn_conv_b, L0_attn_W_ll, L0_attn_b_ll, L0_attn_A_log, L0_attn_W_up2, L0_attn_W_down, L0_attn_b_down), axis=-1)
    x = _layernorm(x + _L0_xattn_ref(x, ctx_1024, L0_xattn_ln_l_w, L0_xattn_ln_l_b, L0_xattn_ln_c_w, L0_xattn_ln_c_b, L0_xattn_Wq, L0_xattn_Wkv, L0_xattn_Wo, L0_xattn_bo), axis=-1)
    x = _layernorm(x + _L0_ffn_ref(x, L0_ffn_Wqkv, L0_ffn_q_scale, L0_ffn_k_scale, L0_ffn_Wo, L0_ffn_ln_g, L0_ffn_ln_b, L0_ffn_W1, L0_ffn_b1, L0_ffn_W2, L0_ffn_b2), axis=-1)
    return x

_drawn_inputs = setup_inputs


def setup_inputs(seed=0):
    import zlib

    import numpy as np

    out = dict(_drawn_inputs(seed))
    spreads = {'L0_attn_ln_g': (1.0, 0.6),
     'L0_attn_ln_b': (0.0, 0.8),
     'L0_xattn_ln_l_w': (1.0, 0.2),
     'L0_xattn_ln_l_b': (0.0, 0.455),
     'L0_xattn_ln_c_w': (1.0, 0.2),
     'L0_xattn_ln_c_b': (0.0, 0.1),
     'L0_xattn_bo': (0.0, 0.1),
     'L0_ffn_q_scale': (1.0, 0.6),
     'L0_ffn_k_scale': (1.0, 0.6),
     'L0_ffn_ln_g': (1.0, 0.6),
     'L0_ffn_ln_b': (0.0, 0.8),
     'L0_ffn_b1': (0.0, 0.8),
     'L0_ffn_b2': (0.0, 0.1)}
    factors = {'L0_attn_W_up1': 8.0,
     'L0_attn_conv_w': 8.0,
     'L0_attn_conv_b': 8.0,
     'L0_attn_W_ll': 8.0,
     'L0_attn_b_ll': 8.0,
     'L0_attn_A_log': 8.0,
     'L0_attn_W_up2': 8.0,
     'L0_attn_W_down': 8.0,
     'L0_ffn_W1': 3.692,
     'L0_ffn_W2': 3.615,
     'L0_attn_b_down': 26.327}
    for name, (base, spread) in spreads.items():
        noise = np.random.default_rng([zlib.crc32(name.encode()), seed]).standard_normal(out[name].shape)
        drawn = base * np.exp(spread * noise) if base else spread * noise
        out[name] = jnp.asarray(drawn.astype(out[name].dtype))
    for name, factor in factors.items():
        out[name] = (out[name] * factor).astype(out[name].dtype)
    return out
```

```python
from contextlib import ExitStack

import numpy as np

import concourse.bass as bass
from concourse import mybir

F32 = mybir.dt.float32
F32R = mybir.dt.float32r
BF16 = mybir.dt.bfloat16
ALU = mybir.AluOpType
ACT = mybir.ActivationFunctionType
AX = mybir.AxisListType

P = 128
B, L, D = 8, 256, 128
TILES = B * L // P
TPB = L // P
EPS = 1e-5
NST = 16
DI = 256
H, DH = 16, 64
INNER = H * DH
DEPTH = 6
WIN = 32
FF = 341
SSQ_SCALE = 2.0 ** 24


def alone(eng, passed):
    eng.sem_inc(passed, 1)


def layer_norm_stats(dve, passed, act_ready, chain, rows, stats, moments):
    for j, row in enumerate(rows):
        ins = dve.bn_stats(out=stats[:, j, :], in_=row)
    chain(ins)
    alone(dve, passed)
    for j in range(len(rows)):
        ins = dve.bn_aggr(out=moments[:, j, :], in_=stats[:, j, :])
    ins.then_inc(act_ready, 1)


class Chain:

    def __init__(self, eng, sem, base, per_iter):
        self.eng, self.sem, self.base, self.per_iter, self.n = eng, sem, base, per_iter, 0

    def __call__(self, ins):
        self.n += 1
        ins.then_inc(self.sem, 1)
        self.eng.wait_ge(self.sem, self.base + self.n)

    def close(self):
        assert self.n == self.per_iter, self.n


def state_space_block(nc, xall, ident, eps_col, w, debug=None):
    NB = 2
    T = NB * L
    NT = NB * TPB
    STEPS = B // NB
    NC = DI // P
    G = P // NST
    UPC = P // G
    UNITS = NC * UPC
    NLOAD = 15
    DVE_CHAIN = 22

    with ExitStack() as ctx:
        def sb(name, shape, dt=F32):
            return ctx.enter_context(nc.sbuf_tensor(name, shape, dt))

        def sem(name):
            return ctx.enter_context(nc.semaphore(name))

        up1 = sb("m_up1", [P, DI])
        up2 = sb("m_up2", [P, DI])
        down = sb("m_down", [P, NC, D])
        wdel = sb("m_wdel", [P, NC, DI])
        wB = sb("m_wB", [P, NC, P])
        wC = sb("m_wC", [P, NC, P])
        cols = sb("m_cols", [P, 2 + 3 * NC + NC * 4])
        ln_g, ln_b = cols[:, 0:1], cols[:, 1:2]
        conv_b = cols[:, 2:2 + NC]
        b_del = cols[:, 2 + NC:2 + 2 * NC]
        b_BC = cols[:, 2 + 2 * NC:2 + 3 * NC]
        conv_w = cols[:, 2 + 3 * NC:2 + 7 * NC].rearrange("p (c k) -> p c k", c=NC)
        alog = sb("m_alog", [P, UNITS])
        bdown = sb("m_bdown", [P, D])
        sel32 = sb("m_sel32", [P, UPC * P])
        sel = sb("m_sel", [P, UPC * P], F32R)
        pick = sb("m_pick", [P, UPC, P])
        summ = sb("m_summ", [P, UNITS, P])
        eA = sb("m_eA", [P, UNITS])
        negA = sb("m_negA", [P, UNITS])
        invA = sb("m_invA", [P, UNITS])
        stats = sb("m_stats", [P, NT, 6])
        mom = sb("m_mom", [P, NT, 2])
        lnv = sb("m_lnv", [P, NT])
        rstd = sb("m_rstd", [P, NT])
        xhat = sb("m_xhat", [P, NT, D])
        xnT = sb("m_xnT", [P, T])
        xpad = sb("m_xpad", [P, NC, NB, 3 + L])
        cv = sb("m_cv", [P, NC, NB, L])
        xc = sb("m_xc", [P, NC, T])
        xch = sb("m_xch", [P, NC, T], F32R)
        xcl = sb("m_xcl", [P, NC, T], F32R)
        gate = sb("m_gate", [P, NC, T])
        pre = sb("m_pre", [P, NC, T])
        ea = sb("m_ea", [P, NC, T])
        u1 = sb("m_u1", [P, NC, T])
        lu = sb("m_lu", [P, NC, T])
        dl = sb("m_dl", [P, NC, T])
        dlh = sb("m_dlh", [P, NC, T], F32R)
        dll = sb("m_dll", [P, NC, T], F32R)
        Bt = sb("m_Bt", [P, T])
        Ct = sb("m_Ct", [P, T])
        Ab = sb("m_Ab", [P, 2, T])
        XB = sb("m_XB", [P, 2, T])
        U = sb("m_U", [P, 2, T])
        Hs = sb("m_Hs", [P, 2, T])
        HC = sb("m_HC", [P, 2, T])
        Yg = sb("m_Yg", [P, NC, T])
        res = sb("m_res", [P, NT, D])
        psD = [ctx.enter_context(nc.psum_tensor(f"m_psD{j}", [P, T], F32)) for j in range(2)]
        psX = [ctx.enter_context(nc.psum_tensor(f"m_psX{j}", [P, T], F32)) for j in range(2)]
        psY = [ctx.enter_context(nc.psum_tensor(f"m_psY{j}", [P, T], F32)) for j in range(NC)]
        psM = [ctx.enter_context(nc.psum_tensor(f"m_psM{j}", [P, T], F32)) for j in range(2)]

        passed = sem("m_passed")
        loaded = sem("m_loaded")
        sel_ready = sem("m_sel_ready")
        eA_ready = sem("m_eA_ready")
        dve_chain = sem("m_dve_chain")
        act_chain = sem("m_act_chain")
        mom_ready = sem("m_mom_ready")
        rstd_ready = sem("m_rstd_ready")
        xhat_ready = sem("m_xhat_ready")
        misc_full = sem("m_misc_full")
        xnT_ready = sem("m_xnT_ready")
        xpad_ready = sem("m_xpad_ready")
        cv_ready = sem("m_cv_ready")
        xc_ready = sem("m_xc_ready")
        pre_ready = sem("m_pre_ready")
        u1_ready = sem("m_u1_ready")
        ea_ready = sem("m_ea_ready")
        lu_ready = sem("m_lu_ready")
        split_ready = sem("m_split_ready")
        BC_ready = sem("m_BC_ready")
        bcast_full = sem("m_bcast_full")
        Ab_ready = sem("m_Ab_ready")
        XB_done = sem("m_XB_done")
        U_done = sem("m_U_done")
        H_ready = sem("m_H_ready")
        HC_ready = sem("m_HC_ready")
        sum_done = sem("m_sum_done")
        Yg_ready = sem("m_Yg_ready")
        step_done = sem("m_step_done")
        MISC = 1 + NC + NC + 2 + NC + 1

        block = ctx.enter_context(nc.Block())

        @block.sync
        def _(sp):
            for dst, src in [(xall[:, :, :], w["x"]), (ident[:, :], w["ident"]), (cols[:, :], w["m_cols"]),
                             (up1[:, :], w["m_up1"]),
                             (wdel[:, :, :], w["m_wdel"]), (wB[:, :, :], w["m_wB"]), (wC[:, :, :], w["m_wC"]),
                             (alog[:, :], w["m_alog"]), (sel32[:, :], w["m_sel"]), (pick[:, :, :], w["m_pick"]),
                             (up2[:, :], w["m_up2"]), (down[:, :, :], w["m_down"]),
                             (bdown[:, :], w["m_bdown"])]:
                sp.dma_start(dst, src).then_inc(loaded, 16)
        LOADS = 16 * 13

        @block.gpsimd
        def _(pool):
            with pool.Fori(0, STEPS) as i:
                for k in range(UNITS):
                    pool.wait_ge(H_ready, i * UNITS + k + 3)
                    pool.wait_ge(sum_done, i * UNITS + k + 1)
                    pool.tensor_tensor(HC[:, k % 2, :], Hs[:, k % 2, :], Ct[:, :], ALU.mult).then_inc(HC_ready, 1)

        @block.scalar
        def _(act):
            act.wait_ge(loaded, LOADS)
            act.activation(eA[:, :], alog[:, :], ACT.Exp).then_inc(eA_ready, 1)
            act.wait_ge(sel_ready, 2)
            with act.Fori(0, STEPS) as i:
                def rsqrt_of_variance(n):
                    act.wait_ge(mom_ready, i * 2 + n)
                    act.activation(lnv[:, :], mom[:, :, 1], ACT.Ln, bias=eps_col).then_inc(act_chain, 1)
                    act.wait_ge(act_chain, i * 2 + n)
                    act.activation(rstd[:, :], lnv[:, :], ACT.Exp, scale=-0.5).then_inc(rstd_ready, 1)

                rsqrt_of_variance(1)
                act.wait_ge(misc_full, i * MISC + 1)
                act.activation(xnT[:, :], psM[0][:, :], ACT.Identity, bias=ln_b, scale=ln_g).then_inc(xnT_ready, 1)
                for c in range(NC):
                    act.wait_ge(misc_full, i * MISC + 2 + c)
                    for b in range(NB):
                        ins = act.activation(xpad[:, c, b, 3:3 + L], psM[(1 + c) % 2][:, b * L:(b + 1) * L], ACT.Copy)
                    ins.then_inc(xpad_ready, 1)
                for c in range(NC):
                    act.wait_ge(cv_ready, i * NC + c + 1)
                    act.activation(xc[:, c, :], cv[:, c, :, :].rearrange("p b t -> p (b t)"), ACT.Silu).then_inc(xc_ready, 1)
                for c in range(NC):
                    act.wait_ge(misc_full, i * MISC + 4 + c)
                    act.activation(gate[:, c, :], psM[(3 + c) % 2][:, :], ACT.Silu).then_inc(xnT_ready, 1)
                for j, dst in enumerate((Bt, Ct)):
                    act.wait_ge(misc_full, i * MISC + 6 + j)
                    act.activation(dst[:, :], psM[(5 + j) % 2][:, :], ACT.Identity, bias=b_BC[:, j:j + 1]).then_inc(BC_ready, 1)
                for c in range(NC):
                    act.wait_ge(misc_full, i * MISC + 8 + c)
                    act.activation(pre[:, c, :], psM[(7 + c) % 2][:, :], ACT.Identity, bias=b_del[:, c:c + 1]).then_inc(pre_ready, 1)
                    act.wait_ge(pre_ready, i * 2 * NC + 2 * c + 1)
                    act.activation(ea[:, c, :], pre[:, c, :], ACT.Abs).then_inc(pre_ready, 1)
                    act.wait_ge(pre_ready, i * 2 * NC + 2 * c + 2)
                    act.activation(ea[:, c, :], ea[:, c, :], ACT.Exp, scale=-1.0).then_inc(ea_ready, 1)
                for c in range(NC):
                    act.wait_ge(u1_ready, i * NC + c + 1)
                    act.activation(lu[:, c, :], u1[:, c, :], ACT.Ln).then_inc(lu_ready, 1)
                for k in range(UNITS):
                    act.wait_ge(bcast_full, i * UNITS + k + 1)
                    act.wait_ge(H_ready, i * UNITS + k + 1)
                    act.activation(Ab[:, k % 2, :], psD[k % 2][:, :], ACT.Exp, scale=negA[:, k:k + 1]).then_inc(Ab_ready, 1)
                rsqrt_of_variance(2)

        @block.vector
        def _(dve):
            dve.wait_ge(loaded, LOADS)
            dve.tensor_copy(sel[:, :], sel32[:, :]).then_inc(sel_ready, 1)
            dve.memset(xpad[:, :, :, 0:3], 0.0)
            dve.sem_inc(H_ready, 2)
            dve.wait_ge(eA_ready, 1)
            dve.tensor_scalar(negA[:, :], eA[:, :], -1.0, None, ALU.mult).then_inc(sel_ready, 1)
            dve.wait_ge(sel_ready, 2)
            dve.reciprocal(invA[:, :], negA[:, :]).then_inc(sel_ready, 1)
            dve.wait_ge(sel_ready, 3)
            for k in range(UNITS):
                ins = dve.tensor_scalar(summ[:, k, :], pick[:, k % UPC, :], invA[:, k:k + 1], None, ALU.mult)
            ins.then_inc(sel_ready, 1)
            with dve.Fori(0, STEPS) as i:
                chain = Chain(dve, dve_chain, i * DVE_CHAIN, DVE_CHAIN)

                def normalise(n, rows, outs):
                    layer_norm_stats(dve, passed, mom_ready, chain, rows, stats, mom)
                    dve.wait_ge(rstd_ready, i * 2 + n)
                    for j in range(NT):
                        ins = dve.tensor_scalar(outs[j], rows[j], mom[:, j, 0:1], rstd[:, j:j + 1], ALU.subtract, ALU.mult)
                    return ins

                xin = [xall[:, bass.ds(i * NT + j, 1), :].rearrange("p a d -> p (a d)") for j in range(NT)]
                normalise(1, xin, [xhat[:, j, :] for j in range(NT)]).then_inc(xhat_ready, 1)
                for c in range(NC):
                    dve.wait_ge(xpad_ready, i * NC + c + 1)
                    chain(dve.tensor_scalar(cv[:, c, :, :], xpad[:, c, :, 0:L], conv_w[:, c, 0:1], conv_b[:, c:c + 1], ALU.mult, ALU.add))
                    for k in range(1, 4):
                        ins = dve.scalar_tensor_tensor(out=cv[:, c, :, :], in0=xpad[:, c, :, k:k + L], scalar=conv_w[:, c, k:k + 1],
                                                       in1=cv[:, c, :, :], op0=ALU.mult, op1=ALU.add)
                        if k < 3:
                            chain(ins)
                    ins.then_inc(cv_ready, 1)
                for c in range(NC):
                    dve.wait_ge(xc_ready, i * NC + c + 1)
                    chain(dve.tensor_copy(xch[:, c, :], xc[:, c, :]))
                    dve.tensor_tensor(xcl[:, c, :], xc[:, c, :], xch[:, c, :].bitcast(F32), ALU.subtract).then_inc(split_ready, 1)
                for c in range(NC):
                    dve.wait_ge(ea_ready, i * NC + c + 1)
                    chain(dve.tensor_scalar(u1[:, c, :], ea[:, c, :], 1.0, None, ALU.add))
                    dve.sem_inc(u1_ready, 1)
                    dve.scalar_tensor_tensor(out=ea[:, c, :], in0=u1[:, c, :], scalar=-1.0, in1=ea[:, c, :], op0=ALU.add, op1=ALU.subtract)
                    chain(dve.tensor_scalar(pre[:, c, :], pre[:, c, :], 0.0, None, ALU.max))
                    dve.wait_ge(lu_ready, i * NC + c + 1)
                    chain(dve.tensor_tensor(dl[:, c, :], lu[:, c, :], ea[:, c, :], ALU.subtract))
                    chain(dve.tensor_tensor(dl[:, c, :], dl[:, c, :], pre[:, c, :], ALU.add))
                    chain(dve.tensor_copy(dlh[:, c, :], dl[:, c, :]))
                    dve.tensor_tensor(dll[:, c, :], dl[:, c, :], dlh[:, c, :].bitcast(F32), ALU.subtract).then_inc(split_ready, 1)
                dve.wait_ge(BC_ready, i * 2 + 1)
                for k in range(UNITS):
                    s = k % 2
                    dve.wait_ge(bcast_full, i * UNITS + k + 1)
                    dve.tensor_tensor(XB[:, s, :], psX[s][:, :], Bt[:, :], ALU.mult).then_inc(XB_done, 1)
                    dve.wait_ge(XB_done, i * UNITS + k + 1)
                    dve.wait_ge(Ab_ready, i * UNITS + k + 1)
                    dve.scalar_tensor_tensor(out=U[:, s, :], in0=Ab[:, s, :], scalar=1.0, in1=XB[:, s, :],
                                             op0=ALU.subtract, op1=ALU.mult).then_inc(U_done, 1)
                    dve.wait_ge(U_done, i * UNITS + k + 1)
                    dve.wait_ge(HC_ready, i * UNITS + k + 1)
                    for b in range(NB):
                        ins = dve.tensor_tensor_scan(Hs[:, s, b * L:(b + 1) * L], Ab[:, s, b * L:(b + 1) * L],
                                                     U[:, s, b * L:(b + 1) * L], 0.0, ALU.mult, ALU.add)
                    ins.then_inc(H_ready, 1)
                dve.wait_ge(sum_done, i * UNITS + UNITS + 2)
                for c in range(NC):
                    ins = dve.tensor_tensor(Yg[:, c, :], psY[c][:, :], gate[:, c, :], ALU.mult)
                ins.then_inc(Yg_ready, 1)
                xt = xall[:, bass.ds(i * NT, NT), :]
                chain(dve.scalar_tensor_tensor(out=res[:, :, :], in0=xt, scalar=2.0,
                                               in1=bdown[:, :].unsqueeze(1).broadcast_to([P, NT, D]), op0=ALU.mult, op1=ALU.add))
                dve.wait_ge(misc_full, i * MISC + MISC)
                chain(dve.tensor_tensor(res[:, :, :], res[:, :, :], psM[1][:, :].rearrange("p (t d) -> p t d", d=D), ALU.add))
                normalise(2, [res[:, j, :] for j in range(NT)], xin).then_inc(step_done, 1)
                chain.close()

        @block.tensor
        def _(pe):
            pe.sem_inc(sum_done, 2)
            pe.sem_inc(HC_ready, 2)
            pe.wait_ge(loaded, LOADS)
            pe.wait_ge(sel_ready, 4)
            with pe.Fori(0, STEPS) as i:
                pe.wait_ge(xhat_ready, i + 1)
                for j in range(NT):
                    ins = pe.transpose(psM[0][:, j * P:(j + 1) * P], xhat[:, j, :], ident[:, :])
                ins.then_inc(misc_full, 1)
                pe.wait_ge(xnT_ready, i * 3 + 1)
                for c in range(NC):
                    pe.matmul(psM[(1 + c) % 2][:, :], up1[:, c * P:(c + 1) * P], xnT[:, :], start=True, stop=True).then_inc(misc_full, 1)
                for c in range(NC):
                    pe.wait_ge(xpad_ready, i * NC + c + 1)
                    pe.matmul(psM[(3 + c) % 2][:, :], up2[:, c * P:(c + 1) * P], xnT[:, :], start=True, stop=True).then_inc(misc_full, 1)
                pe.wait_ge(xc_ready, i * NC + NC)
                for j, wt in enumerate((wB, wC)):
                    pe.wait_ge(xnT_ready, i * 3 + 2 + j)
                    for c in range(NC):
                        ins = pe.matmul(psM[(5 + j) % 2][:, :], wt[:, c, :], xc[:, c, :], start=(c == 0), stop=(c == NC - 1))
                    ins.then_inc(misc_full, 1)
                for m in range(NC):
                    pe.wait_ge(BC_ready, i * 2 + m + 1)
                    for c in range(NC):
                        ins = pe.matmul(psM[(7 + m) % 2][:, :], wdel[:, c, m * P:(m + 1) * P], xc[:, c, :], start=(c == 0), stop=(c == NC - 1))
                    ins.then_inc(misc_full, 1)

                def add_states(k):
                    pe.wait_ge(HC_ready, i * UNITS + k + 3)
                    pe.matmul(psY[k // UPC][:, :], summ[:, k, :], HC[:, k % 2, :], start=(k % UPC == 0), stop=(k % UPC == UPC - 1)).then_inc(sum_done, 1)

                pe.wait_ge(split_ready, i * 2 * NC + 2 * NC)
                for k in range(UNITS):
                    c, g = k // UPC, k % UPC
                    s = k % 2
                    if k >= 2:
                        pe.wait_ge(Ab_ready, i * UNITS + k - 1)
                        pe.wait_ge(XB_done, i * UNITS + k - 1)
                    for ps, hi, lo in ((psD[s], dlh, dll), (psX[s], xch, xcl)):
                        pe.matmul(ps[:, :], sel[:, g * P:(g + 1) * P], hi[:, c, :], start=True, stop=False)
                        ins = pe.matmul(ps[:, :], sel[:, g * P:(g + 1) * P], lo[:, c, :], start=False, stop=True)
                    ins.then_inc(bcast_full, 1)
                    if k >= 2:
                        add_states(k - 2)
                add_states(UNITS - 2)
                add_states(UNITS - 1)
                pe.wait_ge(Yg_ready, i + 1)
                for j in range(NT):
                    for c in range(NC):
                        ins = pe.matmul(psM[1][:, j * P:(j + 1) * P], Yg[:, c, j * P:(j + 1) * P], down[:, c, :], start=(c == 0), stop=(c == NC - 1))
                ins.then_inc(misc_full, 1)
                pe.wait_ge(step_done, i + 1)


def cross_attention_block(nc, xall, ident, eps_col, w):
    NC = INNER // P
    R = 2 * TPB
    FILLS = 1 + 4 + NC + 2 * TPB + 1
    PER_BANK = FILLS // 2
    assert FILLS % 2 == 0
    LOADS = 16 * 8
    DVE_CHAIN = 13
    LO, HI = float(np.exp(-11.0)), float(np.exp(11.0))

    with ExitStack() as ctx:
        def sb(name, shape, dt=F32):
            return ctx.enter_context(nc.sbuf_tensor(name, shape, dt))

        def sem(name):
            return ctx.enter_context(nc.semaphore(name))

        ctxall = sb("x_ctx", [P, TILES, D])
        wq = sb("x_wq", [P, INNER])
        wk = sb("x_wk", [P, INNER])
        wv = sb("x_wv", [P, INNER])
        wo = sb("x_wo", [P, NC, D])
        cols = sb("x_cols", [P, 4])
        bo = sb("x_bo", [P, D])
        stats = sb("x_stats", [P, R, 6])
        mom = sb("x_mom", [P, R, 2])
        lnv = sb("x_lnv", [P, R])
        rstd = sb("x_rstd", [P, R])
        hat = sb("x_hat", [P, R, D])
        latT = sb("x_latT", [P, L])
        ctxT = sb("x_ctxT", [P, L])
        V1 = sb("x_V1", [P, TPB, H, DH + 1])
        qk = sb("x_qk", [P, 2, 2, L])
        E = sb("x_E", [P, 4, TPB, L])
        rden = sb("x_rden", [P, 2, 2, TPB])
        On = sb("x_On", [P, TPB, H, DH])
        OT = sb("x_OT", [P, NC, L])
        res = sb("x_res", [P, TPB, D])
        stats2 = sb("x_stats2", [P, TPB, 6])
        mom2 = sb("x_mom2", [P, TPB, 2])
        lnv2 = sb("x_lnv2", [P, TPB])
        rstd2 = sb("x_rstd2", [P, TPB])
        psM = [ctx.enter_context(nc.psum_tensor(f"x_psM{j}", [P, 512], F32)) for j in range(2)]
        psS = [ctx.enter_context(nc.psum_tensor(f"x_psS{j}", [P, TPB, L], F32)) for j in range(4)]
        psO = [ctx.enter_context(nc.psum_tensor(f"x_psO{j}", [P, 512], F32)) for j in range(2)]

        def o_view(j):
            return psO[j][:, 0:4 * (DH + 1)].rearrange("p (h t e) -> p h t e", h=2, t=TPB)

        passed = sem("x_passed")
        loaded = sem("x_loaded")
        ones_ready = sem("x_ones_ready")
        dve_chain = sem("x_dve_chain")
        act_chain = sem("x_act_chain")
        mom_ready = sem("x_mom_ready")
        rstd_ready = sem("x_rstd_ready")
        mom2_ready = sem("x_mom2_ready")
        rstd2_ready = sem("x_rstd2_ready")
        hat_ready = sem("x_hat_ready")
        misc_full = [sem(f"x_misc_full{j}") for j in range(2)]
        misc_free = [sem(f"x_misc_free{j}") for j in range(2)]
        catT_ready = sem("x_catT_ready")
        S_full = sem("x_S_full")
        E_exp = sem("x_E_exp")
        E_ready = sem("x_E_ready")
        O_full = sem("x_O_full")
        O_free = sem("x_O_free")
        x_done = sem("x_x_done")

        block = ctx.enter_context(nc.Block())

        def wait_fill(eng, i, n):
            eng.wait_ge(misc_full[n % 2], i * PER_BANK + n // 2 + 1)
            return psM[n % 2], misc_free[n % 2]

        F_V, F_QK, F_OT, F_WO = 1, 5, 5 + NC, 5 + NC + 2 * TPB

        @block.sync
        def _(sp):
            for dst, src in [(ctxall[:, :, :], w["ctx"]), (cols[:, :], w["x_cols"]), (wv[:, :], w["x_wv"]), (wq[:, :], w["x_wq"]),
                             (wk[:, :], w["x_wk"]), (wo[:, :, :], w["x_wo"]), (bo[:, :], w["x_bo"]), (ident[:, :], w["ident"])]:
                sp.dma_start(dst, src).then_inc(loaded, 16)

        @block.scalar
        def _(act):
            act.wait_ge(loaded, LOADS)
            act.wait_ge(ones_ready, 1)
            with act.Fori(0, B) as i:
                act.wait_ge(mom_ready, i + 1)
                act.activation(lnv[:, :], mom[:, :, 1], ACT.Ln, bias=eps_col).then_inc(act_chain, 1)
                act.wait_ge(act_chain, i * 2 + 1)
                act.activation(rstd[:, :], lnv[:, :], ACT.Exp, scale=-0.5).then_inc(rstd_ready, 1)
                ps, free = wait_fill(act, i, 0)
                act.activation(ctxT[:, :], ps[:, L:2 * L], ACT.Identity, bias=cols[:, 3:4], scale=cols[:, 2:3]).then_inc(catT_ready, 1)
                act.activation(latT[:, :], ps[:, 0:L], ACT.Identity, bias=cols[:, 1:2], scale=cols[:, 0:1]).then_inc(free, 1)
                for n in range(4):
                    ps, free = wait_fill(act, i, F_V + n)
                    act.activation(V1[:, n // 2, (n % 2) * 8:(n % 2) * 8 + 8, 0:DH],
                                   ps[:, :].rearrange("p (h d) -> p h d", d=DH), ACT.Copy).then_inc(free, 1)
                for h in range(H):
                    act.wait_ge(S_full, i * H + h + 1)
                    if h >= 4:
                        act.wait_ge(O_full, i * NC + (h - 4) // 2 + 1)
                    act.activation(E[:, h % 4, :, :], psS[h % 4][:, :, :], ACT.Exp, scale=DH ** -0.5).then_inc(E_exp, 1)
                for n in range(2 * TPB):
                    ps, free = wait_fill(act, i, F_OT + n)
                    t, c0 = n // 2, (n % 2) * 4
                    act.activation(OT[:, c0:c0 + 4, t * P:(t + 1) * P], ps[:, :].rearrange("p (c q) -> p c q", c=4), ACT.Copy).then_inc(free, 1)
                act.wait_ge(mom2_ready, i + 1)
                act.activation(lnv2[:, :], mom2[:, :, 1], ACT.Ln, bias=eps_col).then_inc(act_chain, 1)
                act.wait_ge(act_chain, i * 2 + 2)
                act.activation(rstd2[:, :], lnv2[:, :], ACT.Exp, scale=-0.5).then_inc(rstd2_ready, 1)

        @block.vector
        def _(dve):
            dve.sem_inc(misc_free[0], 1)
            dve.sem_inc(misc_free[1], 1)
            dve.memset(V1[:, :, :, DH:DH + 1], 1.0).then_inc(ones_ready, 1)
            dve.wait_ge(loaded, LOADS)
            with dve.Fori(0, B) as i:
                chain = Chain(dve, dve_chain, i * DVE_CHAIN, DVE_CHAIN)
                xin = [xall[:, bass.ds(i * TPB + j, 1), :].rearrange("p a d -> p (a d)") for j in range(TPB)]
                rows = xin + [ctxall[:, bass.ds(i * TPB + j, 1), :].rearrange("p a d -> p (a d)") for j in range(TPB)]
                layer_norm_stats(dve, passed, mom_ready, chain, rows, stats, mom)
                dve.wait_ge(rstd_ready, i + 1)
                for j in range(R):
                    ins = dve.tensor_scalar(hat[:, j, :], rows[j], mom[:, j, 0:1], rstd[:, j:j + 1], ALU.subtract, ALU.mult)
                ins.then_inc(hat_ready, 1)

                def project(c):
                    ps, free = wait_fill(dve, i, F_QK + c)
                    if c >= 2:
                        dve.wait_ge(S_full, i * H + 2 * c - 2)
                    dve.tensor_copy(qk[:, c % 2, :, :].rearrange("p a t -> p (a t)"), ps[:, :]).then_inc(free, 1)

                def clip(h):
                    dve.wait_ge(E_exp, i * H + h + 1)
                    dve.tensor_scalar(E[:, h % 4, :, :], E[:, h % 4, :, :], LO, HI, ALU.max, ALU.min).then_inc(E_ready, 1)

                def normalise(c):
                    dve.wait_ge(O_full, i * NC + c + 1)
                    ov = o_view(c % 2)
                    chain(dve.reciprocal(rden[:, c % 2, :, :], ov[:, :, :, DH]))
                    for j in range(2):
                        ins = dve.tensor_tensor(On[:, :, 2 * c + j, :], ov[:, j, :, 0:DH],
                                                rden[:, c % 2, j, :].unsqueeze(2).broadcast_to([P, TPB, DH]), ALU.mult)
                    ins.then_inc(O_free, 1)

                project(0)
                for c in range(NC):
                    if c + 1 < NC:
                        project(c + 1)
                    clip(2 * c)
                    clip(2 * c + 1)
                    if c >= 1:
                        normalise(c - 1)
                normalise(NC - 1)
                chain(dve.tensor_tensor(res[:, :, :], xall[:, bass.ds(i * TPB, TPB), :], bo[:, :].unsqueeze(1).broadcast_to([P, TPB, D]), ALU.add))
                ps, free = wait_fill(dve, i, F_WO)
                ins = dve.tensor_tensor(res[:, :, :], res[:, :, :], ps[:, 0:TPB * D].rearrange("p (t d) -> p t d", d=D), ALU.add)
                chain(ins)
                dve.sem_inc(free, 1)
                rows2 = [res[:, j, :] for j in range(TPB)]
                layer_norm_stats(dve, passed, mom2_ready, chain, rows2, stats2, mom2)
                dve.wait_ge(rstd2_ready, i + 1)
                for j in range(TPB):
                    ins = dve.tensor_scalar(xin[j], rows2[j], mom2[:, j, 0:1], rstd2[:, j:j + 1], ALU.subtract, ALU.mult)
                chain(ins)
                dve.sem_inc(x_done, 1)
                chain.close()

        @block.tensor
        def _(pe):
            pe.wait_ge(loaded, LOADS)
            with pe.Fori(0, B) as i:
                def fill(n):
                    pe.wait_ge(misc_free[n % 2], i * PER_BANK + n // 2 + 1)
                    return psM[n % 2], misc_full[n % 2]

                pe.wait_ge(hat_ready, i + 1)
                ps, full = fill(0)
                for j in range(R):
                    ins = pe.transpose(ps[:, j * P:(j + 1) * P], hat[:, j, :], ident[:, :])
                ins.then_inc(full, 1)
                pe.wait_ge(catT_ready, i + 1)
                for n in range(4):
                    ps, full = fill(F_V + n)
                    pe.matmul(ps[:, :], ctxT[:, (n // 2) * P:(n // 2 + 1) * P], wv[:, (n % 2) * 512:(n % 2 + 1) * 512],
                              start=True, stop=True).then_inc(full, 1)

                def project(c):
                    ps, full = fill(F_QK + c)
                    pe.matmul(ps[:, 0:L], wq[:, c * P:(c + 1) * P], latT[:, :], start=True, stop=True)
                    pe.matmul(ps[:, L:2 * L], wk[:, c * P:(c + 1) * P], ctxT[:, :], start=True, stop=True).then_inc(full, 1)

                def scores(c):
                    n = F_QK + c
                    pe.wait_ge(misc_free[n % 2], i * PER_BANK + n // 2 + 2)
                    for h in (2 * c, 2 * c + 1):
                        r = slice((h % 2) * DH, (h % 2) * DH + DH)
                        if h >= 4:
                            pe.wait_ge(E_exp, i * H + h - 3)
                        for kt in range(TPB):
                            ins = pe.matmul(psS[h % 4][:, kt, :], qk[r, c % 2, 1, kt * P:(kt + 1) * P], qk[r, c % 2, 0, :], start=True, stop=True)
                        ins.then_inc(S_full, 1)

                def times_v(c):
                    pe.wait_ge(E_ready, i * H + 2 * c + 2)
                    if c >= 2:
                        pe.wait_ge(O_free, i * NC + c - 1)
                    ov = o_view(c % 2)
                    for j in range(2):
                        h = 2 * c + j
                        for qt in range(TPB):
                            for kt in range(TPB):
                                ins = pe.matmul(ov[:, j, qt, :], E[:, h % 4, kt, qt * P:(qt + 1) * P], V1[:, kt, h, :], start=(kt == 0), stop=(kt == TPB - 1))
                    ins.then_inc(O_full, 1)

                project(0)
                for c in range(NC):
                    if c + 1 < NC:
                        project(c + 1)
                    scores(c)
                    if c >= 1:
                        times_v(c - 1)
                times_v(NC - 1)
                pe.wait_ge(O_free, i * NC + NC)
                for n in range(2 * TPB):
                    t, c0 = n // 2, (n % 2) * 4
                    ps, full = fill(F_OT + n)
                    for c in range(4):
                        h = 2 * (c0 + c)
                        ins = pe.transpose(ps[:, c * P:(c + 1) * P], On[:, t, h:h + 2, :].rearrange("p h d -> p (h d)"), ident[:, :])
                    ins.then_inc(full, 1)
                ps, full = fill(F_WO)
                n = F_WO - 1
                pe.wait_ge(misc_free[n % 2], i * PER_BANK + n // 2 + 2)
                for t in range(TPB):
                    for c in range(NC):
                        ins = pe.matmul(ps[:, t * D:(t + 1) * D], OT[:, c, t * P:(t + 1) * P], wo[:, c, :], start=(c == 0), stop=(c == NC - 1))
                ins.then_inc(full, 1)
                pe.wait_ge(x_done, i + 1)


W_QKV = 0
W_SCALE = W_QKV + 3 * INNER
W_LN = W_SCALE + 2 * DH
W_O = W_LN + 2
W_1 = W_O + INNER // P * D
W_B1 = W_1 + 2 * FF
W_2 = W_B1 + 2 * FF
W_B2 = W_2 + 3 * D
W_COLS = W_B2 + D
SHARE = -(-W_COLS // B)
W_PAD = SHARE * B


def window_layers(nc, xall, ident, eps_col, w, out):
    ITERS = DEPTH * B
    CH = INNER // P
    KEYS = 3 * WIN
    HQ = P // 2
    A_FILLS = 11
    C_FILLS = 6
    GH = H // 2

    with ExitStack() as ctx:
        def sb(name, shape, dt=F32):
            return ctx.enter_context(nc.sbuf_tensor(name, shape, dt))

        def sem(name):
            return ctx.enter_context(nc.semaphore(name))

        def ps(name, shape):
            return ctx.enter_context(nc.psum_tensor(name, shape, F32))

        W = sb("f_W", [P, 2, W_PAD])
        x0 = sb("f_x0", [P, TILES, D])
        base_tab = sb("f_base_tab", [P, TPB, 2, 2, DH])
        tab = sb("f_tab", [P, 2, 2, 2, DH])
        mask32 = sb("f_mask32", [P, TPB, KEYS])
        maskb = sb("f_maskb", [P, TPB, GH // 2, KEYS], BF16)
        identb = sb("f_identb", [P, P], BF16)
        consts = sb("f_consts", [P, 2])
        xsA = sb("f_xsA", [P, 2, D])
        xT = sb("f_xT", [P, 2, P])
        qkraw = sb("f_qkraw", [P, 2 * INNER])
        m12 = sb("f_m12", [P, 2, 2, INNER])
        sq = sb("f_sq", [P, 2 * INNER])
        ssq = sb("f_ssq", [P, 2 * H])
        lnq = sb("f_lnq", [P, 2 * H])
        rn0 = sb("f_rn0", [P, 2 * H])
        rn = sb("f_rn", [P, 2 * H])
        qkr = sb("f_qkr", [P, 2 * INNER])
        Vt = sb("f_Vt", [P, 2, INNER])
        V96 = sb("f_V96", [KEYS, 2, 2, INNER])
        qT = sb("f_qT", [P, 2, CH, P])
        kT = sb("f_kT", [P, 2, CH, WIN + P])
        mx = sb("f_mx", [P, 2, GH])
        Pr = sb("f_Pr", [P, 2, GH, KEYS])
        den = sb("f_den", [P, 2, GH])
        rden = sb("f_rden", [P, 2, GH])
        PT = sb("f_PT", [KEYS, 2, 4, P])
        oT = sb("f_oT", [P, 2, CH, P])
        x1 = sb("f_x1", [P, 2, D])
        x1b = sb("f_x1b", [P, 2, D])
        xsC = sb("f_xsC", [P, 2, D])
        statC = sb("f_statC", [P, 6])
        momC = sb("f_momC", [P, 2])
        lnC = sb("f_lnC", [P, 1])
        rstdC = sb("f_rstdC", [P, 1])
        hatC = sb("f_hatC", [P, D])
        xnT = sb("f_xnT", [P, P])
        ga = sb("f_ga", [P, 2, FF])
        ge = sb("f_ge", [P, FF])
        hh = sb("f_hh", [P, FF])
        hT = sb("f_hT", [P, 3, P])
        fin_s = sb("f_fin_s", [P, TILES, 6])
        fin_m = sb("f_fin_m", [P, TILES, 2])
        fin_ln = sb("f_fin_ln", [P, TILES])
        fin_r = sb("f_fin_r", [P, TILES])
        psA = [ps(f"f_psA{j}", [P, 512]) for j in range(2)]
        psC = [ps(f"f_psC{j}", [P, 512]) for j in range(2)]
        psS = ps("f_psS", [P, 2, 512])
        psP = ps("f_psP", [P, 4, P])
        psO = ps("f_psO", [P, 4, P])
        S4 = psS[:, :, 0:GH // 2 * KEYS].rearrange("p a (c k) -> p a c k", k=KEYS)

        passed = sem("f_passed")
        loaded = sem("f_loaded")
        setup = sem("f_setup")
        w_loaded = sem("f_w_loaded")
        xsA_ready = [sem(f"f_xsA_ready{t}") for t in range(2)]
        xsC_ready = [sem(f"f_xsC_ready{t}") for t in range(2)]
        V96_ready = [sem(f"f_V96_ready{t}") for t in range(2)]
        A_full = [sem(f"f_A_full{j}") for j in range(2)]
        A_free = [sem(f"f_A_free{j}") for j in range(2)]
        C_full = [sem(f"f_C_full{j}") for j in range(2)]
        C_free = [sem(f"f_C_free{j}") for j in range(2)]
        kprev_ready = sem("f_kprev_ready")
        raw_ready = sem("f_raw_ready")
        m12_done = sem("f_m12_done")
        sq_ready = sem("f_sq_ready")
        ssq_ready = sem("f_ssq_ready")
        act_chain = sem("f_act_chain")
        rn0_ready = sem("f_rn0_ready")
        rn_ready = sem("f_rn_ready")
        tab_ready = sem("f_tab_ready")
        rot_done = sem("f_rot_done")
        qkr_ready = sem("f_qkr_ready")
        V_ready = sem("f_V_ready")
        S_full = sem("f_S_full")
        mx_done = sem("f_mx_done")
        S_free = sem("f_S_free")
        exp_done = sem("f_exp_done")
        den_done = sem("f_den_done")
        rden_ready = sem("f_rden_ready")
        Pr_ready = sem("f_Pr_ready")
        P_full = sem("f_P_full")
        P_free = sem("f_P_free")
        O_full = sem("f_O_full")
        O_free = sem("f_O_free")
        x1_ready = sem("f_x1_ready")
        x1b_ready = sem("f_x1b_ready")
        dve_chain = sem("f_dve_chain")
        momC_ready = sem("f_momC_ready")
        rstdC_ready = sem("f_rstdC_ready")
        hatC_ready = sem("f_hatC_ready")
        ga_ready = sem("f_ga_ready")
        ge_ready = sem("f_ge_ready")
        hh_ready = sem("f_hh_ready")
        x2_done = sem("f_x2_done")
        fin_mom = sem("f_fin_mom")
        fin_rstd = sem("f_fin_rstd")
        fin_done = sem("f_fin_done")
        fin_chain = sem("f_fin_chain")
        stored = sem("f_stored")

        block = ctx.enter_context(nc.Block())

        def slots(eng, slot):
            slot(0, 0, True, False, False)
            slot(0, 1, True, True, False)
            with eng.Fori(1, ITERS) as i:
                slot(i, 0, True, True, True)
                slot(i, 1, True, True, True)
            slot(ITERS, 0, False, True, True)
            slot(ITERS, 1, False, False, True)

        def a_fill(i, t, n):
            f = A_FILLS * t + n - 4
            return f % 2, i * A_FILLS + f // 2

        def c_fill(i, t, n):
            return n % 2, (i * 2 + (t - 2)) * (C_FILLS // 2) + n // 2

        def filled(eng, full, fill):
            eng.wait_ge(full[fill[0]], fill[1] + 1)

        def weights(i_of_layer, col, n):
            if isinstance(i_of_layer, int):
                s = i_of_layer // B % 2
                return W[:, s, col:col + n]
            s = (i_of_layer // B) % 2
            return W[:, :, :].rearrange("p s c -> p (s c)")[:, bass.ds(s * W_PAD + col, n)]

        def tile_of(i, t):
            if isinstance(i, int):
                return xall[:, i % B * TPB + t, :]
            return xall[:, bass.ds((i % B) * TPB + t, 1), :].rearrange("p a d -> p (a d)")

        def weights_here(eng, i):
            eng.wait_ge(w_loaded, (i + 1) * 16)

        @block.sync
        def _(sp):
            for dst, src in [(base_tab[:, :, :, :, :], w["f_tab"]), (mask32[:, :, :], w["f_mask"])]:
                sp.dma_start(dst, src).then_inc(loaded, 16)
            sp.dma_start(W[:, 0, 0:7 * SHARE], w["f_W"][:, 0, 0:7, :].rearrange("p b c -> p (b c)")).then_inc(w_loaded, 16)
            sp.wait_ge(w_loaded, 16)
            sp.dma_start(W[:, 0, 7 * SHARE:], w["f_W"][:, 0, 7, :]).then_inc(w_loaded, 16)
            sp.wait_ge(setup, 1)

            def shift_in(i, t):
                a = i * 2 + t
                sp.wait_ge(x2_done, a + 1)
                sp.wait_ge(raw_ready, a * 4 + 1)
                src = tile_of(i, t)
                sp.dma_start(xsA[:, t, 0:64], src[:, 0:64]).then_inc(xsA_ready[t], 16)
                sp.dma_start(xsA[1:P, t, 64:D], src[0:P - 1, 64:D]).then_inc(xsA_ready[t], 16)
                if t == 1:
                    sp.dma_start(xsA[0:1, 1, 64:D], tile_of(i, 0)[P - 1:P, 64:D]).then_inc(xsA_ready[t], 16)

            def slot(i, t, A, Bst, C):
                if Bst:
                    q = 1 - t
                    v = i * 2 + (t - 1)
                    sp.wait_ge(V_ready, v * 2 + 2)
                    sp.wait_ge(O_free, v * 2 + 2)
                    sp.dma_start(V96[WIN:KEYS, q, 0, :], Vt[0:HQ, q, :]).then_inc(V96_ready[q], 16)
                    sp.dma_start(V96[:, q, 1, :], Vt[WIN:P, q, :]).then_inc(V96_ready[q], 16)
                    if q == 1:
                        sp.dma_start(V96[0:WIN, 1, 0, :], Vt[P - WIN:P, 0, :]).then_inc(V96_ready[q], 16)
                if C:
                    wu = i * 2 + (t - 2)
                    sp.wait_ge(x1_ready, wu + 1)
                    sp.dma_start(xsC[:, t, 0:64], x1[:, t, 0:64]).then_inc(xsC_ready[t], 16)
                    sp.dma_start(xsC[1:P, t, 64:D], x1[0:P - 1, t, 64:D]).then_inc(xsC_ready[t], 16)
                    if t == 1:
                        sp.dma_start(xsC[0:1, 1, 64:D], x1[P - 1:P, 0, 64:D]).then_inc(xsC_ready[t], 16)
                if A:
                    shift_in(i + t, 1 - t)
                if t == 1 and A:
                    sp.wait_ge(x2_done, i * 2 + 16)
                    sp.wait_ge(w_loaded, (i + 2) * 16)
                    if isinstance(i, int):
                        sp.dma_start(W[:, 1, 0:SHARE], w["f_W"][:, 1, 0, :]).then_inc(w_loaded, 16)
                    else:
                        nxt = (i // B + 1)
                        dst = W[:, :, :].rearrange("p s (b c) -> p (s b) c", b=B)[:, bass.ds((nxt % 2) * B + i % B, 1), :]
                        src = w["f_W"].rearrange("p l b c -> p (l b) c")[:, bass.ds((i + B) % (DEPTH * B), 1), :]
                        sp.dma_start(dst, src).then_inc(w_loaded, 16)

            shift_in(0, 0)
            slots(sp, slot)
            sp.wait_ge(w_loaded, (ITERS + 2) * 16)
            sp.wait_ge(xsA_ready[0], (ITERS + 1) * 32)
            sp.wait_ge(fin_done, 1)
            sp.dma_start(out, xall[:, :, :]).then_inc(stored, 16)
            sp.wait_ge(stored, 16)

        @block.gpsimd
        def _(pool):
            pool.wait_ge(setup, 1)
            pool.sem_inc(rot_done, 1)

            def normalise_probs(v, g):
                pool.wait_ge(rden_ready, v * 2 + g + 1)
                pool.tensor_tensor(Pr[:, g, :, :], Pr[:, g, :, :], rden[:, g, :].unsqueeze(2).broadcast_to([P, GH, KEYS]),
                                   ALU.mult).then_inc(Pr_ready, 1)

            def rotate(u, j):
                pool.wait_ge(m12_done, u * 2 + j + 3)
                mv = m12[:, j, :, :].rearrange("p m (h two d) -> p m h two d", two=2, d=DH // 2)
                pool.tensor_tensor(mv[:, 0], mv[:, 0], mv[:, 1, :, ::-1, :], ALU.add).then_inc(rot_done, 1)

            def scale(u, j):
                pool.wait_ge(rot_done, u * 2 + j + 2)
                pool.wait_ge(rn_ready, u + 1)
                pool.tensor_tensor(qkr[:, j * INNER:(j + 1) * INNER].rearrange("p (h d) -> p h d", d=DH),
                                   m12[:, j, 0, :].rearrange("p (h d) -> p h d", d=DH),
                                   rn[:, j * H:(j + 1) * H].unsqueeze(2).broadcast_to([P, H, DH]), ALU.mult).then_inc(qkr_ready, 1)

            def slot(i, t, A, Bst, C):
                u, v, wu = i * 2 + t, i * 2 + (t - 1), i * 2 + (t - 2)
                if A:
                    weights_here(pool, i)
                    pool.wait_ge(m12_done, u * 2 + 1)
                    alone(pool, passed)
                    sc = weights(i, W_SCALE, 2 * DH).rearrange("p (a d) -> p a d", a=2).unsqueeze(2).broadcast_to([P, 2, 2, DH])
                    pool.tensor_tensor(tab[:, t, :, :, :], base_tab[:, t, :, :, :], sc, ALU.mult).then_inc(tab_ready, 1)
                if C:
                    weights_here(pool, i)
                    pool.wait_ge(x1_ready, wu + 1)
                    pool.wait_ge(x2_done, wu + 15)
                    alone(pool, passed)
                    pool.tensor_tensor(x1b[:, t, :], x1[:, t, :], weights(i - 1, W_B2, D), ALU.add).then_inc(x1b_ready, 1)
                if A:
                    rotate(u, 0)
                    rotate(u, 1)
                if Bst:
                    normalise_probs(v, 0)
                if A:
                    if Bst:
                        f = a_fill(i, t, 3)
                        filled(pool, A_full, f)
                        f = a_fill(i, t, 2)
                        filled(pool, A_full, f)
                    scale(u, 0)
                if C:
                    pool.wait_ge(x2_done, wu + 16)
                    pool.wait_ge(ge_ready, wu + 1)
                    pool.wait_ge(ga_ready, wu * 2 + 2)
                    pool.tensor_tensor(hh[:, :], ga[:, 0, :], ge[:, :], ALU.mult).then_inc(hh_ready, 1)
                if Bst:
                    normalise_probs(v, 1)
                if A:
                    scale(u, 1)

            slots(pool, slot)

        @block.scalar
        def _(act):
            act.wait_ge(setup, 1)
            act.sem_inc(raw_ready, 8)
            act.sem_inc(P_free, 4)
            act.sem_inc(O_free, 4)
            for j in range(2):
                act.sem_inc(A_free[j], 1)
                act.sem_inc(C_free[j], 1)
            act.activation(x0[:, :, :], xall[:, :, :], ACT.Copy).then_inc(act_chain, 1)

            def slot(i, t, A, Bst, C):
                q = 1 - t
                u, v, wu = i * 2 + t, i * 2 + (t - 1), i * 2 + (t - 2)
                if Bst:
                    for n in range(4):
                        f = a_fill(i, t, n)
                        filled(act, A_full, f)
                        c0 = (n // 2) * 4
                        src = psA[f[0]][:, :].rearrange("p (c q) -> p c q", c=4)
                        dst = kT[:, q, c0:c0 + 4, WIN:WIN + P] if n % 2 else qT[:, q, c0:c0 + 4, :]
                        act.activation(dst, src, ACT.Copy).then_inc(A_free[f[0]], 1)
                    if q == 1:
                        act.activation(kT[:, 1, :, 0:WIN], kT[:, 0, :, P:P + WIN], ACT.Copy).then_inc(kprev_ready, 1)
                if A:
                    f = a_fill(i, t, 4)
                    filled(act, A_full, f)
                    act.activation(xT[:, t, :], psA[f[0]][:, 0:P], ACT.Copy).then_inc(A_free[f[0]], 1)
                    act.wait_ge(m12_done, u * 2 + 2)
                    for n in range(4):
                        f = a_fill(i, t, 5 + n)
                        filled(act, A_full, f)
                        act.activation(qkraw[:, n * 512:(n + 1) * 512], psA[f[0]][:, :], ACT.Copy).then_inc(raw_ready, 1)
                        act.wait_ge(raw_ready, u * 4 + n + 9)
                        act.sem_inc(A_free[f[0]], 1)
                    act.activation(sq[:, :], qkraw[:, :], ACT.Square).then_inc(sq_ready, 1)
                if Bst:
                    act.wait_ge(S_free, v * 2 + 2)
                    act.activation(Pr[:, 0, :, :], Pr[:, 0, :, :], ACT.Exp).then_inc(exp_done, 1)
                if C:
                    act.wait_ge(momC_ready, wu + 1)
                    act.activation(lnC[:, :], momC[:, 1:2], ACT.Ln, bias=eps_col).then_inc(act_chain, 1)
                    act.wait_ge(act_chain, wu + 2)
                    act.activation(rstdC[:, :], lnC[:, :], ACT.Exp, scale=-0.5).then_inc(rstdC_ready, 1)
                if A:
                    act.wait_ge(ssq_ready, u + 1)
                    act.activation(lnq[:, :], ssq[:, :], ACT.Ln, bias=consts[:, 0:1], scale=SSQ_SCALE).then_inc(rn0_ready, 1)
                    act.wait_ge(rn0_ready, u * 2 + 1)
                    act.activation(rn0[:, :], lnq[:, :], ACT.Exp, bias=consts[:, 1:2], scale=-0.5).then_inc(rn0_ready, 1)
                if C:
                    f = c_fill(i, t, 1)
                    filled(act, C_full, f)
                    weights_here(act, i)
                    alone(act, passed)
                    act.activation(xnT[:, :], psC[f[0]][:, 0:P], ACT.Identity, bias=weights(i - 1, W_LN + 1, 1), scale=weights(i - 1, W_LN, 1)).then_inc(C_free[f[0]], 1)
                if Bst:
                    act.wait_ge(S_free, v * 2 + 3)
                    act.activation(Pr[:, 1, :, :], Pr[:, 1, :, :], ACT.Exp).then_inc(exp_done, 1)

                def evacuate_probs(g, j):
                    act.wait_ge(P_full, v * 4 + 2 * g + j + 1)
                    act.activation(PT[:, j, :, :], psP[0:KEYS, :, :], ACT.Copy).then_inc(P_free, 1)

                def evacuate_v(j):
                    f = a_fill(i, t, 9 + j)
                    filled(act, A_full, f)
                    if j == 0 and not isinstance(i, int):
                        act.wait_ge(V96_ready[1], i * 48)
                        if t == 0:
                            act.wait_ge(V96_ready[0], i * 32)
                    act.activation(Vt[:, t, j * 512:(j + 1) * 512], psA[f[0]][:, :], ACT.Copy).then_inc(V_ready, 1)
                    act.wait_ge(V_ready, u * 2 + j + 1)
                    act.sem_inc(A_free[f[0]], 1)

                def evacuate_out(g):
                    act.wait_ge(O_full, v * 2 + g + 1)
                    act.activation(oT[:, q, 4 * g:4 * g + 4, :], psO[:, :, :], ACT.Copy).then_inc(O_free, 1)

                if Bst:
                    evacuate_probs(0, 0)
                if A:
                    evacuate_v(0)
                if Bst:
                    evacuate_probs(0, 1)
                if C:
                    act.wait_ge(ga_ready, wu * 2 + 1)
                    act.activation(ge[:, :], ga[:, 1, :], ACT.Gelu).then_inc(ge_ready, 1)
                    f = c_fill(i, t, 4)
                    filled(act, C_full, f)
                    act.activation(hT[:, 0:2, :], psC[f[0]][:, 0:2 * P].rearrange("p (c q) -> p c q", c=2), ACT.Copy)
                    act.activation(hT[0:FF - 2 * P, 2, :], psC[f[0]][0:FF - 2 * P, 2 * P:3 * P], ACT.Copy).then_inc(C_free[f[0]], 1)
                if Bst:
                    evacuate_out(0)
                    evacuate_probs(1, 0)
                if A:
                    evacuate_v(1)
                if Bst:
                    evacuate_probs(1, 1)
                    evacuate_out(1)

            slots(act, slot)
            act.wait_ge(fin_mom, 1)
            act.activation(fin_ln[:, :], fin_m[:, :, 1], ACT.Ln, bias=eps_col).then_inc(fin_chain, 1)
            act.wait_ge(fin_chain, 2)
            act.activation(fin_r[:, :], fin_ln[:, :], ACT.Exp, scale=-0.5).then_inc(fin_rstd, 1)

        @block.vector
        def _(dve):
            dve.memset(xsA[0:1, 0, 64:D], 0.0)
            dve.memset(xsC[0:1, 0, 64:D], 0.0)
            dve.memset(kT[:, 0, :, 0:WIN], 0.0)
            dve.memset(V96[0:WIN, 0, 0, :], 0.0)
            dve.memset(consts[:, 0:1], 2.0 ** -70)
            dve.memset(consts[:, 1:2], 0.5 * float(np.log(SSQ_SCALE)))
            dve.wait_ge(loaded, 32)
            dve.tensor_copy(identb[:, :], ident[:, :])
            dve.tensor_copy(maskb[:, :, :, :], mask32[:, :, :].unsqueeze(2).broadcast_to([P, TPB, GH // 2, KEYS])).then_inc(setup, 1)
            dve.sem_inc(m12_done, 2)
            dve.sem_inc(S_free, 1)
            dve.sem_inc(x2_done, 16)

            def less_maximum(v, g):
                dve.wait_ge(S_full, v * 2 + g + 1)
                dve.tensor_reduce(mx[:, g, :].rearrange("p (a c) -> p a c", a=2), S4, axis=AX.X, op=ALU.max).then_inc(mx_done, 1)
                dve.wait_ge(mx_done, v * 2 + g + 1)
                dve.wait_ge(P_free, v * 4 + 2 * g + 2)
                mb = mx[:, g, :].rearrange("p (a c) -> p a c", a=2).unsqueeze(3).broadcast_to([P, 2, GH // 2, KEYS])
                dve.tensor_tensor(Pr[:, g, :, :].rearrange("p (a c) k -> p a c k", a=2), S4, mb, ALU.subtract).then_inc(S_free, 1)

            def denominators(v, g):
                dve.wait_ge(exp_done, v * 2 + g + 1)
                dve.tensor_reduce(den[:, g, :], Pr[:, g, :, :], axis=AX.X, op=ALU.add).then_inc(den_done, 1)
                dve.wait_ge(den_done, v * 2 + g + 1)
                dve.reciprocal(rden[:, g, :], den[:, g, :]).then_inc(rden_ready, 1)

            def slot(i, t, A, Bst, C):
                u, v, wu = i * 2 + t, i * 2 + (t - 1), i * 2 + (t - 2)
                if C:
                    f = c_fill(i, t, 0)
                    filled(dve, C_full, f)
                    dve.tensor_tensor(x1[:, t, :], psC[f[0]][:, 0:D], tile_of(i - 1, t), ALU.add).then_inc(x1_ready, 1)
                    dve.wait_ge(x1_ready, wu + 1)
                    dve.sem_inc(C_free[f[0]], 1)
                if Bst:
                    less_maximum(v, 0)
                if A:
                    dve.wait_ge(tab_ready, u + 1)
                    if Bst:
                        dve.wait_ge(qkr_ready, u * 2)
                    for j in range(2):
                        dve.wait_ge(raw_ready, u * 4 + 2 * j + 10)
                        rv = qkraw[:, j * INNER:(j + 1) * INNER].rearrange("p (h d) -> p h d", d=DH)
                        dve.tensor_tensor(m12[:, j, :, :].rearrange("p m (h d) -> p m h d", d=DH),
                                          rv.unsqueeze(1).broadcast_to([P, 2, H, DH]),
                                          tab[:, t, j, :, :].unsqueeze(2).broadcast_to([P, 2, H, DH]), ALU.mult).then_inc(m12_done, 1)
                if C:
                    dve.wait_ge(xsC_ready[t], i * (32, 48)[t])
                    dve.bn_stats(out=statC[:, :], in_=xsC[:, t, :]).then_inc(dve_chain, 1)
                    dve.wait_ge(dve_chain, wu + 1)
                    alone(dve, passed)
                    dve.bn_aggr(out=momC[:, :], in_=statC[:, :]).then_inc(momC_ready, 1)
                if A:
                    dve.wait_ge(sq_ready, u + 1)
                    dve.tensor_reduce(ssq[:, :], sq[:, :].rearrange("p (h d) -> p h d", d=DH), axis=AX.X, op=ALU.add).then_inc(ssq_ready, 1)
                if C:
                    dve.wait_ge(rstdC_ready, wu + 1)
                    dve.tensor_scalar(hatC[:, :], xsC[:, t, :], momC[:, 0:1], rstdC[:, :], ALU.subtract, ALU.mult).then_inc(hatC_ready, 1)
                if Bst:
                    denominators(v, 0)
                if A:
                    dve.wait_ge(rn0_ready, u * 2 + 2)
                    dve.tensor_scalar(rn[:, 0:H], rn0[:, 0:H], 1e12, 8.0, ALU.min, ALU.mult)
                    dve.tensor_scalar(rn[:, H:2 * H], rn0[:, H:2 * H], 1e12, None, ALU.min).then_inc(rn_ready, 1)
                if Bst:
                    less_maximum(v, 1)
                if C:
                    weights_here(dve, i)
                    for n in (1, 0):
                        f = c_fill(i, t, 2 + (1 - n))
                        filled(dve, C_full, f)
                        dve.tensor_tensor(ga[:, n, :], psC[f[0]][:, 0:FF], weights(i - 1, W_B1 + n * FF, FF), ALU.add).then_inc(ga_ready, 1)
                        dve.wait_ge(ga_ready, wu * 2 + 2 - n)
                        dve.sem_inc(C_free[f[0]], 1)
                if Bst:
                    denominators(v, 1)
                if C:
                    f = c_fill(i, t, 5)
                    filled(dve, C_full, f)
                    dve.wait_ge(x1b_ready, wu + 1)
                    dve.tensor_tensor(tile_of(i - 1, t), psC[f[0]][:, 0:D], x1b[:, t, :], ALU.add).then_inc(x2_done, 1)
                    dve.wait_ge(x2_done, wu + 17)
                    dve.sem_inc(C_free[f[0]], 1)

            slots(dve, slot)
            dve.wait_ge(act_chain, 1)
            dve.tensor_tensor(x0[:, :, :], x0[:, :, :], xall[:, :, :], ALU.add).then_inc(fin_chain, 1)
            dve.wait_ge(fin_chain, 1)
            for j in range(TILES):
                ins = dve.bn_stats(out=fin_s[:, j, :], in_=x0[:, j, :])
            ins.then_inc(dve_chain, 1)
            dve.wait_ge(dve_chain, ITERS * 2 + 1)
            for j in range(TILES):
                ins = dve.bn_aggr(out=fin_m[:, j, :], in_=fin_s[:, j, :])
            ins.then_inc(fin_mom, 1)
            dve.wait_ge(fin_rstd, 1)
            for j in range(TILES):
                ins = dve.tensor_scalar(xall[:, j, :], x0[:, j, :], fin_m[:, j, 0:1], fin_r[:, j:j + 1], ALU.subtract, ALU.mult)
            ins.then_inc(fin_done, 1)

        @block.tensor
        def _(pe):
            pe.wait_ge(setup, 1)

            def fill(ring, free, f):
                pe.wait_ge(free[f[0]], f[1] + 1)
                return ring[f[0]]

            def read_back(free, f):
                pe.wait_ge(free[f[0]], f[1] + 2)

            def slot(i, t, A, Bst, C):
                q = 1 - t
                u, v, wu = i * 2 + t, i * 2 + (t - 1), i * 2 + (t - 2)

                def scores(g):
                    pe.wait_ge(S_free, v * 2 + g + 1)
                    for par in range(2):
                        pe.matmul(psS[:, par, 0:GH // 2 * KEYS], identb[:, :], maskb[:, q, :, :].rearrange("p c k -> p (c k)"), start=True, stop=False, skip_group_check=True)
                    for par in range(2):
                        r = slice(par * DH, par * DH + DH)
                        for c in range(4):
                            for half in range(2):
                                k0 = half * HQ
                                ins = pe.matmul(S4[half * HQ:(half + 1) * HQ, par, c, :], qT[r, q, 4 * g + c, k0:k0 + HQ],
                                                kT[r, q, 4 * g + c, k0:k0 + KEYS], start=False, stop=True, skip_group_check=True)
                    ins.then_inc(S_full, 1)

                def transpose_probs(g, j):
                    pe.wait_ge(Pr_ready, v * 2 + g + 1)
                    pe.wait_ge(P_free, v * 4 + 2 * g + j + 4)
                    for n in range(4):
                        h = 4 * j + n
                        ins = pe.transpose(psP[0:KEYS, n, :], Pr[:, g, (h % 2) * 4 + h // 2, :], ident[:, :])
                    ins.then_inc(P_full, 1)

                def times_v(g, j):
                    pe.wait_ge(P_free, v * 4 + 2 * g + j + 5)
                    if j == 0:
                        pe.wait_ge(O_free, v * 2 + g + 4)
                    if g == 0 and j == 0:
                        n_dma = (32, 48)[q]
                        pe.wait_ge(V96_ready[q], (i + (1 if q == 0 else 0)) * n_dma)
                    for n in range(4):
                        h = 4 * j + n
                        hh_ = 8 * g + h
                        for half in range(2):
                            ins = pe.matmul(psO[(h % 2) * DH:(h % 2) * DH + DH, h // 2, half * HQ:(half + 1) * HQ],
                                            V96[:, q, half, hh_ * DH:(hh_ + 1) * DH], PT[:, j, n, half * HQ:(half + 1) * HQ], start=True, stop=True)
                    if j == 1:
                        ins.then_inc(O_full, 1)

                if C:
                    pe.wait_ge(O_free, wu * 2 + 6)
                    f = c_fill(i, t, 0)
                    p = fill(psC, C_free, f)
                    for c in range(CH):
                        ins = pe.matmul(p[:, 0:D], oT[:, t, c, :], weights(i - 1, W_O + c * D, D), start=(c == 0), stop=(c == CH - 1))
                    ins.then_inc(C_full[f[0]], 1)
                if Bst:
                    pe.wait_ge(qkr_ready, v * 2 + 2)
                    for n in range(4):
                        f = a_fill(i, t, n)
                        p = fill(psA, A_free, f)
                        for c in range(4):
                            col = (n % 2) * INNER + ((n // 2) * 4 + c) * P
                            ins = pe.transpose(p[:, c * P:(c + 1) * P], qkr[:, col:col + P], ident[:, :])
                        ins.then_inc(A_full[f[0]], 1)
                if A:
                    pe.wait_ge(xsA_ready[t], (i + 1) * (32, 48)[t])
                    f = a_fill(i, t, 4)
                    p = fill(psA, A_free, f)
                    pe.transpose(p[:, 0:P], xsA[:, t, :], ident[:, :]).then_inc(A_full[f[0]], 1)
                    read_back(A_free, f)
                    weights_here(pe, i)

                def project(n):
                    f = a_fill(i, t, 5 + n)
                    p = fill(psA, A_free, f)
                    pe.matmul(p[:, :], xT[:, t, :], weights(i, W_QKV + n * 512, 512), start=True, stop=True).then_inc(A_full[f[0]], 1)

                if A:
                    for n in range(4):
                        project(n)
                if Bst:
                    read_back(A_free, a_fill(i, t, 2))
                    read_back(A_free, a_fill(i, t, 3))
                    if q == 1:
                        pe.wait_ge(kprev_ready, i)
                    scores(0)
                if C:
                    pe.wait_ge(hatC_ready, wu + 1)
                    f = c_fill(i, t, 1)
                    p = fill(psC, C_free, f)
                    pe.transpose(p[:, 0:P], hatC[:, :], ident[:, :]).then_inc(C_full[f[0]], 1)
                if Bst:
                    scores(1)
                if C:
                    read_back(C_free, f)
                    for n in (1, 0):
                        f = c_fill(i, t, 2 + (1 - n))
                        p = fill(psC, C_free, f)
                        pe.matmul(p[:, 0:FF], xnT[:, :], weights(i - 1, W_1 + n * FF, FF), start=True, stop=True).then_inc(C_full[f[0]], 1)
                if Bst:
                    transpose_probs(0, 0)
                if A:
                    project(4)
                if Bst:
                    transpose_probs(0, 1)
                    times_v(0, 0)
                if C:
                    pe.wait_ge(hh_ready, wu + 1)
                    f = c_fill(i, t, 4)
                    p = fill(psC, C_free, f)
                    for c in range(3):
                        n = min(P, FF - c * P)
                        ins = pe.transpose(p[0:n, c * P:(c + 1) * P], hh[:, c * P:c * P + n], ident[:, :])
                    ins.then_inc(C_full[f[0]], 1)
                if Bst:
                    times_v(0, 1)
                    transpose_probs(1, 0)
                if A:
                    project(5)
                if Bst:
                    transpose_probs(1, 1)
                    times_v(1, 0)
                if C:
                    read_back(C_free, f)
                    f = c_fill(i, t, 5)
                    p = fill(psC, C_free, f)
                    for c in range(3):
                        n = min(P, FF - c * P)
                        ins = pe.matmul(p[:, 0:D], hT[0:n, c, :], weights(i - 1, W_2 + c * D, D)[0:n, :], start=(c == 0), stop=(c == 2))
                    ins.then_inc(C_full[f[0]], 1)
                if Bst:
                    times_v(1, 1)

            slots(pe, slot)


def host_layout(x):
    f = np.float32
    up = lambda a: np.ascontiguousarray(a, dtype=f)
    w = {}
    w["x"] = up(x["x"].reshape(TILES, P, D).transpose(1, 0, 2))
    w["ident"] = np.eye(P, dtype=f)
    G = P // NST
    W = x["L0_attn_W_ll"]
    kc = lambda a: up(a.T.reshape(2, P, -1).transpose(1, 0, 2))
    w["m_up1"] = up(x["L0_attn_W_up1"].T)
    w["m_up2"] = up(x["L0_attn_W_up2"].T)
    w["m_down"] = kc(x["L0_attn_W_down"])
    w["m_wdel"] = kc(W[:DI])
    w["m_wB"] = kc(np.tile(W[DI:DI + NST], (G, 1)))
    w["m_wC"] = kc(np.tile(W[DI + NST:], (G, 1)))
    b = x["L0_attn_b_ll"]
    w["m_cols"] = up(np.concatenate([
        x["L0_attn_ln_g"][:, None], x["L0_attn_ln_b"][:, None], x["L0_attn_conv_b"].reshape(2, P).T,
        b[:DI].reshape(2, P).T, np.tile(b[DI:DI + NST], G)[:, None], np.tile(b[DI + NST:], G)[:, None],
        x["L0_attn_conv_w"].reshape(2, P, 4).transpose(1, 0, 2).reshape(P, 8)], axis=1))
    w["m_alog"] = up(x["L0_attn_A_log"].reshape(DI // G, P).T)
    w["m_bdown"] = up(np.broadcast_to(x["L0_attn_b_down"], (P, D)))
    col = np.arange(NST * P)
    w["m_sel"] = up(col[None, :] // NST == np.arange(P)[:, None])
    w["m_pick"] = up(np.arange(P)[None, None, :] == (np.arange(P)[:, None, None] // NST + G * np.arange(P // G)[None, :, None]))
    w["ctx"] = up(x["ctx_1024"].reshape(TILES, P, D).transpose(1, 0, 2))
    w["x_cols"] = up(np.stack([x["L0_xattn_ln_l_w"], x["L0_xattn_ln_l_b"], x["L0_xattn_ln_c_w"], x["L0_xattn_ln_c_b"]], axis=1))
    w["x_wq"] = up(x["L0_xattn_Wq"])
    w["x_wk"] = up(x["L0_xattn_Wkv"][:, :INNER])
    w["x_wv"] = up(x["L0_xattn_Wkv"][:, INNER:])
    w["x_wo"] = up(x["L0_xattn_Wo"].reshape(INNER // P, P, D).transpose(1, 0, 2))
    w["x_bo"] = up(np.broadcast_to(x["L0_xattn_bo"], (P, D)))
    pack = np.zeros((P, DEPTH, W_PAD), f)
    rows = lambda a: np.broadcast_to(a, (P,) + a.shape)
    for l in range(DEPTH):
        put = lambda col, a: pack[:a.shape[0], l, col:col + a.shape[1]].__setitem__(slice(None), a)
        put(W_QKV, x["L0_ffn_Wqkv"][l])
        put(W_SCALE, rows(x["L0_ffn_q_scale"][l]))
        put(W_SCALE + DH, rows(x["L0_ffn_k_scale"][l]))
        put(W_LN, x["L0_ffn_ln_g"][l][:, None])
        put(W_LN + 1, x["L0_ffn_ln_b"][l][:, None])
        put(W_O, x["L0_ffn_Wo"][l].reshape(INNER // P, P, D).transpose(1, 0, 2).reshape(P, -1))
        put(W_1, x["L0_ffn_W1"][l])
        put(W_B1, rows(x["L0_ffn_b1"][l]))
        for c in range(3):
            put(W_2 + c * D, x["L0_ffn_W2"][l][c * P:(c + 1) * P])
        put(W_B2, rows(x["L0_ffn_b2"][l]))
    w["f_W"] = pack.reshape(P, DEPTH, B, SHARE)
    half = np.arange(0, DH, 2, dtype=f)
    inv_freq = f(1.0) / f(10000.0) ** (half / f(DH))
    t = np.arange(L, dtype=f)
    freqs = t[:, None] * inv_freq[None, :]
    base = (half + f(0.4 * DH)) / f(1.4 * DH)
    scale = base[None, :] ** ((t - L // 2) / f(WIN // 2))[:, None]
    two = lambda a: np.concatenate([a, a], -1)
    cos, sin, scale = two(np.cos(freqs)), np.concatenate([np.sin(freqs), -np.sin(freqs)], -1), two(scale)
    tab = np.stack([np.stack([cos * s, sin * s]) for s in (scale, f(1.0) / scale)])
    w["f_tab"] = up(tab.reshape(2, 2, TPB, P, DH).transpose(3, 2, 0, 1, 4))
    it = np.arange(L)
    key = (it // (P // 2) * (P // 2) - WIN)[:, None] + np.arange(3 * WIN)[None, :]
    seen = (key <= it[:, None]) & (key >= it[:, None] - WIN) & (key >= 0)
    w["f_mask"] = up(np.where(seen, 0.0, -1e30).reshape(TPB, P, 3 * WIN).transpose(1, 0, 2))
    return w


def decoder_layer(nc, w, out):
    with ExitStack() as ctx:
        xall = ctx.enter_context(nc.sbuf_tensor("xall", [P, TILES, D], F32))
        ident = ctx.enter_context(nc.sbuf_tensor("ident", [P, P], F32))
        eps = ctx.enter_context(nc.sbuf_tensor("eps", [P, 1], F32))
        eps_ready = ctx.enter_context(nc.semaphore("eps_ready"))
        with nc.Block() as block:
            @block.vector
            def _(dve):
                dve.memset(eps[:, :], EPS).then_inc(eps_ready, 1)

            @block.scalar
            def _(act):
                act.wait_ge(eps_ready, 1)

        state_space_block(nc, xall, ident, eps[:, :], w)
        cross_attention_block(nc, xall, ident, eps[:, :], w)
        window_layers(nc, xall, ident, eps[:, :], w, out)


def kernel(**inputs):
    import concourse.bacc as bacc
    from concourse.bass_utils import run_bass_kernel_spmd

    nc = bacc.Bacc("TRN2", target_bir_lowering=False, num_devices=1)
    arrays = host_layout({k: np.asarray(v) for k, v in inputs.items()})
    aps = {k: nc.dram_tensor(f"in_{k}", a.shape, mybir.dt.from_np(a.dtype), kind="ExternalInput").ap() for k, a in arrays.items()}
    out = nc.dram_tensor("out_x", (P, TILES, D), F32, kind="ExternalOutput").ap()
    decoder_layer(nc, aps, out)
    r = run_bass_kernel_spmd(nc, [{f"in_{k}": a for k, a in arrays.items()}], core_ids=[0])
    return np.asarray(r.results[0]["out_x"]).transpose(1, 0, 2).reshape(B, L, D)
```

```python
from contextlib import ExitStack

import numpy as np

import concourse.bass as bass
from concourse import mybir

F32 = mybir.dt.float32
F32R = mybir.dt.float32r
BF16 = mybir.dt.bfloat16
ALU = mybir.AluOpType
ACT = mybir.ActivationFunctionType
AX = mybir.AxisListType

P = 128
B, L, D = 8, 256, 128
TILES = B * L // P
TPB = L // P
EPS = 1e-5
NST = 16
DI = 256
H, DH = 16, 64
INNER = H * DH
DEPTH = 6
WIN = 32
FF = 341
SSQ_SCALE = 2.0 ** 24


def alone(eng, passed):
    eng.sem_inc(passed, 1)


def layer_norm_stats(dve, passed, act_ready, chain, rows, stats, moments):
    for j, row in enumerate(rows):
        ins = dve.bn_stats(out=stats[:, j, :], in_=row)
    chain(ins)
    alone(dve, passed)
    for j in range(len(rows)):
        ins = dve.bn_aggr(out=moments[:, j, :], in_=stats[:, j, :])
    ins.then_inc(act_ready, 1)


LN_EXP = "natural_log_exp_and_others"


class Chain:

    def __init__(self, eng, sem, base, per_iter):
        self.eng, self.sem, self.base, self.per_iter, self.n = eng, sem, base, per_iter, 0

    def __call__(self, ins):
        self.n += 1
        ins.then_inc(self.sem, 1)
        self.eng.wait_ge(self.sem, self.base + self.n)

    def close(self):
        assert self.n == self.per_iter, self.n


def state_space_block(nc, xall, ident, eps_col, w, debug=None):
    NB = 2
    T = NB * L
    NT = NB * TPB
    STEPS = B // NB
    NC = DI // P
    G = P // NST
    UPC = P // G
    UNITS = NC * UPC
    NLOAD = 15
    DVE_CHAIN = 22

    with ExitStack() as ctx:
        def sb(name, shape, dt=F32):
            return ctx.enter_context(nc.sbuf_tensor(name, shape, dt))

        def sem(name):
            return ctx.enter_context(nc.semaphore(name))

        up1 = sb("m_up1", [P, DI])
        up2 = sb("m_up2", [P, DI])
        down = sb("m_down", [P, NC, D])
        wdel = sb("m_wdel", [P, NC, DI])
        wB = sb("m_wB", [P, NC, P])
        wC = sb("m_wC", [P, NC, P])
        cols = sb("m_cols", [P, 2 + 3 * NC + NC * 4])
        ln_g, ln_b = cols[:, 0:1], cols[:, 1:2]
        conv_b = cols[:, 2:2 + NC]
        b_del = cols[:, 2 + NC:2 + 2 * NC]
        b_BC = cols[:, 2 + 2 * NC:2 + 3 * NC]
        conv_w = cols[:, 2 + 3 * NC:2 + 7 * NC].rearrange("p (c k) -> p c k", c=NC)
        alog = sb("m_alog", [P, UNITS])
        bdown = sb("m_bdown", [P, D])
        sel32 = sb("m_sel32", [P, UPC * P])
        sel = sb("m_sel", [P, UPC * P], F32R)
        pick = sb("m_pick", [P, UPC, P])
        summ = sb("m_summ", [P, UNITS, P])
        eA = sb("m_eA", [P, UNITS])
        negA = sb("m_negA", [P, UNITS])
        invA = sb("m_invA", [P, UNITS])
        stats = sb("m_stats", [P, NT, 6])
        mom = sb("m_mom", [P, NT, 2])
        lnv = sb("m_lnv", [P, NT])
        rstd = sb("m_rstd", [P, NT])
        xhat = sb("m_xhat", [P, NT, D])
        xnT = sb("m_xnT", [P, T])
        xpad = sb("m_xpad", [P, NC, NB, 3 + L])
        cv = sb("m_cv", [P, NC, NB, L])
        xc = sb("m_xc", [P, NC, T])
        xch = sb("m_xch", [P, NC, T], F32R)
        xcl = sb("m_xcl", [P, NC, T], F32R)
        gate = sb("m_gate", [P, NC, T])
        pre = sb("m_pre", [P, NC, T])
        ea = sb("m_ea", [P, NC, T])
        u1 = sb("m_u1", [P, NC, T])
        lu = sb("m_lu", [P, NC, T])
        dl = sb("m_dl", [P, NC, T])
        dlh = sb("m_dlh", [P, NC, T], F32R)
        dll = sb("m_dll", [P, NC, T], F32R)
        Bt = sb("m_Bt", [P, T])
        Ct = sb("m_Ct", [P, T])
        Ab = sb("m_Ab", [P, 2, T])
        XB = sb("m_XB", [P, 2, T])
        U = sb("m_U", [P, 2, T])
        Hs = sb("m_Hs", [P, 2, T])
        HC = sb("m_HC", [P, 2, T])
        Yg = sb("m_Yg", [P, NC, T])
        res = sb("m_res", [P, NT, D])
        psD = [ctx.enter_context(nc.psum_tensor(f"m_psD{j}", [P, T], F32)) for j in range(2)]
        psX = [ctx.enter_context(nc.psum_tensor(f"m_psX{j}", [P, T], F32)) for j in range(2)]
        psY = [ctx.enter_context(nc.psum_tensor(f"m_psY{j}", [P, T], F32)) for j in range(NC)]
        psM = [ctx.enter_context(nc.psum_tensor(f"m_psM{j}", [P, T], F32)) for j in range(2)]

        passed = sem("m_passed")
        loaded = sem("m_loaded")
        sel_ready = sem("m_sel_ready")
        eA_ready = sem("m_eA_ready")
        dve_chain = sem("m_dve_chain")
        act_chain = sem("m_act_chain")
        mom_ready = sem("m_mom_ready")
        rstd_ready = sem("m_rstd_ready")
        xhat_ready = sem("m_xhat_ready")
        misc_full = sem("m_misc_full")
        xnT_ready = sem("m_xnT_ready")
        xpad_ready = sem("m_xpad_ready")
        cv_ready = sem("m_cv_ready")
        xc_ready = sem("m_xc_ready")
        pre_ready = sem("m_pre_ready")
        u1_ready = sem("m_u1_ready")
        ea_ready = sem("m_ea_ready")
        lu_ready = sem("m_lu_ready")
        split_ready = sem("m_split_ready")
        BC_ready = sem("m_BC_ready")
        bcast_full = sem("m_bcast_full")
        Ab_ready = sem("m_Ab_ready")
        XB_done = sem("m_XB_done")
        U_done = sem("m_U_done")
        H_ready = sem("m_H_ready")
        HC_ready = sem("m_HC_ready")
        sum_done = sem("m_sum_done")
        Yg_ready = sem("m_Yg_ready")
        step_done = sem("m_step_done")
        MISC = 1 + NC + NC + 2 + NC + 1

        block = ctx.enter_context(nc.Block())

        @block.sync
        def _(sp):
            for dst, src in [(xall[:, :, :], w["x"]), (ident[:, :], w["ident"]), (cols[:, :], w["m_cols"]),
                             (up1[:, :], w["m_up1"]),
                             (wdel[:, :, :], w["m_wdel"]), (wB[:, :, :], w["m_wB"]), (wC[:, :, :], w["m_wC"]),
                             (alog[:, :], w["m_alog"]), (sel32[:, :], w["m_sel"]), (pick[:, :, :], w["m_pick"]),
                             (up2[:, :], w["m_up2"]), (down[:, :, :], w["m_down"]),
                             (bdown[:, :], w["m_bdown"])]:
                sp.dma_start(dst, src).then_inc(loaded, 16)
        LOADS = 16 * 13

        @block.gpsimd
        def _(pool):
            with pool.Fori(0, STEPS) as i:
                for k in range(UNITS):
                    pool.wait_ge(H_ready, i * UNITS + k + 3)
                    pool.wait_ge(sum_done, i * UNITS + k + 1)
                    pool.tensor_tensor(HC[:, k % 2, :], Hs[:, k % 2, :], Ct[:, :], ALU.mult).then_inc(HC_ready, 1)

        @block.scalar
        def _(act):
            act.preload_act_table_set(LN_EXP)
            act.wait_ge(loaded, LOADS)
            act.activation(eA[:, :], alog[:, :], ACT.Exp).then_inc(eA_ready, 1)
            act.wait_ge(sel_ready, 2)
            with act.Fori(0, STEPS) as i:
                def rsqrt_of_variance(n):
                    act.wait_ge(mom_ready, i * 2 + n)
                    act.activation(lnv[:, :], mom[:, :, 1], ACT.Ln, bias=eps_col).then_inc(act_chain, 1)
                    act.wait_ge(act_chain, i * 2 + n)
                    act.activation(rstd[:, :], lnv[:, :], ACT.Exp, scale=-0.5).then_inc(rstd_ready, 1)

                rsqrt_of_variance(1)
                act.wait_ge(misc_full, i * MISC + 1)
                act.activation(xnT[:, :], psM[0][:, :], ACT.Identity, bias=ln_b, scale=ln_g).then_inc(xnT_ready, 1)
                for c in range(NC):
                    act.wait_ge(misc_full, i * MISC + 2 + c)
                    for b in range(NB):
                        ins = act.activation(xpad[:, c, b, 3:3 + L], psM[(1 + c) % 2][:, b * L:(b + 1) * L], ACT.Copy)
                    ins.then_inc(xpad_ready, 1)
                for c in range(NC):
                    act.wait_ge(cv_ready, i * NC + c + 1)
                    act.activation(xc[:, c, :], cv[:, c, :, :].rearrange("p b t -> p (b t)"), ACT.Silu).then_inc(xc_ready, 1)
                for c in range(NC):
                    act.wait_ge(misc_full, i * MISC + 4 + c)
                    act.activation(gate[:, c, :], psM[(3 + c) % 2][:, :], ACT.Silu).then_inc(xnT_ready, 1)
                act.preload_act_table_set(LN_EXP)
                for j, dst in enumerate((Bt, Ct)):
                    act.wait_ge(misc_full, i * MISC + 6 + j)
                    act.activation(dst[:, :], psM[(5 + j) % 2][:, :], ACT.Identity, bias=b_BC[:, j:j + 1]).then_inc(BC_ready, 1)
                for c in range(NC):
                    act.wait_ge(misc_full, i * MISC + 8 + c)
                    act.activation(pre[:, c, :], psM[(7 + c) % 2][:, :], ACT.Identity, bias=b_del[:, c:c + 1]).then_inc(pre_ready, 1)
                    act.wait_ge(pre_ready, i * 2 * NC + 2 * c + 1)
                    act.activation(ea[:, c, :], pre[:, c, :], ACT.Abs).then_inc(pre_ready, 1)
                    act.wait_ge(pre_ready, i * 2 * NC + 2 * c + 2)
                    act.activation(ea[:, c, :], ea[:, c, :], ACT.Exp, scale=-1.0).then_inc(ea_ready, 1)
                for c in range(NC):
                    act.wait_ge(u1_ready, i * NC + c + 1)
                    act.activation(lu[:, c, :], u1[:, c, :], ACT.Ln).then_inc(lu_ready, 1)
                for k in range(UNITS):
                    act.wait_ge(bcast_full, i * UNITS + k + 1)
                    act.wait_ge(H_ready, i * UNITS + k + 1)
                    act.activation(Ab[:, k % 2, :], psD[k % 2][:, :], ACT.Exp, scale=negA[:, k:k + 1]).then_inc(Ab_ready, 1)
                rsqrt_of_variance(2)

        @block.vector
        def _(dve):
            dve.wait_ge(loaded, LOADS)
            dve.tensor_copy(sel[:, :], sel32[:, :]).then_inc(sel_ready, 1)
            dve.memset(xpad[:, :, :, 0:3], 0.0)
            dve.sem_inc(H_ready, 2)
            dve.wait_ge(eA_ready, 1)
            dve.tensor_scalar(negA[:, :], eA[:, :], -1.0, None, ALU.mult).then_inc(sel_ready, 1)
            dve.wait_ge(sel_ready, 2)
            dve.reciprocal(invA[:, :], negA[:, :]).then_inc(sel_ready, 1)
            dve.wait_ge(sel_ready, 3)
            for k in range(UNITS):
                ins = dve.tensor_scalar(summ[:, k, :], pick[:, k % UPC, :], invA[:, k:k + 1], None, ALU.mult)
            ins.then_inc(sel_ready, 1)
            with dve.Fori(0, STEPS) as i:
                chain = Chain(dve, dve_chain, i * DVE_CHAIN, DVE_CHAIN)

                def normalise(n, rows, outs):
                    layer_norm_stats(dve, passed, mom_ready, chain, rows, stats, mom)
                    dve.wait_ge(rstd_ready, i * 2 + n)
                    for j in range(NT):
                        ins = dve.tensor_scalar(outs[j], rows[j], mom[:, j, 0:1], rstd[:, j:j + 1], ALU.subtract, ALU.mult)
                    return ins

                xin = [xall[:, bass.ds(i * NT + j, 1), :].rearrange("p a d -> p (a d)") for j in range(NT)]
                normalise(1, xin, [xhat[:, j, :] for j in range(NT)]).then_inc(xhat_ready, 1)
                for c in range(NC):
                    dve.wait_ge(xpad_ready, i * NC + c + 1)
                    chain(dve.tensor_scalar(cv[:, c, :, :], xpad[:, c, :, 0:L], conv_w[:, c, 0:1], conv_b[:, c:c + 1], ALU.mult, ALU.add))
                    for k in range(1, 4):
                        ins = dve.scalar_tensor_tensor(out=cv[:, c, :, :], in0=xpad[:, c, :, k:k + L], scalar=conv_w[:, c, k:k + 1],
                                                       in1=cv[:, c, :, :], op0=ALU.mult, op1=ALU.add)
                        if k < 3:
                            chain(ins)
                    ins.then_inc(cv_ready, 1)
                for c in range(NC):
                    dve.wait_ge(xc_ready, i * NC + c + 1)
                    chain(dve.tensor_copy(xch[:, c, :], xc[:, c, :]))
                    dve.tensor_tensor(xcl[:, c, :], xc[:, c, :], xch[:, c, :].bitcast(F32), ALU.subtract).then_inc(split_ready, 1)
                for c in range(NC):
                    dve.wait_ge(ea_ready, i * NC + c + 1)
                    chain(dve.tensor_scalar(u1[:, c, :], ea[:, c, :], 1.0, None, ALU.add))
                    dve.sem_inc(u1_ready, 1)
                    dve.scalar_tensor_tensor(out=ea[:, c, :], in0=u1[:, c, :], scalar=-1.0, in1=ea[:, c, :], op0=ALU.add, op1=ALU.subtract)
                    chain(dve.tensor_scalar(pre[:, c, :], pre[:, c, :], 0.0, None, ALU.max))
                    dve.wait_ge(lu_ready, i * NC + c + 1)
                    chain(dve.tensor_tensor(dl[:, c, :], lu[:, c, :], ea[:, c, :], ALU.subtract))
                    chain(dve.tensor_tensor(dl[:, c, :], dl[:, c, :], pre[:, c, :], ALU.add))
                    chain(dve.tensor_copy(dlh[:, c, :], dl[:, c, :]))
                    dve.tensor_tensor(dll[:, c, :], dl[:, c, :], dlh[:, c, :].bitcast(F32), ALU.subtract).then_inc(split_ready, 1)
                dve.wait_ge(BC_ready, i * 2 + 1)
                for k in range(UNITS):
                    s = k % 2
                    dve.wait_ge(bcast_full, i * UNITS + k + 1)
                    dve.tensor_tensor(XB[:, s, :], psX[s][:, :], Bt[:, :], ALU.mult).then_inc(XB_done, 1)
                    dve.wait_ge(XB_done, i * UNITS + k + 1)
                    dve.wait_ge(Ab_ready, i * UNITS + k + 1)
                    dve.scalar_tensor_tensor(out=U[:, s, :], in0=Ab[:, s, :], scalar=1.0, in1=XB[:, s, :],
                                             op0=ALU.subtract, op1=ALU.mult).then_inc(U_done, 1)
                    dve.wait_ge(U_done, i * UNITS + k + 1)
                    dve.wait_ge(HC_ready, i * UNITS + k + 1)
                    for b in range(NB):
                        ins = dve.tensor_tensor_scan(Hs[:, s, b * L:(b + 1) * L], Ab[:, s, b * L:(b + 1) * L],
                                                     U[:, s, b * L:(b + 1) * L], 0.0, ALU.mult, ALU.add)
                    ins.then_inc(H_ready, 1)
                dve.wait_ge(sum_done, i * UNITS + UNITS + 2)
                for c in range(NC):
                    ins = dve.tensor_tensor(Yg[:, c, :], psY[c][:, :], gate[:, c, :], ALU.mult)
                ins.then_inc(Yg_ready, 1)
                xt = xall[:, bass.ds(i * NT, NT), :]
                chain(dve.scalar_tensor_tensor(out=res[:, :, :], in0=xt, scalar=2.0,
                                               in1=bdown[:, :].unsqueeze(1).broadcast_to([P, NT, D]), op0=ALU.mult, op1=ALU.add))
                dve.wait_ge(misc_full, i * MISC + MISC)
                chain(dve.tensor_tensor(res[:, :, :], res[:, :, :], psM[1][:, :].rearrange("p (t d) -> p t d", d=D), ALU.add))
                normalise(2, [res[:, j, :] for j in range(NT)], xin).then_inc(step_done, 1)
                chain.close()

        @block.tensor
        def _(pe):
            pe.sem_inc(sum_done, 2)
            pe.sem_inc(HC_ready, 2)
            pe.wait_ge(loaded, LOADS)
            pe.wait_ge(sel_ready, 4)
            with pe.Fori(0, STEPS) as i:
                pe.wait_ge(xhat_ready, i + 1)
                for j in range(NT):
                    ins = pe.transpose(psM[0][:, j * P:(j + 1) * P], xhat[:, j, :], ident[:, :])
                ins.then_inc(misc_full, 1)
                pe.wait_ge(xnT_ready, i * 3 + 1)
                for c in range(NC):
                    pe.matmul(psM[(1 + c) % 2][:, :], up1[:, c * P:(c + 1) * P], xnT[:, :], start=True, stop=True).then_inc(misc_full, 1)
                for c in range(NC):
                    pe.wait_ge(xpad_ready, i * NC + c + 1)
                    pe.matmul(psM[(3 + c) % 2][:, :], up2[:, c * P:(c + 1) * P], xnT[:, :], start=True, stop=True).then_inc(misc_full, 1)
                pe.wait_ge(xc_ready, i * NC + NC)
                for j, wt in enumerate((wB, wC)):
                    pe.wait_ge(xnT_ready, i * 3 + 2 + j)
                    for c in range(NC):
                        ins = pe.matmul(psM[(5 + j) % 2][:, :], wt[:, c, :], xc[:, c, :], start=(c == 0), stop=(c == NC - 1))
                    ins.then_inc(misc_full, 1)
                for m in range(NC):
                    pe.wait_ge(BC_ready, i * 2 + m + 1)
                    for c in range(NC):
                        ins = pe.matmul(psM[(7 + m) % 2][:, :], wdel[:, c, m * P:(m + 1) * P], xc[:, c, :], start=(c == 0), stop=(c == NC - 1))
                    ins.then_inc(misc_full, 1)

                def add_states(k):
                    pe.wait_ge(HC_ready, i * UNITS + k + 3)
                    pe.matmul(psY[k // UPC][:, :], summ[:, k, :], HC[:, k % 2, :], start=(k % UPC == 0), stop=(k % UPC == UPC - 1)).then_inc(sum_done, 1)

                pe.wait_ge(split_ready, i * 2 * NC + 2 * NC)
                for k in range(UNITS):
                    c, g = k // UPC, k % UPC
                    s = k % 2
                    if k >= 2:
                        pe.wait_ge(Ab_ready, i * UNITS + k - 1)
                        pe.wait_ge(XB_done, i * UNITS + k - 1)
                    for ps, hi, lo in ((psD[s], dlh, dll), (psX[s], xch, xcl)):
                        pe.matmul(ps[:, :], sel[:, g * P:(g + 1) * P], hi[:, c, :], start=True, stop=False)
                        ins = pe.matmul(ps[:, :], sel[:, g * P:(g + 1) * P], lo[:, c, :], start=False, stop=True)
                    ins.then_inc(bcast_full, 1)
                    if k >= 2:
                        add_states(k - 2)
                add_states(UNITS - 2)
                add_states(UNITS - 1)
                pe.wait_ge(Yg_ready, i + 1)
                for j in range(NT):
                    for c in range(NC):
                        ins = pe.matmul(psM[1][:, j * P:(j + 1) * P], Yg[:, c, j * P:(j + 1) * P], down[:, c, :], start=(c == 0), stop=(c == NC - 1))
                ins.then_inc(misc_full, 1)
                pe.wait_ge(step_done, i + 1)


def cross_attention_block(nc, xall, ident, eps_col, w):
    NC = INNER // P
    R = 2 * TPB
    FILLS = 1 + 4 + NC + 2 * TPB + 1
    PER_BANK = FILLS // 2
    assert FILLS % 2 == 0
    LOADS = 16 * 8
    DVE_CHAIN = 13
    LO, HI = float(np.exp(-11.0)), float(np.exp(11.0))

    with ExitStack() as ctx:
        def sb(name, shape, dt=F32):
            return ctx.enter_context(nc.sbuf_tensor(name, shape, dt))

        def sem(name):
            return ctx.enter_context(nc.semaphore(name))

        ctxall = sb("x_ctx", [P, TILES, D])
        wq = sb("x_wq", [P, INNER])
        wk = sb("x_wk", [P, INNER])
        wv = sb("x_wv", [P, INNER])
        wo = sb("x_wo", [P, NC, D])
        cols = sb("x_cols", [P, 4])
        bo = sb("x_bo", [P, D])
        stats = sb("x_stats", [P, R, 6])
        mom = sb("x_mom", [P, R, 2])
        lnv = sb("x_lnv", [P, R])
        rstd = sb("x_rstd", [P, R])
        hat = sb("x_hat", [P, R, D])
        latT = sb("x_latT", [P, L])
        ctxT = sb("x_ctxT", [P, L])
        V1 = sb("x_V1", [P, TPB, H, DH + 1])
        qk = sb("x_qk", [P, 2, 2, L])
        E = sb("x_E", [P, 4, TPB, L])
        rden = sb("x_rden", [P, 2, 2, TPB])
        On = sb("x_On", [P, TPB, H, DH])
        OT = sb("x_OT", [P, NC, L])
        res = sb("x_res", [P, TPB, D])
        stats2 = sb("x_stats2", [P, TPB, 6])
        mom2 = sb("x_mom2", [P, TPB, 2])
        lnv2 = sb("x_lnv2", [P, TPB])
        rstd2 = sb("x_rstd2", [P, TPB])
        psM = [ctx.enter_context(nc.psum_tensor(f"x_psM{j}", [P, 512], F32)) for j in range(2)]
        psS = [ctx.enter_context(nc.psum_tensor(f"x_psS{j}", [P, TPB, L], F32)) for j in range(4)]
        psO = [ctx.enter_context(nc.psum_tensor(f"x_psO{j}", [P, 512], F32)) for j in range(2)]

        def o_view(j):
            return psO[j][:, 0:4 * (DH + 1)].rearrange("p (h t e) -> p h t e", h=2, t=TPB)

        passed = sem("x_passed")
        loaded = sem("x_loaded")
        ones_ready = sem("x_ones_ready")
        dve_chain = sem("x_dve_chain")
        act_chain = sem("x_act_chain")
        mom_ready = sem("x_mom_ready")
        rstd_ready = sem("x_rstd_ready")
        mom2_ready = sem("x_mom2_ready")
        rstd2_ready = sem("x_rstd2_ready")
        hat_ready = sem("x_hat_ready")
        misc_full = [sem(f"x_misc_full{j}") for j in range(2)]
        misc_free = [sem(f"x_misc_free{j}") for j in range(2)]
        catT_ready = sem("x_catT_ready")
        S_full = sem("x_S_full")
        E_exp = sem("x_E_exp")
        E_ready = sem("x_E_ready")
        O_full = sem("x_O_full")
        O_free = sem("x_O_free")
        x_done = sem("x_x_done")

        block = ctx.enter_context(nc.Block())

        def wait_fill(eng, i, n):
            eng.wait_ge(misc_full[n % 2], i * PER_BANK + n // 2 + 1)
            return psM[n % 2], misc_free[n % 2]

        F_V, F_QK, F_OT, F_WO = 1, 5, 5 + NC, 5 + NC + 2 * TPB

        @block.sync
        def _(sp):
            for dst, src in [(ctxall[:, :, :], w["ctx"]), (cols[:, :], w["x_cols"]), (wv[:, :], w["x_wv"]), (wq[:, :], w["x_wq"]),
                             (wk[:, :], w["x_wk"]), (wo[:, :, :], w["x_wo"]), (bo[:, :], w["x_bo"]), (ident[:, :], w["ident"])]:
                sp.dma_start(dst, src).then_inc(loaded, 16)

        @block.scalar
        def _(act):
            act.preload_act_table_set(LN_EXP)
            act.wait_ge(loaded, LOADS)
            act.wait_ge(ones_ready, 1)
            with act.Fori(0, B) as i:
                act.wait_ge(mom_ready, i + 1)
                act.activation(lnv[:, :], mom[:, :, 1], ACT.Ln, bias=eps_col).then_inc(act_chain, 1)
                act.wait_ge(act_chain, i * 2 + 1)
                act.activation(rstd[:, :], lnv[:, :], ACT.Exp, scale=-0.5).then_inc(rstd_ready, 1)
                ps, free = wait_fill(act, i, 0)
                act.activation(ctxT[:, :], ps[:, L:2 * L], ACT.Identity, bias=cols[:, 3:4], scale=cols[:, 2:3]).then_inc(catT_ready, 1)
                act.activation(latT[:, :], ps[:, 0:L], ACT.Identity, bias=cols[:, 1:2], scale=cols[:, 0:1]).then_inc(free, 1)
                for n in range(4):
                    ps, free = wait_fill(act, i, F_V + n)
                    act.activation(V1[:, n // 2, (n % 2) * 8:(n % 2) * 8 + 8, 0:DH],
                                   ps[:, :].rearrange("p (h d) -> p h d", d=DH), ACT.Copy).then_inc(free, 1)
                for h in range(H):
                    act.wait_ge(S_full, i * H + h + 1)
                    if h >= 4:
                        act.wait_ge(O_full, i * NC + (h - 4) // 2 + 1)
                    act.activation(E[:, h % 4, :, :], psS[h % 4][:, :, :], ACT.Exp, scale=DH ** -0.5).then_inc(E_exp, 1)
                for n in range(2 * TPB):
                    ps, free = wait_fill(act, i, F_OT + n)
                    t, c0 = n // 2, (n % 2) * 4
                    act.activation(OT[:, c0:c0 + 4, t * P:(t + 1) * P], ps[:, :].rearrange("p (c q) -> p c q", c=4), ACT.Copy).then_inc(free, 1)
                act.wait_ge(mom2_ready, i + 1)
                act.activation(lnv2[:, :], mom2[:, :, 1], ACT.Ln, bias=eps_col).then_inc(act_chain, 1)
                act.wait_ge(act_chain, i * 2 + 2)
                act.activation(rstd2[:, :], lnv2[:, :], ACT.Exp, scale=-0.5).then_inc(rstd2_ready, 1)

        @block.vector
        def _(dve):
            dve.sem_inc(misc_free[0], 1)
            dve.sem_inc(misc_free[1], 1)
            dve.memset(V1[:, :, :, DH:DH + 1], 1.0).then_inc(ones_ready, 1)
            dve.wait_ge(loaded, LOADS)
            with dve.Fori(0, B) as i:
                chain = Chain(dve, dve_chain, i * DVE_CHAIN, DVE_CHAIN)
                xin = [xall[:, bass.ds(i * TPB + j, 1), :].rearrange("p a d -> p (a d)") for j in range(TPB)]
                rows = xin + [ctxall[:, bass.ds(i * TPB + j, 1), :].rearrange("p a d -> p (a d)") for j in range(TPB)]
                layer_norm_stats(dve, passed, mom_ready, chain, rows, stats, mom)
                dve.wait_ge(rstd_ready, i + 1)
                for j in range(R):
                    ins = dve.tensor_scalar(hat[:, j, :], rows[j], mom[:, j, 0:1], rstd[:, j:j + 1], ALU.subtract, ALU.mult)
                ins.then_inc(hat_ready, 1)

                def project(c):
                    ps, free = wait_fill(dve, i, F_QK + c)
                    if c >= 2:
                        dve.wait_ge(S_full, i * H + 2 * c - 2)
                    dve.tensor_copy(qk[:, c % 2, :, :].rearrange("p a t -> p (a t)"), ps[:, :]).then_inc(free, 1)

                def clip(h):
                    dve.wait_ge(E_exp, i * H + h + 1)
                    dve.tensor_scalar(E[:, h % 4, :, :], E[:, h % 4, :, :], LO, HI, ALU.max, ALU.min).then_inc(E_ready, 1)

                def normalise(c):
                    dve.wait_ge(O_full, i * NC + c + 1)
                    ov = o_view(c % 2)
                    chain(dve.reciprocal(rden[:, c % 2, :, :], ov[:, :, :, DH]))
                    for j in range(2):
                        ins = dve.tensor_tensor(On[:, :, 2 * c + j, :], ov[:, j, :, 0:DH],
                                                rden[:, c % 2, j, :].unsqueeze(2).broadcast_to([P, TPB, DH]), ALU.mult)
                    ins.then_inc(O_free, 1)

                project(0)
                for c in range(NC):
                    if c + 1 < NC:
                        project(c + 1)
                    clip(2 * c)
                    clip(2 * c + 1)
                    if c >= 1:
                        normalise(c - 1)
                normalise(NC - 1)
                chain(dve.tensor_tensor(res[:, :, :], xall[:, bass.ds(i * TPB, TPB), :], bo[:, :].unsqueeze(1).broadcast_to([P, TPB, D]), ALU.add))
                ps, free = wait_fill(dve, i, F_WO)
                ins = dve.tensor_tensor(res[:, :, :], res[:, :, :], ps[:, 0:TPB * D].rearrange("p (t d) -> p t d", d=D), ALU.add)
                chain(ins)
                dve.sem_inc(free, 1)
                rows2 = [res[:, j, :] for j in range(TPB)]
                layer_norm_stats(dve, passed, mom2_ready, chain, rows2, stats2, mom2)
                dve.wait_ge(rstd2_ready, i + 1)
                for j in range(TPB):
                    ins = dve.tensor_scalar(xin[j], rows2[j], mom2[:, j, 0:1], rstd2[:, j:j + 1], ALU.subtract, ALU.mult)
                chain(ins)
                dve.sem_inc(x_done, 1)
                chain.close()

        @block.tensor
        def _(pe):
            pe.wait_ge(loaded, LOADS)
            with pe.Fori(0, B) as i:
                def fill(n):
                    pe.wait_ge(misc_free[n % 2], i * PER_BANK + n // 2 + 1)
                    return psM[n % 2], misc_full[n % 2]

                pe.wait_ge(hat_ready, i + 1)
                ps, full = fill(0)
                for j in range(R):
                    ins = pe.transpose(ps[:, j * P:(j + 1) * P], hat[:, j, :], ident[:, :])
                ins.then_inc(full, 1)
                pe.wait_ge(catT_ready, i + 1)
                for n in range(4):
                    ps, full = fill(F_V + n)
                    pe.matmul(ps[:, :], ctxT[:, (n // 2) * P:(n // 2 + 1) * P], wv[:, (n % 2) * 512:(n % 2 + 1) * 512],
                              start=True, stop=True).then_inc(full, 1)

                def project(c):
                    ps, full = fill(F_QK + c)
                    pe.matmul(ps[:, 0:L], wq[:, c * P:(c + 1) * P], latT[:, :], start=True, stop=True)
                    pe.matmul(ps[:, L:2 * L], wk[:, c * P:(c + 1) * P], ctxT[:, :], start=True, stop=True).then_inc(full, 1)

                def scores(c):
                    n = F_QK + c
                    pe.wait_ge(misc_free[n % 2], i * PER_BANK + n // 2 + 2)
                    for h in (2 * c, 2 * c + 1):
                        r = slice((h % 2) * DH, (h % 2) * DH + DH)
                        if h >= 4:
                            pe.wait_ge(E_exp, i * H + h - 3)
                        for kt in range(TPB):
                            ins = pe.matmul(psS[h % 4][:, kt, :], qk[r, c % 2, 1, kt * P:(kt + 1) * P], qk[r, c % 2, 0, :], start=True, stop=True)
                        ins.then_inc(S_full, 1)

                def times_v(c):
                    pe.wait_ge(E_ready, i * H + 2 * c + 2)
                    if c >= 2:
                        pe.wait_ge(O_free, i * NC + c - 1)
                    ov = o_view(c % 2)
                    for j in range(2):
                        h = 2 * c + j
                        for qt in range(TPB):
                            for kt in range(TPB):
                                ins = pe.matmul(ov[:, j, qt, :], E[:, h % 4, kt, qt * P:(qt + 1) * P], V1[:, kt, h, :], start=(kt == 0), stop=(kt == TPB - 1))
                    ins.then_inc(O_full, 1)

                project(0)
                for c in range(NC):
                    if c + 1 < NC:
                        project(c + 1)
                    scores(c)
                    if c >= 1:
                        times_v(c - 1)
                times_v(NC - 1)
                pe.wait_ge(O_free, i * NC + NC)
                for n in range(2 * TPB):
                    t, c0 = n // 2, (n % 2) * 4
                    ps, full = fill(F_OT + n)
                    for c in range(4):
                        h = 2 * (c0 + c)
                        ins = pe.transpose(ps[:, c * P:(c + 1) * P], On[:, t, h:h + 2, :].rearrange("p h d -> p (h d)"), ident[:, :])
                    ins.then_inc(full, 1)
                ps, full = fill(F_WO)
                n = F_WO - 1
                pe.wait_ge(misc_free[n % 2], i * PER_BANK + n // 2 + 2)
                for t in range(TPB):
                    for c in range(NC):
                        ins = pe.matmul(ps[:, t * D:(t + 1) * D], OT[:, c, t * P:(t + 1) * P], wo[:, c, :], start=(c == 0), stop=(c == NC - 1))
                ins.then_inc(full, 1)
                pe.wait_ge(x_done, i + 1)


W_QKV = 0
W_SCALE = W_QKV + 3 * INNER
W_LN = W_SCALE + 2 * DH
W_O = W_LN + 2
W_1 = W_O + INNER // P * D
W_B1 = W_1 + 2 * FF
W_2 = W_B1 + 2 * FF
W_B2 = W_2 + 3 * D
W_COLS = W_B2 + D
SHARE = -(-W_COLS // B)
W_PAD = SHARE * B


def window_layers(nc, xall, ident, eps_col, w, out):
    ITERS = DEPTH * B
    CH = INNER // P
    KEYS = 3 * WIN
    HQ = P // 2
    A_FILLS = 11
    D_FILLS = 5
    GH = H // 2

    with ExitStack() as ctx:
        def sb(name, shape, dt=F32):
            return ctx.enter_context(nc.sbuf_tensor(name, shape, dt))

        def sem(name):
            return ctx.enter_context(nc.semaphore(name))

        def ps(name, shape):
            return ctx.enter_context(nc.psum_tensor(name, shape, F32))

        W = sb("f_W", [P, 2, W_PAD])
        x0 = sb("f_x0", [P, TILES, D])
        base_tab = sb("f_base_tab", [P, TPB, 2, 2, DH])
        tab = sb("f_tab", [P, 2, 2, 2, DH])
        mask32 = sb("f_mask32", [P, TPB, KEYS])
        maskb = sb("f_maskb", [P, TPB, GH // 2, KEYS], BF16)
        identb = sb("f_identb", [P, P], BF16)
        consts = sb("f_consts", [P, 2])
        xsA = sb("f_xsA", [P, 2, D])
        xT = sb("f_xT", [P, 2, P])
        qkraw = sb("f_qkraw", [P, 2 * INNER])
        m12 = sb("f_m12", [P, 2, 2, INNER])
        sq = sb("f_sq", [P, 2 * INNER])
        ssq = sb("f_ssq", [P, 2 * H])
        lnq = sb("f_lnq", [P, 2 * H])
        rn0 = sb("f_rn0", [P, 2 * H])
        rn = sb("f_rn", [P, 2 * H])
        qkr = sb("f_qkr", [P, 2 * INNER])
        Vt = sb("f_Vt", [P, 2, INNER])
        V96 = sb("f_V96", [KEYS, 2, 2, INNER])
        qT = sb("f_qT", [P, 2, CH, P])
        kT = sb("f_kT", [P, 2, CH, WIN + P])
        mx = sb("f_mx", [P, 2, GH])
        Pr = sb("f_Pr", [P, 2, GH, KEYS])
        den = sb("f_den", [P, 2, GH])
        rden = sb("f_rden", [P, 2, GH])
        PT = sb("f_PT", [KEYS, 2, 4, P])
        oT = sb("f_oT", [P, 2, CH, P])
        x1 = sb("f_x1", [P, 2, D])
        x1b = sb("f_x1b", [P, 2, D])
        xsC = sb("f_xsC", [P, 2, D])
        statC = sb("f_statC", [P, 6])
        momC = sb("f_momC", [P, 2])
        lnC = sb("f_lnC", [P, 1])
        rstdC = sb("f_rstdC", [P, 1])
        hatC = sb("f_hatC", [P, 2, D])
        xnT = sb("f_xnT", [P, P])
        ga = sb("f_ga", [P, 2, FF])
        ge = sb("f_ge", [P, FF])
        hh = sb("f_hh", [P, FF])
        hT = sb("f_hT", [P, 3, P])
        fin_s = sb("f_fin_s", [P, TILES, 6])
        fin_m = sb("f_fin_m", [P, TILES, 2])
        fin_ln = sb("f_fin_ln", [P, TILES])
        fin_r = sb("f_fin_r", [P, TILES])
        psA = [ps(f"f_psA{j}", [P, 512]) for j in range(2)]
        psD = [ps(f"f_psD{j}", [P, 512]) for j in range(2)]
        psS = ps("f_psS", [P, 2, 512])
        psP = ps("f_psP", [P, 4, P])
        psO = ps("f_psO", [P, 4, P])
        S4 = psS[:, :, 0:GH // 2 * KEYS].rearrange("p a (c k) -> p a c k", k=KEYS)

        passed = sem("f_passed")
        loaded = sem("f_loaded")
        setup = sem("f_setup")
        w_loaded = sem("f_w_loaded")
        xsA_ready = [sem(f"f_xsA_ready{t}") for t in range(2)]
        xsC_ready = [sem(f"f_xsC_ready{t}") for t in range(2)]
        V96_ready = [sem(f"f_V96_ready{t}") for t in range(2)]
        A_full = [sem(f"f_A_full{j}") for j in range(2)]
        A_free = [sem(f"f_A_free{j}") for j in range(2)]
        D_full = [sem(f"f_D_full{j}") for j in range(2)]
        D_free = [sem(f"f_D_free{j}") for j in range(2)]
        kprev_ready = sem("f_kprev_ready")
        raw_ready = sem("f_raw_ready")
        m12_done = sem("f_m12_done")
        sq_ready = sem("f_sq_ready")
        ssq_ready = sem("f_ssq_ready")
        act_chain = sem("f_act_chain")
        rn0_ready = sem("f_rn0_ready")
        rn_ready = sem("f_rn_ready")
        tab_ready = sem("f_tab_ready")
        rot_done = sem("f_rot_done")
        qkr_ready = sem("f_qkr_ready")
        V_ready = sem("f_V_ready")
        S_full = sem("f_S_full")
        mx_done = sem("f_mx_done")
        S_free = sem("f_S_free")
        exp_done = sem("f_exp_done")
        den_done = sem("f_den_done")
        rden_ready = sem("f_rden_ready")
        Pr_ready = sem("f_Pr_ready")
        P_full = sem("f_P_full")
        P_free = sem("f_P_free")
        O_full = sem("f_O_full")
        O_free = sem("f_O_free")
        x1_ready = sem("f_x1_ready")
        x1b_ready = sem("f_x1b_ready")
        dve_chain = sem("f_dve_chain")
        momC_ready = sem("f_momC_ready")
        rstdC_ready = sem("f_rstdC_ready")
        wo_full = sem("f_wo_full")
        xnT_ready = sem("f_xnT_ready")
        hatC_ready = sem("f_hatC_ready")
        ga_ready = sem("f_ga_ready")
        ge_ready = sem("f_ge_ready")
        hh_ready = sem("f_hh_ready")
        x2_done = sem("f_x2_done")
        fin_mom = sem("f_fin_mom")
        fin_rstd = sem("f_fin_rstd")
        fin_done = sem("f_fin_done")
        fin_chain = sem("f_fin_chain")
        stored = sem("f_stored")

        block = ctx.enter_context(nc.Block())

        def slots(eng, slot):
            slot(0, 0, "A")
            slot(0, 1, "AB")
            slot(1, 0, "ABC")
            slot(1, 1, "ABCD")
            with eng.Fori(2, ITERS) as i:
                slot(i, 0, "ABCD")
                slot(i, 1, "ABCD")
            slot(ITERS, 0, "BCD")
            slot(ITERS, 1, "CD")
            slot(ITERS + 1, 0, "D")

        def is_first(i):
            return isinstance(i, int) and i == 0

        def a_fill(i, t, n):
            if is_first(i) and t == 0 and n < 4:
                n += 4
            elif isinstance(i, int) and i == ITERS:
                n -= 4
            f = A_FILLS * t + n + 1
            return f % 2, i * A_FILLS + f // 2

        A_FIRST = (0, 2)

        def d_fill(i, t, n):
            f = D_FILLS * (t - 3) + n
            return f % 2, i * D_FILLS + f // 2

        def unit_d(i, t):
            return (i - 2, 1) if t == 0 else (i - 1, 0)

        def filled(eng, full, fill):
            eng.wait_ge(full[fill[0]], fill[1] + 1)

        def weights(i_of_layer, col, n):
            if isinstance(i_of_layer, int):
                s = i_of_layer // B % 2
                return W[:, s, col:col + n]
            s = (i_of_layer // B) % 2
            return W[:, :, :].rearrange("p s c -> p (s c)")[:, bass.ds(s * W_PAD + col, n)]

        def tile_of(i, t):
            if isinstance(i, int):
                return xall[:, i % B * TPB + t, :]
            return xall[:, bass.ds((i % B) * TPB + t, 1), :].rearrange("p a d -> p (a d)")

        def weights_here(eng, i):
            eng.wait_ge(w_loaded, (min(i, ITERS) + 1 if isinstance(i, int) else i + 1) * 16)

        @block.sync
        def _(sp):
            for dst, src in [(base_tab[:, :, :, :, :], w["f_tab"]), (mask32[:, :, :], w["f_mask"])]:
                sp.dma_start(dst, src).then_inc(loaded, 16)
            sp.dma_start(W[:, 0, 0:7 * SHARE], w["f_W"][:, 0, 0:7, :].rearrange("p b c -> p (b c)")).then_inc(w_loaded, 16)
            sp.wait_ge(w_loaded, 16)
            sp.dma_start(W[:, 0, 7 * SHARE:], w["f_W"][:, 0, 7, :]).then_inc(w_loaded, 16)
            sp.wait_ge(setup, 1)

            def shift_in(i, t):
                a = i * 2 + t
                sp.wait_ge(x2_done, a + 1)
                sp.wait_ge(raw_ready, a * 4 + 1)
                src = tile_of(i, t)
                sp.dma_start(xsA[:, t, 0:64], src[:, 0:64]).then_inc(xsA_ready[t], 16)
                sp.dma_start(xsA[1:P, t, 64:D], src[0:P - 1, 64:D]).then_inc(xsA_ready[t], 16)
                if t == 1:
                    sp.dma_start(xsA[0:1, 1, 64:D], tile_of(i, 0)[P - 1:P, 64:D]).then_inc(xsA_ready[t], 16)

            def slot(i, t, stages):
                if "A" in stages:
                    shift_in(i + t, 1 - t)
                if "C" in stages:
                    sp.wait_ge(x1_ready, i * 2 + (t - 1))
                    sp.dma_start(xsC[:, t, 0:64], x1[:, t, 0:64]).then_inc(xsC_ready[t], 16)
                    sp.dma_start(xsC[1:P, t, 64:D], x1[0:P - 1, t, 64:D]).then_inc(xsC_ready[t], 16)
                    if t == 1:
                        sp.dma_start(xsC[0:1, 1, 64:D], x1[P - 1:P, 0, 64:D]).then_inc(xsC_ready[t], 16)
                if "A" in stages:
                    u = i * 2 + t
                    sp.wait_ge(V_ready, u * 2 + 2)
                    sp.wait_ge(O_free, u * 2 + 2)
                    sp.dma_start(V96[WIN:KEYS, t, 0, :], Vt[0:HQ, t, :]).then_inc(V96_ready[t], 16)
                    sp.dma_start(V96[:, t, 1, :], Vt[WIN:P, t, :]).then_inc(V96_ready[t], 16)
                    if t == 1:
                        sp.dma_start(V96[0:WIN, 1, 0, :], Vt[P - WIN:P, 0, :]).then_inc(V96_ready[t], 16)
                if "A" in stages and t == 1 and not is_first(i):
                    share = i - 1
                    nxt = share // B + 1
                    dst = W[:, :, :].rearrange("p s (b c) -> p (s b) c", b=B)[:, bass.ds((nxt % 2) * B + share % B, 1), :]
                    src = w["f_W"].rearrange("p l b c -> p (l b) c")[:, bass.ds((share + B) % (DEPTH * B), 1), :]
                    sp.wait_ge(x2_done, share * 2 + 16)
                    alone(sp, passed)
                    sp.wait_ge(w_loaded, (share + 2) * 16)
                    sp.dma_start(dst, src).then_inc(w_loaded, 16)

            shift_in(0, 0)
            slots(sp, slot)
            sp.wait_ge(w_loaded, (ITERS + 1) * 16)
            sp.wait_ge(xsA_ready[0], (ITERS + 1) * 32)
            sp.wait_ge(fin_done, 1)
            sp.dma_start(out, xall[:, :, :]).then_inc(stored, 16)
            sp.wait_ge(stored, 16)

        @block.gpsimd
        def _(pool):
            pool.wait_ge(setup, 1)
            pool.sem_inc(rot_done, 1)

            def normalise_probs(v, g):
                pool.wait_ge(rden_ready, v * 2 + g + 1)
                pool.tensor_tensor(Pr[:, g, :, :], Pr[:, g, :, :], rden[:, g, :].unsqueeze(2).broadcast_to([P, GH, KEYS]),
                                   ALU.mult).then_inc(Pr_ready, 1)

            def rotate(u, j):
                pool.wait_ge(m12_done, u * 2 + j + 3)
                mv = m12[:, j, :, :].rearrange("p m (h two d) -> p m h two d", two=2, d=DH // 2)
                pool.tensor_tensor(mv[:, 0], mv[:, 0], mv[:, 1, :, ::-1, :], ALU.add).then_inc(rot_done, 1)

            def scale(u, j):
                pool.wait_ge(rot_done, u * 2 + j + 2)
                pool.wait_ge(rn_ready, u + 1)
                pool.tensor_tensor(qkr[:, j * INNER:(j + 1) * INNER].rearrange("p (h d) -> p h d", d=DH),
                                   m12[:, j, 0, :].rearrange("p (h d) -> p h d", d=DH),
                                   rn[:, j * H:(j + 1) * H].unsqueeze(2).broadcast_to([P, H, DH]), ALU.mult).then_inc(qkr_ready, 1)

            def slot(i, t, stages):
                u, v, wu, du = i * 2 + t, i * 2 + (t - 1), i * 2 + (t - 2), i * 2 + (t - 3)
                if "A" in stages:
                    weights_here(pool, i)
                    pool.wait_ge(m12_done, u * 2 + 1)
                    alone(pool, passed)
                    sc = weights(i, W_SCALE, 2 * DH).rearrange("p (a d) -> p a d", a=2).unsqueeze(2).broadcast_to([P, 2, 2, DH])
                    pool.tensor_tensor(tab[:, t, :, :, :], base_tab[:, t, :, :, :], sc, ALU.mult).then_inc(tab_ready, 1)
                    rotate(u, 0)
                    rotate(u, 1)
                if "B" in stages:
                    normalise_probs(v, 0)
                if "D" in stages:
                    pool.wait_ge(x2_done, du + 16)
                    pool.wait_ge(ge_ready, du + 1)
                    pool.wait_ge(ga_ready, du * 2 + 2)
                    pool.tensor_tensor(hh[:, :], ga[:, 0, :], ge[:, :], ALU.mult).then_inc(hh_ready, 1)
                if "A" in stages:
                    if "B" in stages:
                        filled(pool, A_full, a_fill(i, t, 6))
                        filled(pool, A_full, a_fill(i, t, 7))
                    scale(u, 0)
                if "C" in stages:
                    pool.wait_ge(x1_ready, wu + 1)
                    pool.wait_ge(x2_done, wu + 15)
                    alone(pool, passed)
                    pool.tensor_tensor(x1b[:, t, :], x1[:, t, :], weights(i - 1, W_B2, D), ALU.add).then_inc(x1b_ready, 1)
                if "B" in stages:
                    normalise_probs(v, 1)
                if "A" in stages:
                    scale(u, 1)

            slots(pool, slot)

        @block.scalar
        def _(act):
            act.preload_act_table_set(LN_EXP)
            act.wait_ge(setup, 1)
            act.sem_inc(raw_ready, 8)
            act.sem_inc(P_free, 4)
            act.sem_inc(O_free, 4)
            for j in range(2):
                act.sem_inc(A_free[j], 3)
                act.sem_inc(D_free[j], 1)
            act.activation(x0[:, :, :], xall[:, :, :], ACT.Copy).then_inc(act_chain, 1)

            def evacuate_tokens(f, t):
                filled(act, A_full, f)
                act.activation(xT[:, t, :], psA[f[0]][:, 0:P], ACT.Copy).then_inc(A_free[f[0]], 1)

            def slot(i, t, stages):
                q = 1 - t
                u, v, wu, du = i * 2 + t, i * 2 + (t - 1), i * 2 + (t - 2), i * 2 + (t - 3)
                di, dt = unit_d(i, t)

                def evacuate_probs(g, j):
                    unit = (v, wu)[g]
                    act.wait_ge(P_full, unit * 4 + 2 * g + j + 1)
                    act.activation(PT[:, j, :, :], psP[0:KEYS, :, :], ACT.Copy).then_inc(P_free, 1)

                def evacuate_v(j):
                    f = a_fill(i, t, 8 + j)
                    filled(act, A_full, f)
                    if j == 0 and not is_first(i):
                        act.wait_ge(V96_ready[1], i * 48)
                        if t == 0:
                            act.wait_ge(V96_ready[0], i * 32)
                    act.activation(Vt[:, t, j * 512:(j + 1) * 512], psA[f[0]][:, :], ACT.Copy).then_inc(V_ready, 1)
                    act.wait_ge(V_ready, u * 2 + j + 1)
                    act.sem_inc(A_free[f[0]], 1)

                def evacuate_out(g):
                    act.wait_ge(O_full, (v, wu)[g] * 2 + g + 1)
                    act.activation(oT[:, (q, t)[g], 4 * g:4 * g + 4, :], psO[:, :, :], ACT.Copy).then_inc(O_free, 1)

                def exponentials(g):
                    act.wait_ge(S_free, v * 2 + g + 2)
                    act.activation(Pr[:, g, :, :], Pr[:, g, :, :], ACT.Exp).then_inc(exp_done, 1)

                def evacuate_raw(n):
                    if n == 0:
                        act.wait_ge(m12_done, u * 2 + 2)
                    f = a_fill(i, t, n)
                    filled(act, A_full, f)
                    act.activation(qkraw[:, n * 512:(n + 1) * 512], psA[f[0]][:, :], ACT.Copy).then_inc(raw_ready, 1)
                    act.wait_ge(raw_ready, u * 4 + n + 9)
                    act.sem_inc(A_free[f[0]], 1)

                def evacuate_qk(n):
                    f = a_fill(i, t, 4 + n)
                    filled(act, A_full, f)
                    c0 = (n // 2) * 4
                    src = psA[f[0]][:, :].rearrange("p (c q) -> p c q", c=4)
                    dst = kT[:, q, c0:c0 + 4, WIN:WIN + P] if n % 2 else qT[:, q, c0:c0 + 4, :]
                    act.activation(dst, src, ACT.Copy).then_inc(A_free[f[0]], 1)

                if "D" in stages:
                    f = d_fill(i, t, 0)
                    filled(act, D_full, f)
                    weights_here(act, i - 1)
                    alone(act, passed)
                    act.activation(xnT[:, :], psD[f[0]][:, 0:P], ACT.Identity, bias=weights(di, W_LN + 1, 1), scale=weights(di, W_LN, 1)).then_inc(D_free[f[0]], 1)
                if "A" in stages:
                    evacuate_raw(0)
                    evacuate_raw(1)
                if "C" in stages:
                    evacuate_probs(1, 0)
                if "A" in stages:
                    evacuate_raw(2)
                if "C" in stages:
                    evacuate_probs(1, 1)
                if "A" in stages:
                    evacuate_raw(3)
                if "C" in stages:
                    evacuate_out(1)
                if "B" in stages:
                    for n in range(4):
                        evacuate_qk(n)
                    if q == 1:
                        act.activation(kT[:, 1, :, 0:WIN], kT[:, 0, :, P:P + WIN], ACT.Copy).then_inc(kprev_ready, 1)
                if "A" in stages:
                    act.activation(sq[:, :], qkraw[:, :], ACT.Square).then_inc(sq_ready, 1)
                if "B" in stages:
                    exponentials(0)
                if "A" in stages:
                    evacuate_v(0)
                    act.wait_ge(ssq_ready, u + 1)
                    act.activation(lnq[:, :], ssq[:, :], ACT.Ln, bias=consts[:, 0:1], scale=SSQ_SCALE).then_inc(rn0_ready, 1)
                    act.wait_ge(rn0_ready, u * 2 + 1)
                    act.activation(rn0[:, :], lnq[:, :], ACT.Exp, bias=consts[:, 1:2], scale=-0.5).then_inc(rn0_ready, 1)
                if "D" in stages:
                    act.wait_ge(ga_ready, du * 2 + 1)
                    act.activation(ge[:, :], ga[:, 1, :], ACT.Gelu).then_inc(ge_ready, 1)
                    act.preload_act_table_set(LN_EXP)
                if "A" in stages:
                    evacuate_v(1)
                if "B" in stages:
                    evacuate_probs(0, 0)
                    exponentials(1)
                if "D" in stages:
                    f = d_fill(i, t, 3)
                    filled(act, D_full, f)
                    act.activation(hT[:, 0:2, :], psD[f[0]][:, 0:2 * P].rearrange("p (c q) -> p c q", c=2), ACT.Copy)
                    act.activation(hT[0:FF - 2 * P, 2, :], psD[f[0]][0:FF - 2 * P, 2 * P:3 * P], ACT.Copy).then_inc(D_free[f[0]], 1)
                if "B" in stages:
                    evacuate_probs(0, 1)
                if "A" in stages:
                    evacuate_tokens(a_fill(i, t, 10), 1 - t)
                if "C" in stages:
                    act.wait_ge(momC_ready, wu + 1)
                    act.activation(lnC[:, :], momC[:, 1:2], ACT.Ln, bias=eps_col).then_inc(act_chain, 1)
                    act.wait_ge(act_chain, wu + 2)
                    act.activation(rstdC[:, :], lnC[:, :], ACT.Exp, scale=-0.5).then_inc(rstdC_ready, 1)
                if "B" in stages:
                    evacuate_out(0)

            evacuate_tokens(A_FIRST, 0)
            slots(act, slot)
            act.wait_ge(fin_mom, 1)
            act.activation(fin_ln[:, :], fin_m[:, :, 1], ACT.Ln, bias=eps_col).then_inc(fin_chain, 1)
            act.wait_ge(fin_chain, 2)
            act.activation(fin_r[:, :], fin_ln[:, :], ACT.Exp, scale=-0.5).then_inc(fin_rstd, 1)

        @block.vector
        def _(dve):
            dve.memset(xsA[0:1, 0, 64:D], 0.0)
            dve.memset(xsC[0:1, 0, 64:D], 0.0)
            dve.memset(kT[:, 0, :, 0:WIN], 0.0)
            dve.memset(V96[0:WIN, 0, 0, :], 0.0)
            dve.memset(consts[:, 0:1], 2.0 ** -70)
            dve.memset(consts[:, 1:2], 0.5 * float(np.log(SSQ_SCALE)))
            dve.wait_ge(loaded, 32)
            dve.tensor_copy(identb[:, :], ident[:, :])
            dve.tensor_copy(maskb[:, :, :, :], mask32[:, :, :].unsqueeze(2).broadcast_to([P, TPB, GH // 2, KEYS])).then_inc(setup, 1)
            dve.sem_inc(m12_done, 2)
            dve.sem_inc(S_free, 1)
            dve.sem_inc(x2_done, 16)

            def less_maximum(v, g):
                dve.wait_ge(S_full, v * 2 + g + 1)
                dve.tensor_reduce(mx[:, g, :].rearrange("p (a c) -> p a c", a=2), S4, axis=AX.X, op=ALU.max).then_inc(mx_done, 1)
                dve.wait_ge(mx_done, v * 2 + g + 1)
                dve.wait_ge(P_free, v * 4 + 2 * g + 2)
                mb = mx[:, g, :].rearrange("p (a c) -> p a c", a=2).unsqueeze(3).broadcast_to([P, 2, GH // 2, KEYS])
                dve.tensor_tensor(Pr[:, g, :, :].rearrange("p (a c) k -> p a c k", a=2), S4, mb, ALU.subtract).then_inc(S_free, 1)

            def denominators(v, g):
                dve.wait_ge(exp_done, v * 2 + g + 1)
                dve.tensor_reduce(den[:, g, :], Pr[:, g, :, :], axis=AX.X, op=ALU.add).then_inc(den_done, 1)
                dve.wait_ge(den_done, v * 2 + g + 1)
                dve.reciprocal(rden[:, g, :], den[:, g, :]).then_inc(rden_ready, 1)

            def slot(i, t, stages):
                u, v, wu, du = i * 2 + t, i * 2 + (t - 1), i * 2 + (t - 2), i * 2 + (t - 3)
                di, dt = unit_d(i, t)

                def add_bias(n):
                    f = d_fill(i, t, 1 + (1 - n))
                    filled(dve, D_full, f)
                    dve.tensor_tensor(ga[:, n, :], psD[f[0]][:, 0:FF], weights(di, W_B1 + n * FF, FF), ALU.add).then_inc(ga_ready, 1)
                    dve.wait_ge(ga_ready, du * 2 + 2 - n)
                    dve.sem_inc(D_free[f[0]], 1)

                if "A" in stages:
                    dve.wait_ge(tab_ready, u + 1)
                    if "B" in stages:
                        dve.wait_ge(qkr_ready, u * 2)
                    for j in range(2):
                        dve.wait_ge(raw_ready, u * 4 + 2 * j + 10)
                        rv = qkraw[:, j * INNER:(j + 1) * INNER].rearrange("p (h d) -> p h d", d=DH)
                        dve.tensor_tensor(m12[:, j, :, :].rearrange("p m (h d) -> p m h d", d=DH),
                                          rv.unsqueeze(1).broadcast_to([P, 2, H, DH]),
                                          tab[:, t, j, :, :].unsqueeze(2).broadcast_to([P, 2, H, DH]), ALU.mult).then_inc(m12_done, 1)
                if "D" in stages:
                    weights_here(dve, i)
                    add_bias(1)
                if "B" in stages:
                    less_maximum(v, 0)
                if "A" in stages:
                    dve.wait_ge(sq_ready, u + 1)
                    dve.tensor_reduce(ssq[:, :], sq[:, :].rearrange("p (h d) -> p h d", d=DH), axis=AX.X, op=ALU.add).then_inc(ssq_ready, 1)
                if "B" in stages:
                    denominators(v, 0)
                if "A" in stages:
                    dve.wait_ge(rn0_ready, u * 2 + 2)
                    dve.tensor_scalar(rn[:, 0:H], rn0[:, 0:H], 1e12, 8.0, ALU.min, ALU.mult)
                    dve.tensor_scalar(rn[:, H:2 * H], rn0[:, H:2 * H], 1e12, None, ALU.min).then_inc(rn_ready, 1)
                if "D" in stages:
                    add_bias(0)
                if "C" in stages:
                    dve.wait_ge(wo_full, wu + 1)
                    dve.tensor_tensor(x1[:, t, :], psO[:, 0, :], tile_of(i - 1, t), ALU.add).then_inc(x1_ready, 1)
                if "B" in stages:
                    less_maximum(v, 1)
                if "C" in stages:
                    dve.wait_ge(xsC_ready[t], i * (32, 48)[t])
                    dve.bn_stats(out=statC[:, :], in_=xsC[:, t, :]).then_inc(dve_chain, 1)
                    dve.wait_ge(dve_chain, wu + 1)
                    alone(dve, passed)
                    dve.bn_aggr(out=momC[:, :], in_=statC[:, :]).then_inc(momC_ready, 1)
                if "B" in stages:
                    denominators(v, 1)
                if "C" in stages:
                    dve.wait_ge(rstdC_ready, wu + 1)
                    dve.tensor_scalar(hatC[:, t, :], xsC[:, t, :], momC[:, 0:1], rstdC[:, :], ALU.subtract, ALU.mult).then_inc(hatC_ready, 1)
                if "D" in stages:
                    f = d_fill(i, t, 4)
                    filled(dve, D_full, f)
                    dve.wait_ge(x1b_ready, du + 1)
                    dve.tensor_tensor(tile_of(di, dt), psD[f[0]][:, 0:D], x1b[:, dt, :], ALU.add).then_inc(x2_done, 1)
                    dve.wait_ge(x2_done, du + 17)
                    dve.sem_inc(D_free[f[0]], 1)

            slots(dve, slot)
            dve.wait_ge(act_chain, 1)
            dve.tensor_tensor(x0[:, :, :], x0[:, :, :], xall[:, :, :], ALU.add).then_inc(fin_chain, 1)
            dve.wait_ge(fin_chain, 1)
            for j in range(TILES):
                ins = dve.bn_stats(out=fin_s[:, j, :], in_=x0[:, j, :])
            ins.then_inc(dve_chain, 1)
            dve.wait_ge(dve_chain, ITERS * 2 + 1)
            for j in range(TILES):
                ins = dve.bn_aggr(out=fin_m[:, j, :], in_=fin_s[:, j, :])
            ins.then_inc(fin_mom, 1)
            dve.wait_ge(fin_rstd, 1)
            for j in range(TILES):
                ins = dve.tensor_scalar(xall[:, j, :], x0[:, j, :], fin_m[:, j, 0:1], fin_r[:, j:j + 1], ALU.subtract, ALU.mult)
            ins.then_inc(fin_done, 1)

        @block.tensor
        def _(pe):
            pe.wait_ge(setup, 1)
            for j in range(2):
                pe.sem_inc(A_full[j], 2)

            def fill(ring, free, f):
                pe.wait_ge(free[f[0]], f[1] + 1)
                return ring[f[0]]

            def read_back(free, f):
                pe.wait_ge(free[f[0]], f[1] + 2)

            def transpose_tokens(f, i, t):
                pe.wait_ge(xsA_ready[t], (i + 1) * (32, 48)[t])
                p = fill(psA, A_free, f)
                pe.transpose(p[:, 0:P], xsA[:, t, :], ident[:, :]).then_inc(A_full[f[0]], 1)

            def slot(i, t, stages):
                q = 1 - t
                u, v, wu, du = i * 2 + t, i * 2 + (t - 1), i * 2 + (t - 2), i * 2 + (t - 3)
                di, dt = unit_d(i, t)

                def scores(g):
                    pe.wait_ge(S_free, v * 2 + g + 1)
                    for par in range(2):
                        pe.matmul(psS[:, par, 0:GH // 2 * KEYS], identb[:, :], maskb[:, q, :, :].rearrange("p c k -> p (c k)"), start=True, stop=False, skip_group_check=True)
                    for par in range(2):
                        r = slice(par * DH, par * DH + DH)
                        for c in range(4):
                            for half in range(2):
                                k0 = half * HQ
                                ins = pe.matmul(S4[half * HQ:(half + 1) * HQ, par, c, :], qT[r, q, 4 * g + c, k0:k0 + HQ],
                                                kT[r, q, 4 * g + c, k0:k0 + KEYS], start=False, stop=True, skip_group_check=True)
                    ins.then_inc(S_full, 1)

                def transpose_probs(g, j):
                    unit = (v, wu)[g]
                    pe.wait_ge(Pr_ready, unit * 2 + g + 1)
                    pe.wait_ge(P_free, unit * 4 + 2 * g + j + 4)
                    for n in range(4):
                        h = 4 * j + n
                        ins = pe.transpose(psP[0:KEYS, n, :], Pr[:, g, (h % 2) * 4 + h // 2, :], ident[:, :])
                    ins.then_inc(P_full, 1)

                def times_v(g, j):
                    unit, tile = ((v, q), (wu, t))[g]
                    pe.wait_ge(P_free, unit * 4 + 2 * g + j + 5)
                    if j == 0:
                        pe.wait_ge(O_free, unit * 2 + g + 4)
                        if g == 0 and "C" in stages:
                            pe.wait_ge(x1_ready, wu + 1)
                    if g == 0 and j == 0:
                        n_dma = (32, 48)[q]
                        pe.wait_ge(V96_ready[q], (i + (1 if q == 0 else 0)) * n_dma)
                    for n in range(4):
                        h = 4 * j + n
                        hh_ = 8 * g + h
                        for half in range(2):
                            ins = pe.matmul(psO[(h % 2) * DH:(h % 2) * DH + DH, h // 2, half * HQ:(half + 1) * HQ],
                                            V96[:, tile, half, hh_ * DH:(hh_ + 1) * DH], PT[:, j, n, half * HQ:(half + 1) * HQ], start=True, stop=True)
                    if j == 1:
                        ins.then_inc(O_full, 1)

                def transpose_qk(n):
                    f = a_fill(i, t, 4 + n)
                    p = fill(psA, A_free, f)
                    for c in range(4):
                        col = (n % 2) * INNER + ((n // 2) * 4 + c) * P
                        ins = pe.transpose(p[:, c * P:(c + 1) * P], qkr[:, col:col + P], ident[:, :])
                    ins.then_inc(A_full[f[0]], 1)

                def project(n):
                    f = a_fill(i, t, (0, 1, 2, 3, 8, 9)[n])
                    p = fill(psA, A_free, f)
                    pe.matmul(p[:, :], xT[:, t, :], weights(i, W_QKV + n * 512, 512), start=True, stop=True).then_inc(A_full[f[0]], 1)

                if "D" in stages:
                    pe.wait_ge(hatC_ready, du + 1)
                    fd = d_fill(i, t, 0)
                    p = fill(psD, D_free, fd)
                    pe.transpose(p[:, 0:P], hatC[:, dt, :], ident[:, :]).then_inc(D_full[fd[0]], 1)
                if "A" in stages:
                    read_back(A_free, A_FIRST if is_first(i) and t == 0 else a_fill(i - (1 - t), 1 - t, 10))
                    weights_here(pe, i)
                    project(0)
                    project(1)
                if "C" in stages:
                    transpose_probs(1, 0)
                if "A" in stages:
                    project(2)
                if "C" in stages:
                    transpose_probs(1, 1)
                if "A" in stages:
                    project(3)
                if "C" in stages:
                    times_v(1, 0)
                    times_v(1, 1)
                if "B" in stages:
                    pe.wait_ge(qkr_ready, v * 2 + 2)
                    for n in range(4):
                        transpose_qk(n)
                if "D" in stages:
                    read_back(D_free, fd)
                    for n in (1, 0):
                        f = d_fill(i, t, 1 + (1 - n))
                        p = fill(psD, D_free, f)
                        pe.matmul(p[:, 0:FF], xnT[:, :], weights(di, W_1 + n * FF, FF), start=True, stop=True).then_inc(D_full[f[0]], 1)
                if "B" in stages:
                    read_back(A_free, a_fill(i, t, 6))
                    read_back(A_free, a_fill(i, t, 7))
                    if q == 1:
                        pe.wait_ge(kprev_ready, i)
                    scores(0)
                if "A" in stages:
                    project(4)
                if "C" in stages:
                    pe.wait_ge(O_free, wu * 2 + 6)
                    for c in range(CH):
                        ins = pe.matmul(psO[:, 0, :], oT[:, t, c, :], weights(i - 1, W_O + c * D, D), start=(c == 0), stop=(c == CH - 1))
                    ins.then_inc(wo_full, 1)
                if "B" in stages:
                    scores(1)
                if "A" in stages:
                    project(5)
                if "B" in stages:
                    transpose_probs(0, 0)
                if "D" in stages:
                    pe.wait_ge(hh_ready, du + 1)
                    fd = d_fill(i, t, 3)
                    p = fill(psD, D_free, fd)
                    for c in range(3):
                        n = min(P, FF - c * P)
                        ins = pe.transpose(p[0:n, c * P:(c + 1) * P], hh[:, c * P:c * P + n], ident[:, :])
                    ins.then_inc(D_full[fd[0]], 1)
                if "B" in stages:
                    transpose_probs(0, 1)
                if "A" in stages:
                    transpose_tokens(a_fill(i, t, 10), i + t, 1 - t)
                if "B" in stages:
                    times_v(0, 0)
                    times_v(0, 1)
                if "D" in stages:
                    weights_here(pe, i)
                    read_back(D_free, fd)
                    f = d_fill(i, t, 4)
                    p = fill(psD, D_free, f)
                    for c in range(3):
                        n = min(P, FF - c * P)
                        ins = pe.matmul(p[:, 0:D], hT[0:n, c, :], weights(di, W_2 + c * D, D)[0:n, :], start=(c == 0), stop=(c == 2))
                    ins.then_inc(D_full[f[0]], 1)

            transpose_tokens(A_FIRST, 0, 0)
            slots(pe, slot)


def host_layout(x):
    f = np.float32
    up = lambda a: np.ascontiguousarray(a, dtype=f)
    w = {}
    w["x"] = up(x["x"].reshape(TILES, P, D).transpose(1, 0, 2))
    w["ident"] = np.eye(P, dtype=f)
    G = P // NST
    W = x["L0_attn_W_ll"]
    kc = lambda a: up(a.T.reshape(2, P, -1).transpose(1, 0, 2))
    w["m_up1"] = up(x["L0_attn_W_up1"].T)
    w["m_up2"] = up(x["L0_attn_W_up2"].T)
    w["m_down"] = kc(x["L0_attn_W_down"])
    w["m_wdel"] = kc(W[:DI])
    w["m_wB"] = kc(np.tile(W[DI:DI + NST], (G, 1)))
    w["m_wC"] = kc(np.tile(W[DI + NST:], (G, 1)))
    b = x["L0_attn_b_ll"]
    w["m_cols"] = up(np.concatenate([
        x["L0_attn_ln_g"][:, None], x["L0_attn_ln_b"][:, None], x["L0_attn_conv_b"].reshape(2, P).T,
        b[:DI].reshape(2, P).T, np.tile(b[DI:DI + NST], G)[:, None], np.tile(b[DI + NST:], G)[:, None],
        x["L0_attn_conv_w"].reshape(2, P, 4).transpose(1, 0, 2).reshape(P, 8)], axis=1))
    w["m_alog"] = up(x["L0_attn_A_log"].reshape(DI // G, P).T)
    w["m_bdown"] = up(np.broadcast_to(x["L0_attn_b_down"], (P, D)))
    col = np.arange(NST * P)
    w["m_sel"] = up(col[None, :] // NST == np.arange(P)[:, None])
    w["m_pick"] = up(np.arange(P)[None, None, :] == (np.arange(P)[:, None, None] // NST + G * np.arange(P // G)[None, :, None]))
    w["ctx"] = up(x["ctx_1024"].reshape(TILES, P, D).transpose(1, 0, 2))
    w["x_cols"] = up(np.stack([x["L0_xattn_ln_l_w"], x["L0_xattn_ln_l_b"], x["L0_xattn_ln_c_w"], x["L0_xattn_ln_c_b"]], axis=1))
    w["x_wq"] = up(x["L0_xattn_Wq"])
    w["x_wk"] = up(x["L0_xattn_Wkv"][:, :INNER])
    w["x_wv"] = up(x["L0_xattn_Wkv"][:, INNER:])
    w["x_wo"] = up(x["L0_xattn_Wo"].reshape(INNER // P, P, D).transpose(1, 0, 2))
    w["x_bo"] = up(np.broadcast_to(x["L0_xattn_bo"], (P, D)))
    pack = np.zeros((P, DEPTH, W_PAD), f)
    rows = lambda a: np.broadcast_to(a, (P,) + a.shape)
    for l in range(DEPTH):
        put = lambda col, a: pack[:a.shape[0], l, col:col + a.shape[1]].__setitem__(slice(None), a)
        put(W_QKV, x["L0_ffn_Wqkv"][l])
        put(W_SCALE, rows(x["L0_ffn_q_scale"][l]))
        put(W_SCALE + DH, rows(x["L0_ffn_k_scale"][l]))
        put(W_LN, x["L0_ffn_ln_g"][l][:, None])
        put(W_LN + 1, x["L0_ffn_ln_b"][l][:, None])
        put(W_O, x["L0_ffn_Wo"][l].reshape(INNER // P, P, D).transpose(1, 0, 2).reshape(P, -1))
        put(W_1, x["L0_ffn_W1"][l])
        put(W_B1, rows(x["L0_ffn_b1"][l]))
        for c in range(3):
            put(W_2 + c * D, x["L0_ffn_W2"][l][c * P:(c + 1) * P])
        put(W_B2, rows(x["L0_ffn_b2"][l]))
    w["f_W"] = pack.reshape(P, DEPTH, B, SHARE)
    half = np.arange(0, DH, 2, dtype=f)
    inv_freq = f(1.0) / f(10000.0) ** (half / f(DH))
    t = np.arange(L, dtype=f)
    freqs = t[:, None] * inv_freq[None, :]
    base = (half + f(0.4 * DH)) / f(1.4 * DH)
    scale = base[None, :] ** ((t - L // 2) / f(WIN // 2))[:, None]
    two = lambda a: np.concatenate([a, a], -1)
    cos, sin, scale = two(np.cos(freqs)), np.concatenate([np.sin(freqs), -np.sin(freqs)], -1), two(scale)
    tab = np.stack([np.stack([cos * s, sin * s]) for s in (scale, f(1.0) / scale)])
    w["f_tab"] = up(tab.reshape(2, 2, TPB, P, DH).transpose(3, 2, 0, 1, 4))
    it = np.arange(L)
    key = (it // (P // 2) * (P // 2) - WIN)[:, None] + np.arange(3 * WIN)[None, :]
    seen = (key <= it[:, None]) & (key >= it[:, None] - WIN) & (key >= 0)
    w["f_mask"] = up(np.where(seen, 0.0, -1e30).reshape(TPB, P, 3 * WIN).transpose(1, 0, 2))
    return w


def decoder_layer(nc, w, out):
    with ExitStack() as ctx:
        xall = ctx.enter_context(nc.sbuf_tensor("xall", [P, TILES, D], F32))
        ident = ctx.enter_context(nc.sbuf_tensor("ident", [P, P], F32))
        eps = ctx.enter_context(nc.sbuf_tensor("eps", [P, 1], F32))
        eps_ready = ctx.enter_context(nc.semaphore("eps_ready"))
        with nc.Block() as block:
            @block.vector
            def _(dve):
                dve.memset(eps[:, :], EPS).then_inc(eps_ready, 1)

            @block.scalar
            def _(act):
                act.wait_ge(eps_ready, 1)

        state_space_block(nc, xall, ident, eps[:, :], w)
        cross_attention_block(nc, xall, ident, eps[:, :], w)
        window_layers(nc, xall, ident, eps[:, :], w, out)


def kernel(**inputs):
    import concourse.bacc as bacc
    from concourse.bass_utils import run_bass_kernel_spmd

    nc = bacc.Bacc("TRN2", target_bir_lowering=False, num_devices=1)
    arrays = host_layout({k: np.asarray(v) for k, v in inputs.items()})
    aps = {k: nc.dram_tensor(f"in_{k}", a.shape, mybir.dt.from_np(a.dtype), kind="ExternalInput").ap() for k, a in arrays.items()}
    out = nc.dram_tensor("out_x", (P, TILES, D), F32, kind="ExternalOutput").ap()
    decoder_layer(nc, aps, out)
    r = run_bass_kernel_spmd(nc, [{f"in_{k}": a for k, a in arrays.items()}], core_ids=[0])
    return np.asarray(r.results[0]["out_x"]).transpose(1, 0, 2).reshape(B, L, D)
```

```python
from contextlib import ExitStack

import numpy as np

import concourse.bass as bass
from concourse import mybir

F32 = mybir.dt.float32
F32R = mybir.dt.float32r
BF16 = mybir.dt.bfloat16
ALU = mybir.AluOpType
ACT = mybir.ActivationFunctionType
AX = mybir.AxisListType

P = 128
B, L, D = 8, 256, 128
TILES = B * L // P
TPB = L // P
EPS = 1e-5
NST = 16
DI = 256
H, DH = 16, 64
INNER = H * DH
DEPTH = 6
WIN = 32
FF = 341
SSQ_SCALE = 2.0 ** 24


def alone(eng, passed):
    eng.sem_inc(passed, 1)


def layer_norm_stats(dve, passed, act_ready, chain, rows, stats, moments):
    for j, row in enumerate(rows):
        ins = dve.bn_stats(out=stats[:, j, :], in_=row)
    chain(ins)
    alone(dve, passed)
    for j in range(len(rows)):
        ins = dve.bn_aggr(out=moments[:, j, :], in_=stats[:, j, :])
    ins.then_inc(act_ready, 1)


LN_EXP = "natural_log_exp_and_others"


class Chain:

    def __init__(self, eng, sem, base, per_iter):
        self.eng, self.sem, self.base, self.per_iter, self.n = eng, sem, base, per_iter, 0

    def __call__(self, ins):
        self.n += 1
        ins.then_inc(self.sem, 1)
        self.eng.wait_ge(self.sem, self.base + self.n)

    def close(self):
        assert self.n == self.per_iter, self.n


def state_space_block(nc, xall, ident, eps_col, w, prefetch):
    NB = 2
    T = NB * L
    NT = NB * TPB
    STEPS = B // NB
    NC = DI // P
    G = P // NST
    UPC = P // G
    UNITS = NC * UPC
    LAG = 3
    DVE_CHAIN = 23

    with ExitStack() as ctx:
        def sb(name, shape, dt=F32):
            return ctx.enter_context(nc.sbuf_tensor(name, shape, dt))

        def sem(name):
            return ctx.enter_context(nc.semaphore(name))

        up1 = sb("m_up1", [P, DI])
        up2 = sb("m_up2", [P, DI])
        down = sb("m_down", [P, NC, D])
        wdel = sb("m_wdel", [P, NC, DI])
        wB = sb("m_wB", [P, NC, P])
        wC = sb("m_wC", [P, NC, P])
        cols = sb("m_cols", [P, 2 + 3 * NC + NC * 4])
        ln_g, ln_b = cols[:, 0:1], cols[:, 1:2]
        conv_b = cols[:, 2:2 + NC]
        b_del = cols[:, 2 + NC:2 + 2 * NC]
        b_BC = cols[:, 2 + 2 * NC:2 + 3 * NC]
        conv_w = cols[:, 2 + 3 * NC:2 + 7 * NC].rearrange("p (c k) -> p c k", c=NC)
        alog = sb("m_alog", [P, UNITS])
        bdown = sb("m_bdown", [P, D])
        sel = sb("m_sel", [P, UPC * P], F32R)
        pick = sb("m_pick", [P, UPC, P])
        summ = sb("m_summ", [P, UNITS, P])
        eA = sb("m_eA", [P, UNITS])
        negA = sb("m_negA", [P, UNITS])
        invA = sb("m_invA", [P, UNITS])
        stats = sb("m_stats", [P, NT, 6])
        mom = sb("m_mom", [P, NT, 2])
        lnv = sb("m_lnv", [P, NT])
        rstd = sb("m_rstd", [P, NT])
        xhat = sb("m_xhat", [P, NT, D])
        xnT = sb("m_xnT", [P, T])
        xpad = sb("m_xpad", [P, NC, NB, 3 + L])
        cv = sb("m_cv", [P, NC, NB, L])
        xc = sb("m_xc", [P, NC, T])
        xch = sb("m_xch", [P, NC, T], F32R)
        xcl = sb("m_xcl", [P, NC, T], F32R)
        gate = sb("m_gate", [P, NC, T])
        pre = sb("m_pre", [P, NC, T])
        ea = sb("m_ea", [P, NC, T])
        u1 = sb("m_u1", [P, NC, T])
        lu = sb("m_lu", [P, NC, T])
        dl = lu
        dlh = sb("m_dlh", [P, NC, T], F32R)
        dll = sb("m_dll", [P, NC, T], F32R)
        Bt = sb("m_Bt", [P, T])
        Ct = sb("m_Ct", [P, T])
        Ab = sb("m_Ab", [P, 2, T])
        XBU = sb("m_XBU", [P, 4, T])
        XB, U = XBU[:, 0:2, :], XBU[:, 2:4, :]
        sel32 = XBU[:, :, :].rearrange("p a t -> p (a t)")
        assert UPC * P == 4 * T
        Hs = sb("m_Hs", [P, 2, T])
        HC = sb("m_HC", [P, LAG, T])
        Yg = sb("m_Yg", [P, NC, T])
        res = sb("m_res", [P, NT, D])
        psD = [ctx.enter_context(nc.psum_tensor(f"m_psD{j}", [P, T], F32)) for j in range(2)]
        psX = [ctx.enter_context(nc.psum_tensor(f"m_psX{j}", [P, T], F32)) for j in range(2)]
        psY = [ctx.enter_context(nc.psum_tensor(f"m_psY{j}", [P, T], F32)) for j in range(NC)]
        psM = [ctx.enter_context(nc.psum_tensor(f"m_psM{j}", [P, T], F32)) for j in range(2)]

        passed = sem("m_passed")
        first_loaded = sem("m_first_loaded")
        loaded = sem("m_loaded")
        sel_ready = sem("m_sel_ready")
        eA_ready = sem("m_eA_ready")
        dve_chain = sem("m_dve_chain")
        act_chain = sem("m_act_chain")
        mom_ready = sem("m_mom_ready")
        rstd_ready = sem("m_rstd_ready")
        xhat_ready = sem("m_xhat_ready")
        misc_full = sem("m_misc_full")
        xnT_ready = sem("m_xnT_ready")
        xpad_ready = sem("m_xpad_ready")
        cv_ready = sem("m_cv_ready")
        xc_ready = sem("m_xc_ready")
        pre_ready = sem("m_pre_ready")
        u1_ready = sem("m_u1_ready")
        ea_ready = sem("m_ea_ready")
        lu_ready = sem("m_lu_ready")
        split_ready = sem("m_split_ready")
        BC_ready = sem("m_BC_ready")
        bcast_full = sem("m_bcast_full")
        Ab_ready = sem("m_Ab_ready")
        XB_done = sem("m_XB_done")
        U_done = sem("m_U_done")
        H_ready = sem("m_H_ready")
        HC_ready = sem("m_HC_ready")
        sum_done = sem("m_sum_done")
        Yg_ready = sem("m_Yg_ready")
        down_read = sem("m_down_read")
        head_chain = sem("m_head_chain")
        MISC = 1 + NC + NC + 2 + NC + 1

        block = ctx.enter_context(nc.Block())

        @block.sync
        def _(sp):
            for dst, src in [(xall[:, :, :], w["x"]), (ident[:, :], w["ident"]), (cols[:, :], w["m_cols"])]:
                sp.dma_start(dst, src).then_inc(first_loaded, 16)
            for dst, src in [(up1[:, :], w["m_up1"]),
                             (wdel[:, :, :], w["m_wdel"]), (wB[:, :, :], w["m_wB"]), (wC[:, :, :], w["m_wC"]),
                             (alog[:, :], w["m_alog"]), (sel32[:, :], w["m_sel"]), (pick[:, :, :], w["m_pick"]),
                             (up2[:, :], w["m_up2"]), (down[:, :, :], w["m_down"]),
                             (bdown[:, :], w["m_bdown"])]:
                sp.dma_start(dst, src).then_inc(loaded, 16)
            prefetch(sp)
        LOADS = 16 * 10

        @block.gpsimd
        def _(pool):
            with pool.Fori(0, STEPS) as i:
                for k in range(UNITS):
                    pool.wait_ge(H_ready, i * UNITS + k + 3)
                    pool.wait_ge(sum_done, i * UNITS + k + 1)
                    pool.tensor_tensor(HC[:, k % LAG, :], Hs[:, k % 2, :], Ct[:, :], ALU.mult).then_inc(HC_ready, 1)

        @block.scalar
        def _(act):
            act.preload_act_table_set(LN_EXP)

            def rsqrt_of_variance(i, n):
                act.wait_ge(mom_ready, i * 2 + n)
                act.activation(lnv[:, :], mom[:, :, 1], ACT.Ln, bias=eps_col).then_inc(act_chain, 1)
                act.wait_ge(act_chain, i * 2 + n)
                act.activation(rstd[:, :], lnv[:, :], ACT.Exp, scale=-0.5).then_inc(rstd_ready, 1)

            def scale_transposed(i):
                act.wait_ge(misc_full, i * MISC + 1)
                act.activation(xnT[:, :], psM[0][:, :], ACT.Identity, bias=ln_b, scale=ln_g).then_inc(xnT_ready, 1)

            act.wait_ge(first_loaded, 16 * 3)
            rsqrt_of_variance(0, 1)
            scale_transposed(0)
            act.wait_ge(loaded, LOADS)
            act.activation(eA[:, :], alog[:, :], ACT.Exp).then_inc(eA_ready, 1)
            act.wait_ge(sel_ready, 2)
            with act.Fori(0, STEPS) as i:
                for c in range(NC):
                    act.wait_ge(misc_full, i * MISC + 2 + c)
                    for b in range(NB):
                        ins = act.activation(xpad[:, c, b, 3:3 + L], psM[(1 + c) % 2][:, b * L:(b + 1) * L], ACT.Copy)
                    ins.then_inc(xpad_ready, 1)
                for c in range(NC):
                    act.wait_ge(misc_full, i * MISC + 4 + c)
                    act.activation(gate[:, c, :], psM[(3 + c) % 2][:, :], ACT.Silu).then_inc(xnT_ready, 1)
                for c in range(NC):
                    act.wait_ge(cv_ready, i * NC + c + 1)
                    act.activation(xc[:, c, :], cv[:, c, :, :].rearrange("p b t -> p (b t)"), ACT.Silu).then_inc(xc_ready, 1)
                act.preload_act_table_set(LN_EXP)
                for c in range(NC):
                    act.wait_ge(misc_full, i * MISC + 6 + c)
                    act.activation(pre[:, c, :], psM[(5 + c) % 2][:, :], ACT.Identity, bias=b_del[:, c:c + 1]).then_inc(pre_ready, 1)
                    act.wait_ge(pre_ready, i * 2 * NC + 2 * c + 1)
                    act.activation(ea[:, c, :], pre[:, c, :], ACT.Abs).then_inc(pre_ready, 1)
                    act.wait_ge(pre_ready, i * 2 * NC + 2 * c + 2)
                    act.activation(ea[:, c, :], ea[:, c, :], ACT.Exp, scale=-1.0).then_inc(ea_ready, 1)
                for c in range(NC):
                    act.wait_ge(u1_ready, i * NC + c + 1)
                    act.activation(lu[:, c, :], u1[:, c, :], ACT.Ln).then_inc(lu_ready, 1)
                for j, dst in enumerate((Bt, Ct)):
                    act.wait_ge(misc_full, i * MISC + 8 + j)
                    act.activation(dst[:, :], psM[(7 + j) % 2][:, :], ACT.Identity, bias=b_BC[:, j:j + 1]).then_inc(BC_ready, 1)
                for k in range(UNITS):
                    act.wait_ge(bcast_full, i * UNITS + k + 1)
                    act.wait_ge(H_ready, i * UNITS + k + 1)
                    act.activation(Ab[:, k % 2, :], psD[k % 2][:, :], ACT.Exp, scale=negA[:, k:k + 1]).then_inc(Ab_ready, 1)
                rsqrt_of_variance(i, 2)
                scale_transposed(i + 1)
                rsqrt_of_variance(i, 3)

        @block.vector
        def _(dve):
            dve.wait_ge(first_loaded, 16 * 3)
            dve.sem_inc(down_read, 1)

            def normalise(i, n, rows, outs, chain):
                layer_norm_stats(dve, passed, mom_ready, chain, rows, stats, mom)
                dve.wait_ge(rstd_ready, i * 2 + n)
                for j in range(NT):
                    ins = dve.tensor_scalar(outs[j], rows[j], mom[:, j, 0:1], rstd[:, j:j + 1], ALU.subtract, ALU.mult)
                return ins

            def step_rows(b):
                return [xall[:, bass.ds(b * NT + j, 1), :].rearrange("p a d -> p (a d)") for j in range(NT)]

            hats = [xhat[:, j, :] for j in range(NT)]
            normalise(0, 1, step_rows(0), hats, Chain(dve, head_chain, 0, 1)).then_inc(xhat_ready, 1)
            dve.wait_ge(loaded, LOADS)
            dve.tensor_copy(sel[:, :], sel32[:, :]).then_inc(sel_ready, 1)
            dve.memset(xpad[:, :, :, 0:3], 0.0)
            dve.sem_inc(H_ready, 2)
            dve.wait_ge(eA_ready, 1)
            dve.tensor_scalar(negA[:, :], eA[:, :], -1.0, None, ALU.mult).then_inc(sel_ready, 1)
            dve.wait_ge(sel_ready, 2)
            dve.reciprocal(invA[:, :], negA[:, :]).then_inc(sel_ready, 1)
            dve.wait_ge(sel_ready, 3)
            for k in range(UNITS):
                ins = dve.tensor_scalar(summ[:, k, :], pick[:, k % UPC, :], invA[:, k:k + 1], None, ALU.mult)
            ins.then_inc(sel_ready, 1)
            with dve.Fori(0, STEPS) as i:
                chain = Chain(dve, dve_chain, i * DVE_CHAIN, DVE_CHAIN)
                for c in range(NC):
                    dve.wait_ge(xpad_ready, i * NC + c + 1)
                    chain(dve.tensor_scalar(cv[:, c, :, :], xpad[:, c, :, 0:L], conv_w[:, c, 0:1], conv_b[:, c:c + 1], ALU.mult, ALU.add))
                    for k in range(1, 4):
                        ins = dve.scalar_tensor_tensor(out=cv[:, c, :, :], in0=xpad[:, c, :, k:k + L], scalar=conv_w[:, c, k:k + 1],
                                                       in1=cv[:, c, :, :], op0=ALU.mult, op1=ALU.add)
                        if k < 3:
                            chain(ins)
                    ins.then_inc(cv_ready, 1)
                for c in range(NC):
                    dve.wait_ge(xc_ready, i * NC + c + 1)
                    chain(dve.tensor_copy(xch[:, c, :], xc[:, c, :]))
                    dve.tensor_tensor(xcl[:, c, :], xc[:, c, :], xch[:, c, :].bitcast(F32), ALU.subtract).then_inc(split_ready, 1)
                for c in range(NC):
                    dve.wait_ge(ea_ready, i * NC + c + 1)
                    chain(dve.tensor_scalar(u1[:, c, :], ea[:, c, :], 1.0, None, ALU.add))
                    dve.sem_inc(u1_ready, 1)
                    dve.scalar_tensor_tensor(out=ea[:, c, :], in0=u1[:, c, :], scalar=-1.0, in1=ea[:, c, :], op0=ALU.add, op1=ALU.subtract)
                    chain(dve.tensor_scalar(pre[:, c, :], pre[:, c, :], 0.0, None, ALU.max))
                for c in range(NC):
                    dve.wait_ge(lu_ready, i * NC + c + 1)
                    chain(dve.tensor_tensor(dl[:, c, :], lu[:, c, :], ea[:, c, :], ALU.subtract))
                    chain(dve.tensor_tensor(dl[:, c, :], dl[:, c, :], pre[:, c, :], ALU.add))
                    chain(dve.tensor_copy(dlh[:, c, :], dl[:, c, :]))
                    dve.tensor_tensor(dll[:, c, :], dl[:, c, :], dlh[:, c, :].bitcast(F32), ALU.subtract).then_inc(split_ready, 1)
                dve.wait_ge(BC_ready, i * 2 + 1)
                def x_times_b(k):
                    s = k % 2
                    dve.wait_ge(bcast_full, i * UNITS + k + 1)
                    dve.tensor_tensor(XB[:, s, :], psX[s][:, :], Bt[:, :], ALU.mult).then_inc(XB_done, 1)

                x_times_b(0)
                for k in range(UNITS):
                    s = k % 2
                    dve.wait_ge(XB_done, i * UNITS + k + 1)
                    dve.wait_ge(Ab_ready, i * UNITS + k + 1)
                    dve.scalar_tensor_tensor(out=U[:, s, :], in0=Ab[:, s, :], scalar=1.0, in1=XB[:, s, :],
                                             op0=ALU.subtract, op1=ALU.mult).then_inc(U_done, 1)
                    if k + 1 < UNITS:
                        x_times_b(k + 1)
                    dve.wait_ge(U_done, i * UNITS + k + 1)
                    dve.wait_ge(HC_ready, i * UNITS + k + 1)
                    for b in range(NB):
                        ins = dve.tensor_tensor_scan(Hs[:, s, b * L:(b + 1) * L], Ab[:, s, b * L:(b + 1) * L],
                                                     U[:, s, b * L:(b + 1) * L], 0.0, ALU.mult, ALU.add)
                    ins.then_inc(H_ready, 1)
                normalise(i, 2, step_rows((i + 1) % STEPS), hats, chain).then_inc(xhat_ready, 1)
                dve.wait_ge(sum_done, i * UNITS + UNITS + LAG)
                for c in range(NC):
                    ins = dve.tensor_tensor(Yg[:, c, :], psY[c][:, :], gate[:, c, :], ALU.mult)
                ins.then_inc(Yg_ready, 1)
                xt = xall[:, bass.ds(i * NT, NT), :]
                chain(dve.scalar_tensor_tensor(out=res[:, :, :], in0=xt, scalar=2.0,
                                               in1=bdown[:, :].unsqueeze(1).broadcast_to([P, NT, D]), op0=ALU.mult, op1=ALU.add))
                dve.wait_ge(misc_full, i * MISC + MISC)
                chain(dve.tensor_tensor(res[:, :, :], res[:, :, :], psM[1][:, :].rearrange("p (t d) -> p t d", d=D), ALU.add))
                dve.sem_inc(down_read, 1)
                chain(normalise(i, 3, [res[:, j, :] for j in range(NT)], step_rows(i), chain))
                chain.close()

        @block.tensor
        def _(pe):
            pe.sem_inc(sum_done, LAG)
            pe.sem_inc(HC_ready, 2)

            def transpose_rows(i):
                pe.wait_ge(xhat_ready, i + 1)
                for j in range(NT):
                    ins = pe.transpose(psM[0][:, j * P:(j + 1) * P], xhat[:, j, :], ident[:, :])
                ins.then_inc(misc_full, 1)

            pe.wait_ge(first_loaded, 16 * 3)
            transpose_rows(0)
            pe.wait_ge(loaded, LOADS)
            pe.wait_ge(sel_ready, 4)
            with pe.Fori(0, STEPS) as i:
                pe.wait_ge(xnT_ready, i * 3 + 1)
                pe.wait_ge(down_read, i + 1)
                for c in range(NC):
                    pe.matmul(psM[(1 + c) % 2][:, :], up1[:, c * P:(c + 1) * P], xnT[:, :], start=True, stop=True).then_inc(misc_full, 1)
                for c in range(NC):
                    pe.wait_ge(xpad_ready, i * NC + c + 1)
                    pe.matmul(psM[(3 + c) % 2][:, :], up2[:, c * P:(c + 1) * P], xnT[:, :], start=True, stop=True).then_inc(misc_full, 1)
                pe.wait_ge(xc_ready, i * NC + NC)
                for m in range(NC):
                    pe.wait_ge(xnT_ready, i * 3 + 2 + m)
                    for c in range(NC):
                        ins = pe.matmul(psM[(5 + m) % 2][:, :], wdel[:, c, m * P:(m + 1) * P], xc[:, c, :], start=(c == 0), stop=(c == NC - 1))
                    ins.then_inc(misc_full, 1)
                for j, wt in enumerate((wB, wC)):
                    pe.wait_ge(pre_ready, i * 2 * NC + 2 * j + 1)
                    for c in range(NC):
                        ins = pe.matmul(psM[(7 + j) % 2][:, :], wt[:, c, :], xc[:, c, :], start=(c == 0), stop=(c == NC - 1))
                    ins.then_inc(misc_full, 1)

                def add_states(k):
                    pe.wait_ge(HC_ready, i * UNITS + k + 3)
                    pe.matmul(psY[k // UPC][:, :], summ[:, k, :], HC[:, k % LAG, :], start=(k % UPC == 0), stop=(k % UPC == UPC - 1)).then_inc(sum_done, 1)

                for k in range(UNITS):
                    c, g = k // UPC, k % UPC
                    if g == 0:
                        pe.wait_ge(split_ready, i * 2 * NC + NC + c + 1)
                    s = k % 2
                    if k >= 2:
                        pe.wait_ge(Ab_ready, i * UNITS + k - 1)
                        pe.wait_ge(XB_done, i * UNITS + k - 1)
                    for ps, hi, lo in ((psD[s], dlh, dll), (psX[s], xch, xcl)):
                        pe.matmul(ps[:, :], sel[:, g * P:(g + 1) * P], hi[:, c, :], start=True, stop=False)
                        ins = pe.matmul(ps[:, :], sel[:, g * P:(g + 1) * P], lo[:, c, :], start=False, stop=True)
                    ins.then_inc(bcast_full, 1)
                    if k >= LAG:
                        add_states(k - LAG)
                for k in range(UNITS - LAG, UNITS):
                    add_states(k)
                pe.wait_ge(Yg_ready, i + 1)
                for j in range(NT):
                    for c in range(NC):
                        ins = pe.matmul(psM[1][:, j * P:(j + 1) * P], Yg[:, c, j * P:(j + 1) * P], down[:, c, :], start=(c == 0), stop=(c == NC - 1))
                ins.then_inc(misc_full, 1)
                transpose_rows(i + 1)


class CrossAttentionInputs:

    def __init__(self, nc, ctx, w):
        def sb(name, shape):
            return ctx.enter_context(nc.sbuf_tensor(name, shape, F32))

        self.ctxall = sb("x_ctx", [P, TILES, D])
        self.cols = sb("x_cols", [P, 4])
        self.wv = sb("x_wv", [P, INNER])
        self.wq = sb("x_wq", [P, INNER])
        self.wk = sb("x_wk", [P, INNER])
        self.wo = sb("x_wo", [P, INNER // P, D])
        self.bo = sb("x_bo", [P, D])
        self.loaded = ctx.enter_context(nc.semaphore("x_loaded"))
        self.w = w

    def load(self, sp):
        for dst, src in [(self.ctxall[:, :, :], "ctx"), (self.cols[:, :], "x_cols"), (self.wv[:, :], "x_wv"), (self.wq[:, :], "x_wq"),
                         (self.wk[:, :], "x_wk"), (self.wo[:, :, :], "x_wo"), (self.bo[:, :], "x_bo")]:
            sp.dma_start(dst, self.w[src]).then_inc(self.loaded, 16)


def cross_attention_block(nc, xall, ident, eps_col, inputs, prefetch):
    NC = INNER // P
    R = 2 * TPB
    FILLS = 1 + 4 + NC + 2 * TPB + 1
    PER_BANK = FILLS // 2
    assert FILLS % 2 == 0
    LOADS = 16 * 7
    DVE_CHAIN = 13
    LO, HI = float(np.exp(-11.0)), float(np.exp(11.0))

    with ExitStack() as ctx:
        def sb(name, shape, dt=F32):
            return ctx.enter_context(nc.sbuf_tensor(name, shape, dt))

        def sem(name):
            return ctx.enter_context(nc.semaphore(name))

        ctxall, cols, bo = inputs.ctxall, inputs.cols, inputs.bo
        wq, wk, wv, wo = inputs.wq, inputs.wk, inputs.wv, inputs.wo
        loaded = inputs.loaded
        stats = sb("x_stats", [P, R, 6])
        mom = sb("x_mom", [P, R, 2])
        lnv = sb("x_lnv", [P, R])
        rstd = sb("x_rstd", [P, R])
        hat = sb("x_hat", [P, R, D])
        latT = sb("x_latT", [P, L])
        ctxT = sb("x_ctxT", [P, L])
        V1 = sb("x_V1", [P, TPB, H, DH + 1])
        qk = sb("x_qk", [P, 2, 2, L])
        E = sb("x_E", [P, 4, TPB, L])
        rden = sb("x_rden", [P, 2, 2, TPB])
        On = sb("x_On", [P, TPB, H, DH])
        OT = sb("x_OT", [P, NC, L])
        res = sb("x_res", [P, TPB, D])
        stats2 = sb("x_stats2", [P, TPB, 6])
        mom2 = sb("x_mom2", [P, TPB, 2])
        lnv2 = sb("x_lnv2", [P, TPB])
        rstd2 = sb("x_rstd2", [P, TPB])
        psM = [ctx.enter_context(nc.psum_tensor(f"x_psM{j}", [P, 512], F32)) for j in range(2)]
        psS = [ctx.enter_context(nc.psum_tensor(f"x_psS{j}", [P, TPB, L], F32)) for j in range(4)]
        psO = [ctx.enter_context(nc.psum_tensor(f"x_psO{j}", [P, 512], F32)) for j in range(2)]

        def o_view(j):
            return psO[j][:, 0:4 * (DH + 1)].rearrange("p (h t e) -> p h t e", h=2, t=TPB)

        passed = sem("x_passed")
        ones_ready = sem("x_ones_ready")
        dve_chain = sem("x_dve_chain")
        head_chain = sem("x_head_chain")
        act_chain = sem("x_act_chain")
        mom_ready = sem("x_mom_ready")
        rstd_ready = sem("x_rstd_ready")
        mom2_ready = sem("x_mom2_ready")
        rstd2_ready = sem("x_rstd2_ready")
        hat_ready = sem("x_hat_ready")
        misc_full = [sem(f"x_misc_full{j}") for j in range(2)]
        misc_free = [sem(f"x_misc_free{j}") for j in range(2)]
        catT_ready = sem("x_catT_ready")
        S_full = sem("x_S_full")
        E_exp = sem("x_E_exp")
        E_ready = sem("x_E_ready")
        O_full = sem("x_O_full")
        O_free = sem("x_O_free")

        block = ctx.enter_context(nc.Block())

        def wait_fill(eng, i, n):
            eng.wait_ge(misc_full[n % 2], i * PER_BANK + n // 2 + 1)
            return psM[n % 2], misc_free[n % 2]

        F_V, F_QK, F_OT, F_WO = 1, 5, 5 + NC, 5 + NC + 2 * TPB

        @block.sync
        def _(sp):
            prefetch(sp)

        @block.scalar
        def _(act):
            act.preload_act_table_set(LN_EXP)
            act.wait_ge(loaded, LOADS)
            act.wait_ge(ones_ready, 1)

            def rsqrt_of_variance(i):
                act.wait_ge(mom_ready, i + 1)
                act.activation(lnv[:, :], mom[:, :, 1], ACT.Ln, bias=eps_col).then_inc(act_chain, 1)
                act.wait_ge(act_chain, max(i * 2, 1) if isinstance(i, int) else i * 2)
                act.activation(rstd[:, :], lnv[:, :], ACT.Exp, scale=-0.5).then_inc(rstd_ready, 1)

            def scale_transposed(i):
                ps, free = wait_fill(act, i, 0)
                act.activation(ctxT[:, :], ps[:, L:2 * L], ACT.Identity, bias=cols[:, 3:4], scale=cols[:, 2:3]).then_inc(catT_ready, 1)
                act.activation(latT[:, :], ps[:, 0:L], ACT.Identity, bias=cols[:, 1:2], scale=cols[:, 0:1]).then_inc(free, 1)

            rsqrt_of_variance(0)
            scale_transposed(0)
            with act.Fori(0, B) as i:
                for n in range(4):
                    ps, free = wait_fill(act, i, F_V + n)
                    act.activation(V1[:, n // 2, (n % 2) * 8:(n % 2) * 8 + 8, 0:DH],
                                   ps[:, :].rearrange("p (h d) -> p h d", d=DH), ACT.Copy).then_inc(free, 1)
                for h in range(H):
                    act.wait_ge(S_full, i * H + h + 1)
                    if h >= 4:
                        act.wait_ge(O_full, i * NC + (h - 4) // 2 + 1)
                    act.activation(E[:, h % 4, :, :], psS[h % 4][:, :, :], ACT.Exp, scale=DH ** -0.5).then_inc(E_exp, 1)
                for n in range(2 * TPB):
                    ps, free = wait_fill(act, i, F_OT + n)
                    t, c0 = n % 2, (n // 2) * 4
                    act.activation(OT[:, c0:c0 + 4, t * P:(t + 1) * P], ps[:, :].rearrange("p (c q) -> p c q", c=4), ACT.Copy).then_inc(free, 1)
                rsqrt_of_variance(i + 1)
                scale_transposed(i + 1)
                act.wait_ge(mom2_ready, i + 1)
                act.activation(lnv2[:, :], mom2[:, :, 1], ACT.Ln, bias=eps_col).then_inc(act_chain, 1)
                act.wait_ge(act_chain, i * 2 + 3)
                act.activation(rstd2[:, :], lnv2[:, :], ACT.Exp, scale=-0.5).then_inc(rstd2_ready, 1)

        @block.vector
        def _(dve):
            dve.sem_inc(misc_free[0], 1)
            dve.sem_inc(misc_free[1], 1)
            dve.memset(V1[:, :, :, DH:DH + 1], 1.0).then_inc(ones_ready, 1)
            dve.wait_ge(loaded, LOADS)

            def batch_rows(tiles, b):
                return [tiles[:, bass.ds(b * TPB + j, 1), :].rearrange("p a d -> p (a d)") for j in range(TPB)]

            def normalise_rows(b, n, chain):
                rows = batch_rows(xall, b) + batch_rows(ctxall, b)
                layer_norm_stats(dve, passed, mom_ready, chain, rows, stats, mom)
                dve.wait_ge(rstd_ready, n + 1)
                for j in range(R):
                    ins = dve.tensor_scalar(hat[:, j, :], rows[j], mom[:, j, 0:1], rstd[:, j:j + 1], ALU.subtract, ALU.mult)
                ins.then_inc(hat_ready, 1)

            normalise_rows(0, 0, Chain(dve, head_chain, 0, 1))
            with dve.Fori(0, B) as i:
                chain = Chain(dve, dve_chain, i * DVE_CHAIN, DVE_CHAIN)
                xin = batch_rows(xall, i)

                def project(c):
                    ps, free = wait_fill(dve, i, F_QK + c)
                    if c >= 2:
                        dve.wait_ge(S_full, i * H + 2 * c - 2)
                    dve.tensor_copy(qk[:, c % 2, :, :].rearrange("p a t -> p (a t)"), ps[:, :]).then_inc(free, 1)

                def clip(h):
                    dve.wait_ge(E_exp, i * H + h + 1)
                    dve.tensor_scalar(E[:, h % 4, :, :], E[:, h % 4, :, :], LO, HI, ALU.max, ALU.min).then_inc(E_ready, 1)

                def normalise(c):
                    dve.wait_ge(O_full, i * NC + c + 1)
                    ov = o_view(c % 2)
                    chain(dve.reciprocal(rden[:, c % 2, :, :], ov[:, :, :, DH]))
                    for j in range(2):
                        ins = dve.tensor_tensor(On[:, :, 2 * c + j, :], ov[:, j, :, 0:DH],
                                                rden[:, c % 2, j, :].unsqueeze(2).broadcast_to([P, TPB, DH]), ALU.mult)
                    ins.then_inc(O_free, 1)

                project(0)
                for c in range(NC):
                    if c + 1 < NC:
                        project(c + 1)
                    clip(2 * c)
                    clip(2 * c + 1)
                    if c >= 1:
                        normalise(c - 1)
                normalise(NC - 1)
                chain(dve.tensor_tensor(res[:, :, :], xall[:, bass.ds(i * TPB, TPB), :], bo[:, :].unsqueeze(1).broadcast_to([P, TPB, D]), ALU.add))
                normalise_rows((i + 1) % B, i + 1, chain)
                ps, free = wait_fill(dve, i, F_WO)
                ins = dve.tensor_tensor(res[:, :, :], res[:, :, :], ps[:, 0:TPB * D].rearrange("p (t d) -> p t d", d=D), ALU.add)
                chain(ins)
                dve.sem_inc(free, 1)
                rows2 = [res[:, j, :] for j in range(TPB)]
                layer_norm_stats(dve, passed, mom2_ready, chain, rows2, stats2, mom2)
                dve.wait_ge(rstd2_ready, i + 1)
                for j in range(TPB):
                    ins = dve.tensor_scalar(xin[j], rows2[j], mom2[:, j, 0:1], rstd2[:, j:j + 1], ALU.subtract, ALU.mult)
                chain(ins)
                chain.close()

        @block.tensor
        def _(pe):
            pe.wait_ge(loaded, LOADS)

            def bank(i, n):
                pe.wait_ge(misc_free[n % 2], i * PER_BANK + n // 2 + 1)
                return psM[n % 2], misc_full[n % 2]

            def transpose_rows(i):
                pe.wait_ge(hat_ready, i + 1)
                ps, full = bank(i, 0)
                for j in range(R):
                    ins = pe.transpose(ps[:, j * P:(j + 1) * P], hat[:, j, :], ident[:, :])
                ins.then_inc(full, 1)

            transpose_rows(0)
            with pe.Fori(0, B) as i:
                def fill(n):
                    return bank(i, n)

                pe.wait_ge(catT_ready, i + 1)
                for n in range(4):
                    ps, full = fill(F_V + n)
                    pe.matmul(ps[:, :], ctxT[:, (n // 2) * P:(n // 2 + 1) * P], wv[:, (n % 2) * 512:(n % 2 + 1) * 512],
                              start=True, stop=True).then_inc(full, 1)

                def project(c):
                    ps, full = fill(F_QK + c)
                    pe.matmul(ps[:, 0:L], wq[:, c * P:(c + 1) * P], latT[:, :], start=True, stop=True)
                    pe.matmul(ps[:, L:2 * L], wk[:, c * P:(c + 1) * P], ctxT[:, :], start=True, stop=True).then_inc(full, 1)

                def scores(c):
                    n = F_QK + c
                    pe.wait_ge(misc_free[n % 2], i * PER_BANK + n // 2 + 2)
                    for h in (2 * c, 2 * c + 1):
                        r = slice((h % 2) * DH, (h % 2) * DH + DH)
                        if h >= 4:
                            pe.wait_ge(E_exp, i * H + h - 3)
                        for kt in range(TPB):
                            ins = pe.matmul(psS[h % 4][:, kt, :], qk[r, c % 2, 1, kt * P:(kt + 1) * P], qk[r, c % 2, 0, :], start=True, stop=True)
                        ins.then_inc(S_full, 1)

                def times_v(c):
                    pe.wait_ge(E_ready, i * H + 2 * c + 2)
                    if c >= 2:
                        pe.wait_ge(O_free, i * NC + c - 1)
                    ov = o_view(c % 2)
                    for j in range(2):
                        h = 2 * c + j
                        for qt in range(TPB):
                            for kt in range(TPB):
                                ins = pe.matmul(ov[:, j, qt, :], E[:, h % 4, kt, qt * P:(qt + 1) * P], V1[:, kt, h, :], start=(kt == 0), stop=(kt == TPB - 1))
                    ins.then_inc(O_full, 1)

                def transpose_out(n):
                    t, c0 = n % 2, (n // 2) * 4
                    ps, full = fill(F_OT + n)
                    for c in range(4):
                        h = 2 * (c0 + c)
                        ins = pe.transpose(ps[:, c * P:(c + 1) * P], On[:, t, h:h + 2, :].rearrange("p h d -> p (h d)"), ident[:, :])
                    ins.then_inc(full, 1)

                project(0)
                for c in range(NC):
                    if c + 1 < NC:
                        project(c + 1)
                    scores(c)
                    if c == NC - 1:
                        pe.wait_ge(O_free, i * NC + 4)
                        transpose_out(0)
                        transpose_out(1)
                    if c >= 1:
                        times_v(c - 1)
                times_v(NC - 1)
                pe.wait_ge(O_free, i * NC + NC)
                transpose_out(2)
                transpose_out(3)
                ps, full = fill(F_WO)
                for t in range(TPB):
                    n = F_OT + 2 + t
                    pe.wait_ge(misc_free[n % 2], i * PER_BANK + n // 2 + 2)
                    for c in range(NC):
                        ins = pe.matmul(ps[:, t * D:(t + 1) * D], OT[:, c, t * P:(t + 1) * P], wo[:, c, :], start=(c == 0), stop=(c == NC - 1))
                ins.then_inc(full, 1)
                transpose_rows(i + 1)


W_QKV = 0
W_SCALE = W_QKV + 3 * INNER
W_LN = W_SCALE + 2 * DH
W_O = W_LN + 2
W_1 = W_O + INNER // P * D
W_B1 = W_1 + 2 * FF
W_2 = W_B1 + 2 * FF
W_B2 = W_2 + 3 * D
W_COLS = W_B2 + D
SHARE = -(-W_COLS // B)
W_PAD = SHARE * B


class WindowInputs:

    def __init__(self, nc, ctx, w):
        def sb(name, shape):
            return ctx.enter_context(nc.sbuf_tensor(name, shape, F32))

        self.W = sb("f_W", [P, 2, W_PAD])
        self.base_tab = sb("f_base_tab", [P, TPB, 2, 2, DH])
        self.mask32 = sb("f_mask32", [P, TPB, 3 * WIN])
        self.loaded = ctx.enter_context(nc.semaphore("f_loaded"))
        self.w_loaded = ctx.enter_context(nc.semaphore("f_w_loaded"))
        self.w = w

    def load(self, sp):
        for dst, src in [(self.base_tab[:, :, :, :, :], "f_tab"), (self.mask32[:, :, :], "f_mask")]:
            sp.dma_start(dst, self.w[src]).then_inc(self.loaded, 16)
        sp.dma_start(self.W[:, 0, 0:7 * SHARE], self.w["f_W"][:, 0, 0:7, :].rearrange("p b c -> p (b c)")).then_inc(self.w_loaded, 16)
        sp.wait_ge(self.w_loaded, 16)
        sp.dma_start(self.W[:, 0, 7 * SHARE:], self.w["f_W"][:, 0, 7, :]).then_inc(self.w_loaded, 16)


def window_layers(nc, xall, ident, eps_col, inputs, out):
    ITERS = DEPTH * B
    CH = INNER // P
    KEYS = 3 * WIN
    HQ = P // 2
    A_FILLS = 10
    GH = H // 2

    with ExitStack() as ctx:
        def sb(name, shape, dt=F32):
            return ctx.enter_context(nc.sbuf_tensor(name, shape, dt))

        def sem(name):
            return ctx.enter_context(nc.semaphore(name))

        def ps(name, shape):
            return ctx.enter_context(nc.psum_tensor(name, shape, F32))

        W, base_tab, mask32 = inputs.W, inputs.base_tab, inputs.mask32
        loaded, w_loaded, w = inputs.loaded, inputs.w_loaded, inputs.w
        x0 = sb("f_x0", [P, TILES, D])
        tab = sb("f_tab", [P, 2, 2, 2, DH])
        maskb = sb("f_maskb", [P, TPB, GH // 2, KEYS], BF16)
        identb = sb("f_identb", [P, P], BF16)
        consts = sb("f_consts", [P, 2])
        xsA = sb("f_xsA", [P, 2, D])
        xT = sb("f_xT", [P, 2, P])
        qkraw = sb("f_qkraw", [P, 2 * INNER])
        m12 = sb("f_m12", [P, 2, 2, INNER])
        sq = sb("f_sq", [P, 2 * INNER])
        ssq = sb("f_ssq", [P, 2 * H])
        lnq = sb("f_lnq", [P, 2 * H])
        rn0 = sb("f_rn0", [P, 2 * H])
        rn = sb("f_rn", [P, 2 * H])
        qkr = sb("f_qkr", [P, 2 * INNER])
        Vt = sb("f_Vt", [P, 2, INNER])
        V96 = sb("f_V96", [KEYS, 2, 2, INNER])
        qT = sb("f_qT", [P, 2, CH, P])
        kT = sb("f_kT", [P, 2, CH, WIN + P])
        mx = sb("f_mx", [P, 2, GH])
        Pr = sb("f_Pr", [P, 2, GH, KEYS])
        den = sb("f_den", [P, 2, GH])
        rden = sb("f_rden", [P, 2, GH])
        PT = sb("f_PT", [KEYS, 2, 4, P])
        oT = sb("f_oT", [P, 2, CH, P])
        x1 = sb("f_x1", [P, 2, D])
        x1b = sb("f_x1b", [P, 2, D])
        xsC = sb("f_xsC", [P, 2, D])
        statC = sb("f_statC", [P, 6])
        momC = sb("f_momC", [P, 2])
        lnC = sb("f_lnC", [P, 1])
        rstdC = sb("f_rstdC", [P, 1])
        hatC = sb("f_hatC", [P, 2, D])
        xnT = sb("f_xnT", [P, P])
        ga = sb("f_ga", [P, 2, FF])
        ge = sb("f_ge", [P, FF])
        hh = sb("f_hh", [P, FF])
        hT = sb("f_hT", [P, 3, P])
        fin_s = sb("f_fin_s", [P, TILES, 6])
        fin_m = sb("f_fin_m", [P, TILES, 2])
        fin_ln = sb("f_fin_ln", [P, TILES])
        fin_r = sb("f_fin_r", [P, TILES])
        psA = [ps(f"f_psA{j}", [P, 512]) for j in range(2)]
        psD = [ps(f"f_psD{j}", [P, 512]) for j in range(2)]
        psS = ps("f_psS", [P, 2, 512])
        psP = ps("f_psP", [P, 4, P])
        psO = ps("f_psO", [P, 4, P])
        S4 = psS[:, :, 0:GH // 2 * KEYS].rearrange("p a (c k) -> p a c k", k=KEYS)

        passed = sem("f_passed")
        setup = sem("f_setup")
        xsA_ready = [sem(f"f_xsA_ready{t}") for t in range(2)]
        xsC_ready = [sem(f"f_xsC_ready{t}") for t in range(2)]
        V96_ready = [sem(f"f_V96_ready{t}") for t in range(2)]
        A_full = [sem(f"f_A_full{n}") for n in range(A_FILLS)]
        A_free = [sem(f"f_A_free{n}") for n in range(A_FILLS)]
        xT_full = sem("f_xT_full")
        xT_ready = sem("f_xT_ready")
        kprev_ready = sem("f_kprev_ready")
        m12_done = [sem(f"f_m12_done{j}") for j in range(2)]
        sq_ready = sem("f_sq_ready")
        ssq_ready = sem("f_ssq_ready")
        act_chain = sem("f_act_chain")
        lnq_done = sem("f_lnq_done")
        rn0_ready = sem("f_rn0_ready")
        rn_ready = sem("f_rn_ready")
        tab_ready = sem("f_tab_ready")
        rot_done = [sem(f"f_rot_done{j}") for j in range(2)]
        qkr_ready = [sem(f"f_qkr_ready{j}") for j in range(2)]
        S_full = [sem(f"f_S_full{g}") for g in range(2)]
        mx_done = [sem(f"f_mx_done{g}") for g in range(2)]
        S_free = [sem(f"f_S_free{g}") for g in range(2)]
        exp_done = [sem(f"f_exp_done{g}") for g in range(2)]
        den_done = [sem(f"f_den_done{g}") for g in range(2)]
        rden_ready = [sem(f"f_rden_ready{g}") for g in range(2)]
        Pr_ready = [[sem(f"f_Pr_ready{g}{j}") for j in range(2)] for g in range(2)]
        P_full = [[sem(f"f_P_full{g}{j}") for j in range(2)] for g in range(2)]
        P_free = [[sem(f"f_P_free{g}{j}") for j in range(2)] for g in range(2)]
        O_full = [sem(f"f_O_full{g}") for g in range(2)]
        O_free = [sem(f"f_O_free{g}") for g in range(2)]
        wo_full = sem("f_wo_full")
        x1_ready = sem("f_x1_ready")
        x1b_ready = sem("f_x1b_ready")
        dve_chain = sem("f_dve_chain")
        momC_ready = sem("f_momC_ready")
        rstdC_ready = sem("f_rstdC_ready")
        hatC_ready = sem("f_hatC_ready")
        xn_full = sem("f_xn_full")
        xnT_ready = sem("f_xnT_ready")
        ga_full = [sem("f_a_full"), sem("f_gate_full")]
        ga_ready = [sem("f_a_ready"), sem("f_gate_ready")]
        ge_ready = sem("f_ge_ready")
        hh_ready = sem("f_hh_ready")
        hT_full = sem("f_hT_full")
        hT_ready = sem("f_hT_ready")
        w2_full = sem("f_w2_full")
        x2_done = sem("f_x2_done")
        fin_mom = sem("f_fin_mom")
        fin_rstd = sem("f_fin_rstd")
        fin_done = sem("f_fin_done")
        fin_chain = sem("f_fin_chain")
        stored = sem("f_stored")

        block = ctx.enter_context(nc.Block())

        def slots(eng, slot):
            slot(0, 0, "A")
            slot(0, 1, "AB")
            slot(1, 0, "ABC")
            slot(1, 1, "ABCD")
            with eng.Fori(2, ITERS) as i:
                slot(i, 0, "ABCD")
                slot(i, 1, "ABCD")
            slot(ITERS, 0, "BCD")
            slot(ITERS, 1, "CD")
            slot(ITERS + 1, 0, "D")

        def is_first(i):
            return isinstance(i, int) and i == 0

        def at_least(eng, s, n):
            if not (isinstance(n, int) and n <= 0):
                eng.wait_ge(s, n)

        def unit_d(i, t):
            return (i - 2, 1) if t == 0 else (i - 1, 0)

        def weights(i_of_layer, col, n):
            if isinstance(i_of_layer, int):
                s = i_of_layer // B % 2
                return W[:, s, col:col + n]
            s = (i_of_layer // B) % 2
            return W[:, bass.ds(s, 1), col:col + n].rearrange("p a c -> p (a c)")

        def tile_of(i, t):
            if isinstance(i, int):
                return xall[:, i % B * TPB + t, :]
            return xall[:, bass.ds((i % B) * TPB + t, 1), :].rearrange("p a d -> p (a d)")

        def weights_here(eng, k, last_share):
            eng.wait_ge(w_loaded, max(k + last_share - 5, 1) * 16 if isinstance(k, int) else (k + last_share - 5) * 16)

        def share_of(last_col):
            return max(5, (last_col - 1) // SHARE)

        @block.sync
        def _(sp):
            sp.wait_ge(setup, 1)

            def shift_in(i, t):
                a = i * 2 + t
                sp.wait_ge(x2_done, a + 1)
                alone(sp, passed)
                at_least(sp, A_free[9], a - 1)
                src = tile_of(i, t)
                sp.dma_start(xsA[:, t, 0:64], src[:, 0:64]).then_inc(xsA_ready[t], 16)
                sp.dma_start(xsA[1:P, t, 64:D], src[0:P - 1, 64:D]).then_inc(xsA_ready[t], 16)
                if t == 1:
                    sp.dma_start(xsA[0:1, 1, 64:D], tile_of(i, 0)[P - 1:P, 64:D]).then_inc(xsA_ready[t], 16)

            def slot(i, t, stages):
                if "A" in stages:
                    shift_in(i + t, 1 - t)
                if "C" in stages:
                    sp.wait_ge(x1_ready, i * 2 + (t - 1))
                    sp.dma_start(xsC[:, t, 0:64], x1[:, t, 0:64]).then_inc(xsC_ready[t], 16)
                    sp.dma_start(xsC[1:P, t, 64:D], x1[0:P - 1, t, 64:D]).then_inc(xsC_ready[t], 16)
                    if t == 1:
                        sp.dma_start(xsC[0:1, 1, 64:D], x1[P - 1:P, 0, 64:D]).then_inc(xsC_ready[t], 16)
                if "A" in stages:
                    u = i * 2 + t
                    sp.wait_ge(A_free[9], u + 1)
                    at_least(sp, O_free[1], u - 1)
                    sp.dma_start(V96[WIN:KEYS, t, 0, :], Vt[0:HQ, t, :]).then_inc(V96_ready[t], 16)
                    sp.dma_start(V96[:, t, 1, :], Vt[WIN:P, t, :]).then_inc(V96_ready[t], 16)
                    if t == 1:
                        sp.dma_start(V96[0:WIN, 1, 0, :], Vt[P - WIN:P, 0, :]).then_inc(V96_ready[t], 16)
                if "A" in stages and t == 1 and not is_first(i):
                    share = i - 1
                    nxt = share // B + 1
                    dst = W[:, :, :].rearrange("p s (b c) -> p (s b) c", b=B)[:, bass.ds((nxt % 2) * B + share % B, 1), :]
                    src = w["f_W"].rearrange("p l b c -> p (l b) c")[:, bass.ds((share + B) % (DEPTH * B), 1), :]
                    sp.wait_ge(x2_done, share * 2 + 16)
                    alone(sp, passed)
                    sp.wait_ge(w_loaded, (share + 2) * 16)
                    sp.dma_start(dst, src).then_inc(w_loaded, 16)

            shift_in(0, 0)
            slots(sp, slot)
            sp.wait_ge(w_loaded, (ITERS + 1) * 16)
            sp.wait_ge(xsA_ready[0], (ITERS + 1) * 32)
            sp.wait_ge(fin_done, 1)
            sp.dma_start(out, xall[:, :, :]).then_inc(stored, 16)
            sp.wait_ge(stored, 16)

        @block.gpsimd
        def _(pool):
            pool.wait_ge(setup, 1)

            def normalise_probs(v, g):
                pool.wait_ge(rden_ready[g], v + 1)
                for j in range(2):
                    pv = Pr[:, g, :, :].rearrange("p (a c) k -> p a c k", a=2)[:, :, 2 * j:2 * j + 2, :]
                    rv = rden[:, g, :].rearrange("p (a c) -> p a c", a=2)[:, :, 2 * j:2 * j + 2]
                    pool.tensor_tensor(pv, pv, rv.unsqueeze(3).broadcast_to([P, 2, 2, KEYS]), ALU.mult).then_inc(Pr_ready[g][j], 1)

            def rotate(u, j):
                pool.wait_ge(m12_done[j], u + 1)
                mv = m12[:, j, :, :].rearrange("p m (h two d) -> p m h two d", two=2, d=DH // 2)
                pool.tensor_tensor(mv[:, 0], mv[:, 0], mv[:, 1, :, ::-1, :], ALU.add).then_inc(rot_done[j], 1)

            def scale(u, j):
                pool.wait_ge(rot_done[j], u + 1)
                pool.wait_ge(rn_ready, u + 1)
                pool.tensor_tensor(qkr[:, j * INNER:(j + 1) * INNER].rearrange("p (h d) -> p h d", d=DH),
                                   m12[:, j, 0, :].rearrange("p (h d) -> p h d", d=DH),
                                   rn[:, j * H:(j + 1) * H].unsqueeze(2).broadcast_to([P, H, DH]), ALU.mult).then_inc(qkr_ready[j], 1)

            def slot(i, t, stages):
                u, v, wu, du = i * 2 + t, i * 2 + (t - 1), i * 2 + (t - 2), i * 2 + (t - 3)
                if "A" in stages:
                    weights_here(pool, i, share_of(W_LN))
                    at_least(pool, m12_done[0], u)
                    alone(pool, passed)
                    sc = weights(i, W_SCALE, 2 * DH).rearrange("p (a d) -> p a d", a=2).unsqueeze(2).broadcast_to([P, 2, 2, DH])
                    pool.tensor_tensor(tab[:, t, :, :, :], base_tab[:, t, :, :, :], sc, ALU.mult).then_inc(tab_ready, 1)
                    rotate(u, 0)
                    rotate(u, 1)
                if "D" in stages:
                    pool.wait_ge(x2_done, du + 16)
                    pool.wait_ge(ge_ready, du + 1)
                    pool.wait_ge(ga_ready[0], du + 1)
                    pool.tensor_tensor(hh[:, :], ga[:, 0, :], ge[:, :], ALU.mult).then_inc(hh_ready, 1)
                if "B" in stages:
                    normalise_probs(v, 0)
                if "C" in stages:
                    weights_here(pool, i - 1, share_of(W_COLS))
                    pool.wait_ge(x1_ready, wu + 1)
                    pool.wait_ge(x2_done, wu + 15)
                    alone(pool, passed)
                    pool.tensor_tensor(x1b[:, t, :], x1[:, t, :], weights(i - 1, W_B2, D), ALU.add).then_inc(x1b_ready, 1)
                if "B" in stages:
                    normalise_probs(v, 1)
                if "A" in stages:
                    if "B" in stages:
                        pool.wait_ge(A_full[7], v + 1)
                    scale(u, 0)
                    scale(u, 1)

            slots(pool, slot)

        @block.scalar
        def _(act):
            act.preload_act_table_set(LN_EXP)
            act.wait_ge(setup, 1)
            act.activation(x0[:, :, :], xall[:, :, :], ACT.Copy).then_inc(act_chain, 1)

            def evacuate_tokens(u, t):
                act.wait_ge(xT_full, u + 1)
                act.activation(xT[:, t, :], psD[0][:, 0:P], ACT.Copy).then_inc(xT_ready, 1)

            def slot(i, t, stages):
                q = 1 - t
                u, v, wu, du = i * 2 + t, i * 2 + (t - 1), i * 2 + (t - 2), i * 2 + (t - 3)
                di, dt = unit_d(i, t)

                def evacuate_probs(g, j):
                    unit = (v, wu)[g]
                    act.wait_ge(P_full[g][j], unit + 1)
                    act.activation(PT[:, j, :, :], psP[0:KEYS, :, :], ACT.Copy).then_inc(P_free[g][j], 1)

                def evacuate_v(j):
                    act.wait_ge(A_full[8 + j], u + 1)
                    if j == 0 and not is_first(i):
                        act.wait_ge(V96_ready[1], i * 48)
                        if t == 0:
                            act.wait_ge(V96_ready[0], i * 32)
                    act.activation(Vt[:, t, j * 512:(j + 1) * 512], psA[j][:, :], ACT.Copy).then_inc(A_free[8 + j], 1)

                def evacuate_out(g):
                    act.wait_ge(O_full[g], (v, wu)[g] + 1)
                    act.activation(oT[:, (q, t)[g], 4 * g:4 * g + 4, :], psO[:, :, :], ACT.Copy).then_inc(O_free[g], 1)

                def exponentials(g):
                    act.wait_ge(S_free[g], v + 1)
                    act.activation(Pr[:, g, :, :], Pr[:, g, :, :], ACT.Exp).then_inc(exp_done[g], 1)

                def evacuate_raw(n):
                    if n == 0:
                        at_least(act, m12_done[1], u)
                    act.wait_ge(A_full[n], u + 1)
                    act.activation(qkraw[:, n * 512:(n + 1) * 512], psA[n % 2][:, :], ACT.Copy).then_inc(A_free[n], 1)

                def evacuate_qk(n):
                    act.wait_ge(A_full[4 + n], v + 1)
                    c0 = (n // 2) * 4
                    src = psA[n % 2][:, :].rearrange("p (c q) -> p c q", c=4)
                    dst = kT[:, q, c0:c0 + 4, WIN:WIN + P] if n % 2 else qT[:, q, c0:c0 + 4, :]
                    act.activation(dst, src, ACT.Copy).then_inc(A_free[4 + n], 1)

                if "A" in stages:
                    evacuate_raw(0)
                    evacuate_raw(1)
                if "C" in stages:
                    evacuate_probs(1, 0)
                if "D" in stages:
                    act.wait_ge(xn_full, du + 1)
                    weights_here(act, di, share_of(W_O))
                    alone(act, passed)
                    act.activation(xnT[:, :], psD[0][:, 0:P], ACT.Identity, bias=weights(di, W_LN + 1, 1), scale=weights(di, W_LN, 1)).then_inc(xnT_ready, 1)
                if "A" in stages:
                    evacuate_raw(2)
                if "C" in stages:
                    evacuate_probs(1, 1)
                if "A" in stages:
                    evacuate_raw(3)
                if "B" in stages:
                    if q == 1:
                        act.activation(kT[:, 1, :, 0:WIN], kT[:, 0, :, P:P + WIN], ACT.Copy).then_inc(kprev_ready, 1)
                    evacuate_qk(0)
                    evacuate_qk(1)
                if "C" in stages:
                    evacuate_out(1)
                if "B" in stages:
                    evacuate_qk(2)
                    evacuate_qk(3)
                if "A" in stages:
                    act.wait_ge(A_free[3], u + 1)
                    act.activation(sq[:, :], qkraw[:, :], ACT.Square).then_inc(sq_ready, 1)
                if "D" in stages:
                    act.wait_ge(ga_ready[1], du + 1)
                    act.activation(ge[:, :], ga[:, 1, :], ACT.Gelu).then_inc(ge_ready, 1)
                    act.preload_act_table_set(LN_EXP)
                if "B" in stages:
                    exponentials(0)
                if "A" in stages:
                    evacuate_v(0)
                if "A" in stages:
                    evacuate_v(1)
                if "B" in stages:
                    evacuate_probs(0, 0)
                if "D" in stages:
                    act.wait_ge(hT_full, du + 1)
                    act.activation(hT[:, 0:2, :], psD[1][:, 0:2 * P].rearrange("p (c q) -> p c q", c=2), ACT.Copy)
                    act.activation(hT[0:FF - 2 * P, 2, :], psD[1][0:FF - 2 * P, 2 * P:3 * P], ACT.Copy).then_inc(hT_ready, 1)
                if "A" in stages:
                    evacuate_tokens(u + 1, 1 - t)
                if "B" in stages:
                    exponentials(1)
                    evacuate_probs(0, 1)
                if "A" in stages:
                    act.wait_ge(ssq_ready, u + 1)
                    act.activation(lnq[:, :], ssq[:, :], ACT.Ln, bias=consts[:, 0:1], scale=SSQ_SCALE).then_inc(lnq_done, 1)
                    act.wait_ge(lnq_done, u + 1)
                    act.activation(rn0[:, :], lnq[:, :], ACT.Exp, bias=consts[:, 1:2], scale=-0.5).then_inc(rn0_ready, 1)
                if "C" in stages:
                    act.wait_ge(momC_ready, wu + 1)
                    act.activation(lnC[:, :], momC[:, 1:2], ACT.Ln, bias=eps_col).then_inc(act_chain, 1)
                    act.wait_ge(act_chain, wu + 2)
                    act.activation(rstdC[:, :], lnC[:, :], ACT.Exp, scale=-0.5).then_inc(rstdC_ready, 1)
                if "B" in stages:
                    evacuate_out(0)

            evacuate_tokens(0, 0)
            slots(act, slot)
            act.wait_ge(fin_mom, 1)
            act.activation(fin_ln[:, :], fin_m[:, :, 1], ACT.Ln, bias=eps_col).then_inc(fin_chain, 1)
            act.wait_ge(fin_chain, 2)
            act.activation(fin_r[:, :], fin_ln[:, :], ACT.Exp, scale=-0.5).then_inc(fin_rstd, 1)

        @block.vector
        def _(dve):
            dve.memset(xsA[0:1, 0, 64:D], 0.0)
            dve.memset(xsC[0:1, 0, 64:D], 0.0)
            dve.memset(kT[:, 0, :, 0:WIN], 0.0)
            dve.memset(V96[0:WIN, 0, 0, :], 0.0)
            dve.memset(consts[:, 0:1], 2.0 ** -70)
            dve.memset(consts[:, 1:2], 0.5 * float(np.log(SSQ_SCALE)))
            dve.wait_ge(loaded, 32)
            dve.tensor_copy(identb[:, :], ident[:, :])
            dve.tensor_copy(maskb[:, :, :, :], mask32[:, :, :].unsqueeze(2).broadcast_to([P, TPB, GH // 2, KEYS])).then_inc(setup, 1)
            dve.sem_inc(x2_done, 16)

            def less_maximum(v, g):
                dve.wait_ge(S_full[g], v + 1)
                dve.tensor_reduce(mx[:, g, :].rearrange("p (a c) -> p a c", a=2), S4, axis=AX.X, op=ALU.max).then_inc(mx_done[g], 1)
                dve.wait_ge(mx_done[g], v + 1)
                at_least(dve, P_free[g][1], v)
                mb = mx[:, g, :].rearrange("p (a c) -> p a c", a=2).unsqueeze(3).broadcast_to([P, 2, GH // 2, KEYS])
                dve.tensor_tensor(Pr[:, g, :, :].rearrange("p (a c) k -> p a c k", a=2), S4, mb, ALU.subtract).then_inc(S_free[g], 1)

            def denominators(v, g):
                dve.wait_ge(exp_done[g], v + 1)
                dve.tensor_reduce(den[:, g, :], Pr[:, g, :, :], axis=AX.X, op=ALU.add).then_inc(den_done[g], 1)
                dve.wait_ge(den_done[g], v + 1)
                dve.reciprocal(rden[:, g, :], den[:, g, :]).then_inc(rden_ready[g], 1)

            def slot(i, t, stages):
                u, v, wu, du = i * 2 + t, i * 2 + (t - 1), i * 2 + (t - 2), i * 2 + (t - 3)
                di, dt = unit_d(i, t)

                def add_bias(n):
                    dve.wait_ge(ga_full[n], du + 1)
                    dve.tensor_tensor(ga[:, n, :], psD[n][:, 0:FF], weights(di, W_B1 + n * FF, FF), ALU.add).then_inc(ga_ready[n], 1)

                if "A" in stages:
                    dve.wait_ge(tab_ready, u + 1)
                    if "B" in stages:
                        dve.wait_ge(qkr_ready[1], u)
                    for j in range(2):
                        dve.wait_ge(A_free[2 * j + 1], u + 1)
                        rv = qkraw[:, j * INNER:(j + 1) * INNER].rearrange("p (h d) -> p h d", d=DH)
                        dve.tensor_tensor(m12[:, j, :, :].rearrange("p m (h d) -> p m h d", d=DH),
                                          rv.unsqueeze(1).broadcast_to([P, 2, H, DH]),
                                          tab[:, t, j, :, :].unsqueeze(2).broadcast_to([P, 2, H, DH]), ALU.mult).then_inc(m12_done[j], 1)
                if "D" in stages:
                    weights_here(dve, di, share_of(W_2))
                    add_bias(1)
                    add_bias(0)
                if "B" in stages:
                    less_maximum(v, 0)
                if "B" in stages:
                    denominators(v, 0)
                if "C" in stages:
                    dve.wait_ge(wo_full, wu + 1)
                    dve.tensor_tensor(x1[:, t, :], psO[:, 0, :], tile_of(i - 1, t), ALU.add).then_inc(x1_ready, 1)
                if "B" in stages:
                    less_maximum(v, 1)
                if "A" in stages:
                    dve.wait_ge(sq_ready, u + 1)
                    dve.tensor_reduce(ssq[:, :], sq[:, :].rearrange("p (h d) -> p h d", d=DH), axis=AX.X, op=ALU.add).then_inc(ssq_ready, 1)
                if "C" in stages:
                    dve.wait_ge(xsC_ready[t], i * (32, 48)[t])
                    dve.bn_stats(out=statC[:, :], in_=xsC[:, t, :]).then_inc(dve_chain, 1)
                    dve.wait_ge(dve_chain, wu + 1)
                    alone(dve, passed)
                    dve.bn_aggr(out=momC[:, :], in_=statC[:, :]).then_inc(momC_ready, 1)
                if "B" in stages:
                    denominators(v, 1)
                if "A" in stages:
                    dve.wait_ge(rn0_ready, u + 1)
                    dve.tensor_scalar(rn[:, 0:H], rn0[:, 0:H], 1e12, 8.0, ALU.min, ALU.mult)
                    dve.tensor_scalar(rn[:, H:2 * H], rn0[:, H:2 * H], 1e12, None, ALU.min).then_inc(rn_ready, 1)
                if "C" in stages:
                    dve.wait_ge(rstdC_ready, wu + 1)
                    dve.tensor_scalar(hatC[:, t, :], xsC[:, t, :], momC[:, 0:1], rstdC[:, :], ALU.subtract, ALU.mult).then_inc(hatC_ready, 1)
                if "D" in stages:
                    dve.wait_ge(w2_full, du + 1)
                    dve.wait_ge(x1b_ready, du + 1)
                    dve.tensor_tensor(tile_of(di, dt), psD[0][:, 0:D], x1b[:, dt, :], ALU.add).then_inc(x2_done, 1)

            slots(dve, slot)
            dve.wait_ge(act_chain, 1)
            dve.wait_ge(x2_done, ITERS * 2 + 16)
            dve.tensor_tensor(x0[:, :, :], x0[:, :, :], xall[:, :, :], ALU.add).then_inc(fin_chain, 1)
            dve.wait_ge(fin_chain, 1)
            for j in range(TILES):
                ins = dve.bn_stats(out=fin_s[:, j, :], in_=x0[:, j, :])
            ins.then_inc(dve_chain, 1)
            dve.wait_ge(dve_chain, ITERS * 2 + 1)
            for j in range(TILES):
                ins = dve.bn_aggr(out=fin_m[:, j, :], in_=fin_s[:, j, :])
            ins.then_inc(fin_mom, 1)
            dve.wait_ge(fin_rstd, 1)
            for j in range(TILES):
                ins = dve.tensor_scalar(xall[:, j, :], x0[:, j, :], fin_m[:, j, 0:1], fin_r[:, j:j + 1], ALU.subtract, ALU.mult)
            ins.then_inc(fin_done, 1)

        @block.tensor
        def _(pe):
            pe.wait_ge(setup, 1)

            def transpose_tokens(u, i, t):
                pe.wait_ge(xsA_ready[t], (i + 1) * (32, 48)[t])
                pe.transpose(psD[0][:, 0:P], xsA[:, t, :], ident[:, :]).then_inc(xT_full, 1)

            def slot(i, t, stages):
                q = 1 - t
                u, v, wu, du = i * 2 + t, i * 2 + (t - 1), i * 2 + (t - 2), i * 2 + (t - 3)
                di, dt = unit_d(i, t)

                def free_bank(n):
                    if n < 2:
                        at_least(pe, A_free[n + 8], u)
                    elif n >= 8 and "B" not in stages:
                        pe.wait_ge(A_free[n - 6], u + 1)
                    elif n in (4, 5) and "A" not in stages:
                        pe.wait_ge(A_free[n + 4], u)
                    elif n in (4, 5):
                        pe.wait_ge(A_free[n - 2], u + 1)
                    elif n in (6, 7):
                        pe.wait_ge(A_free[n - 2], v + 1)
                    elif n < 4:
                        pe.wait_ge(A_free[n - 2], u + 1)

                def scores(g):
                    if g == 0:
                        at_least(pe, S_free[1], v)
                    else:
                        pe.wait_ge(S_free[0], v + 1)
                    for par in range(2):
                        pe.matmul(psS[:, par, 0:GH // 2 * KEYS], identb[:, :], maskb[:, q, :, :].rearrange("p c k -> p (c k)"), start=True, stop=False, skip_group_check=True)
                    for par in range(2):
                        r = slice(par * DH, par * DH + DH)
                        for c in range(4):
                            for half in range(2):
                                k0 = half * HQ
                                ins = pe.matmul(S4[half * HQ:(half + 1) * HQ, par, c, :], qT[r, q, 4 * g + c, k0:k0 + HQ],
                                                kT[r, q, 4 * g + c, k0:k0 + KEYS], start=False, stop=True, skip_group_check=True)
                    ins.then_inc(S_full[g], 1)

                def transpose_probs(g, j):
                    unit = (v, wu)[g]
                    pe.wait_ge(Pr_ready[g][j], unit + 1)
                    if j == 1:
                        pe.wait_ge(P_free[g][0], unit + 1)
                    for n in range(4):
                        h = 4 * j + n
                        ins = pe.transpose(psP[0:KEYS, n, :], Pr[:, g, (h % 2) * 4 + h // 2, :], ident[:, :])
                    ins.then_inc(P_full[g][j], 1)

                def times_v(g, j):
                    unit, tile = ((v, q), (wu, t))[g]
                    if j == 1:
                        pe.wait_ge(P_free[g][1], unit + 1)
                    elif g == 1:
                        pe.wait_ge(O_free[0], unit + 1)
                    elif "C" in stages:
                        pe.wait_ge(x1_ready, wu + 1)
                    if g == 0 and j == 0:
                        n_dma = (32, 48)[q]
                        pe.wait_ge(V96_ready[q], (i + (1 if q == 0 else 0)) * n_dma)
                    for n in range(4):
                        h = 4 * j + n
                        hh_ = 8 * g + h
                        for half in range(2):
                            ins = pe.matmul(psO[(h % 2) * DH:(h % 2) * DH + DH, h // 2, half * HQ:(half + 1) * HQ],
                                            V96[:, tile, half, hh_ * DH:(hh_ + 1) * DH], PT[:, j, n, half * HQ:(half + 1) * HQ], start=True, stop=True)
                    if j == 1:
                        ins.then_inc(O_full[g], 1)

                def transpose_qk(n):
                    free_bank(4 + n)
                    p = psA[n % 2]
                    for c in range(4):
                        col = (n % 2) * INNER + ((n // 2) * 4 + c) * P
                        ins = pe.transpose(p[:, c * P:(c + 1) * P], qkr[:, col:col + P], ident[:, :])
                    ins.then_inc(A_full[4 + n], 1)

                def project(n):
                    n_fill = (0, 1, 2, 3, 8, 9)[n]
                    free_bank(n_fill)
                    pe.matmul(psA[n % 2][:, :], xT[:, t, :], weights(i, W_QKV + n * 512, 512), start=True, stop=True).then_inc(A_full[n_fill], 1)

                if "A" in stages:
                    pe.wait_ge(xT_ready, u + 1)
                    weights_here(pe, i, share_of(W_SCALE))
                    project(0)
                    project(1)
                if "D" in stages:
                    pe.wait_ge(hatC_ready, du + 1)
                    pe.wait_ge(x2_done, du + 16)
                    pe.transpose(psD[0][:, 0:P], hatC[:, dt, :], ident[:, :]).then_inc(xn_full, 1)
                if "C" in stages:
                    transpose_probs(1, 0)
                if "A" in stages:
                    project(2)
                if "C" in stages:
                    transpose_probs(1, 1)
                if "A" in stages:
                    project(3)
                if "C" in stages:
                    times_v(1, 0)
                    times_v(1, 1)
                def w1(n):
                    pe.matmul(psD[n][:, 0:FF], xnT[:, :], weights(di, W_1 + n * FF, FF), start=True, stop=True).then_inc(ga_full[n], 1)

                if "B" in stages:
                    pe.wait_ge(qkr_ready[1], v + 1)
                    transpose_qk(0)
                    transpose_qk(1)
                if "D" in stages:
                    weights_here(pe, di, share_of(W_B1))
                    pe.wait_ge(xnT_ready, du + 1)
                    w1(1)
                if "B" in stages:
                    transpose_qk(2)
                    transpose_qk(3)
                if "D" in stages:
                    w1(0)
                if "B" in stages:
                    pe.wait_ge(A_free[6], v + 1)
                    pe.wait_ge(A_free[7], v + 1)
                    if q == 1:
                        pe.wait_ge(kprev_ready, i)
                    scores(0)
                if "A" in stages:
                    project(4)
                if "C" in stages:
                    pe.wait_ge(O_free[1], wu + 1)
                    for c in range(CH):
                        ins = pe.matmul(psO[:, 0, :], oT[:, t, c, :], weights(i - 1, W_O + c * D, D), start=(c == 0), stop=(c == CH - 1))
                    ins.then_inc(wo_full, 1)
                if "B" in stages:
                    scores(1)
                if "A" in stages:
                    project(5)
                if "B" in stages:
                    transpose_probs(0, 0)
                if "D" in stages:
                    pe.wait_ge(hh_ready, du + 1)
                    p = psD[1]
                    for c in range(3):
                        n = min(P, FF - c * P)
                        ins = pe.transpose(p[0:n, c * P:(c + 1) * P], hh[:, c * P:c * P + n], ident[:, :])
                    ins.then_inc(hT_full, 1)
                if "A" in stages:
                    transpose_tokens(u + 1, i + t, 1 - t)
                if "B" in stages:
                    transpose_probs(0, 1)
                if "B" in stages:
                    times_v(0, 0)
                if "D" in stages:
                    weights_here(pe, di, share_of(W_B2))
                    pe.wait_ge(hT_ready, du + 1)
                    if "A" in stages:
                        pe.wait_ge(xT_ready, u + 2)
                    p = psD[0]
                    for c in range(3):
                        n = min(P, FF - c * P)
                        ins = pe.matmul(p[:, 0:D], hT[0:n, c, :], weights(di, W_2 + c * D, D)[0:n, :], start=(c == 0), stop=(c == 2))
                    ins.then_inc(w2_full, 1)
                if "B" in stages:
                    times_v(0, 1)

            transpose_tokens(0, 0, 0)
            slots(pe, slot)


def host_layout(x):
    f = np.float32
    up = lambda a: np.ascontiguousarray(a, dtype=f)
    w = {}
    w["x"] = up(x["x"].reshape(TILES, P, D).transpose(1, 0, 2))
    w["ident"] = np.eye(P, dtype=f)
    G = P // NST
    W = x["L0_attn_W_ll"]
    kc = lambda a: up(a.T.reshape(2, P, -1).transpose(1, 0, 2))
    w["m_up1"] = up(x["L0_attn_W_up1"].T)
    w["m_up2"] = up(x["L0_attn_W_up2"].T)
    w["m_down"] = kc(x["L0_attn_W_down"])
    w["m_wdel"] = kc(W[:DI])
    w["m_wB"] = kc(np.tile(W[DI:DI + NST], (G, 1)))
    w["m_wC"] = kc(np.tile(W[DI + NST:], (G, 1)))
    b = x["L0_attn_b_ll"]
    w["m_cols"] = up(np.concatenate([
        x["L0_attn_ln_g"][:, None], x["L0_attn_ln_b"][:, None], x["L0_attn_conv_b"].reshape(2, P).T,
        b[:DI].reshape(2, P).T, np.tile(b[DI:DI + NST], G)[:, None], np.tile(b[DI + NST:], G)[:, None],
        x["L0_attn_conv_w"].reshape(2, P, 4).transpose(1, 0, 2).reshape(P, 8)], axis=1))
    w["m_alog"] = up(x["L0_attn_A_log"].reshape(DI // G, P).T)
    w["m_bdown"] = up(np.broadcast_to(x["L0_attn_b_down"], (P, D)))
    col = np.arange(NST * P)
    w["m_sel"] = up(col[None, :] // NST == np.arange(P)[:, None])
    w["m_pick"] = up(np.arange(P)[None, None, :] == (np.arange(P)[:, None, None] // NST + G * np.arange(P // G)[None, :, None]))
    w["ctx"] = up(x["ctx_1024"].reshape(TILES, P, D).transpose(1, 0, 2))
    w["x_cols"] = up(np.stack([x["L0_xattn_ln_l_w"], x["L0_xattn_ln_l_b"], x["L0_xattn_ln_c_w"], x["L0_xattn_ln_c_b"]], axis=1))
    w["x_wq"] = up(x["L0_xattn_Wq"])
    w["x_wk"] = up(x["L0_xattn_Wkv"][:, :INNER])
    w["x_wv"] = up(x["L0_xattn_Wkv"][:, INNER:])
    w["x_wo"] = up(x["L0_xattn_Wo"].reshape(INNER // P, P, D).transpose(1, 0, 2))
    w["x_bo"] = up(np.broadcast_to(x["L0_xattn_bo"], (P, D)))
    pack = np.zeros((P, DEPTH, W_PAD), f)
    rows = lambda a: np.broadcast_to(a, (P,) + a.shape)
    for l in range(DEPTH):
        put = lambda col, a: pack[:a.shape[0], l, col:col + a.shape[1]].__setitem__(slice(None), a)
        put(W_QKV, x["L0_ffn_Wqkv"][l])
        put(W_SCALE, rows(x["L0_ffn_q_scale"][l]))
        put(W_SCALE + DH, rows(x["L0_ffn_k_scale"][l]))
        put(W_LN, x["L0_ffn_ln_g"][l][:, None])
        put(W_LN + 1, x["L0_ffn_ln_b"][l][:, None])
        put(W_O, x["L0_ffn_Wo"][l].reshape(INNER // P, P, D).transpose(1, 0, 2).reshape(P, -1))
        put(W_1, x["L0_ffn_W1"][l])
        put(W_B1, rows(x["L0_ffn_b1"][l]))
        for c in range(3):
            put(W_2 + c * D, x["L0_ffn_W2"][l][c * P:(c + 1) * P])
        put(W_B2, rows(x["L0_ffn_b2"][l]))
    w["f_W"] = pack.reshape(P, DEPTH, B, SHARE)
    half = np.arange(0, DH, 2, dtype=f)
    inv_freq = f(1.0) / f(10000.0) ** (half / f(DH))
    t = np.arange(L, dtype=f)
    freqs = t[:, None] * inv_freq[None, :]
    base = (half + f(0.4 * DH)) / f(1.4 * DH)
    scale = base[None, :] ** ((t - L // 2) / f(WIN // 2))[:, None]
    two = lambda a: np.concatenate([a, a], -1)
    cos, sin, scale = two(np.cos(freqs)), np.concatenate([np.sin(freqs), -np.sin(freqs)], -1), two(scale)
    tab = np.stack([np.stack([cos * s, sin * s]) for s in (scale, f(1.0) / scale)])
    w["f_tab"] = up(tab.reshape(2, 2, TPB, P, DH).transpose(3, 2, 0, 1, 4))
    it = np.arange(L)
    key = (it // (P // 2) * (P // 2) - WIN)[:, None] + np.arange(3 * WIN)[None, :]
    seen = (key <= it[:, None]) & (key >= it[:, None] - WIN) & (key >= 0)
    w["f_mask"] = up(np.where(seen, 0.0, -1e30).reshape(TPB, P, 3 * WIN).transpose(1, 0, 2))
    return w


def decoder_layer(nc, w, out):
    with ExitStack() as ctx:
        xall = ctx.enter_context(nc.sbuf_tensor("xall", [P, TILES, D], F32))
        ident = ctx.enter_context(nc.sbuf_tensor("ident", [P, P], F32))
        eps = ctx.enter_context(nc.sbuf_tensor("eps", [P, 1], F32))
        eps_ready = ctx.enter_context(nc.semaphore("eps_ready"))
        with nc.Block() as block:
            @block.vector
            def _(dve):
                dve.memset(eps[:, :], EPS).then_inc(eps_ready, 1)

            @block.scalar
            def _(act):
                act.wait_ge(eps_ready, 1)

        with ExitStack() as window_ctx:
            window = WindowInputs(nc, window_ctx, w)
            with ExitStack() as cross_ctx:
                cross = CrossAttentionInputs(nc, cross_ctx, w)
                state_space_block(nc, xall, ident, eps[:, :], w, cross.load)
                cross_attention_block(nc, xall, ident, eps[:, :], cross, window.load)
            window_layers(nc, xall, ident, eps[:, :], window, out)


def kernel(**inputs):
    import concourse.bacc as bacc
    from concourse.bass_utils import run_bass_kernel_spmd

    nc = bacc.Bacc("TRN2", target_bir_lowering=False, num_devices=1)
    arrays = host_layout({k: np.asarray(v) for k, v in inputs.items()})
    aps = {k: nc.dram_tensor(f"in_{k}", a.shape, mybir.dt.from_np(a.dtype), kind="ExternalInput").ap() for k, a in arrays.items()}
    out = nc.dram_tensor("out_x", (P, TILES, D), F32, kind="ExternalOutput").ap()
    decoder_layer(nc, aps, out)
    r = run_bass_kernel_spmd(nc, [{f"in_{k}": a for k, a in arrays.items()}], core_ids=[0])
    return np.asarray(r.results[0]["out_x"]).transpose(1, 0, 2).reshape(B, L, D)
```
